# Optimizing a Trainium2 kernel written in Bass

```python
import numpy as np
import jax
import jax.numpy as jnp

def _softmax(x, axis=-1):
    return jax.nn.softmax(x, axis=axis)

def _gelu(x):
    return jax.nn.gelu(x, approximate=True)

def _silu(x):
    return jax.nn.silu(x)

def _sigmoid(x):
    return jax.nn.sigmoid(x)

def _layernorm(x, axis=-1, eps=1e-05):
    m = jnp.mean(x, axis=axis, keepdims=True)
    v = jnp.var(x, axis=axis, keepdims=True)
    return (x - m) / jnp.sqrt(v + eps)

def _scatter_add(tgt, idx, src, axis=0):
    return tgt.at[idx].add(src)

def _segment_sum(src, seg, n):
    return jax.ops.segment_sum(src, seg, n)
kernel_name = 'mk_gnn_ffn_d2_gnn_r8_b639d5'

def setup_inputs(seed: int=0):
    np.random.seed(seed)
    _w = jnp.asarray

    def _rec_inputs():
        import jax
        import jax.numpy as jnp
        _gk = jax.random.key(seed)
        x = -8.776e-05 + 1 * jax.random.normal(jax.random.fold_in(_gk, 1), (1250, 512), jnp.float32)
        src = jax.random.randint(jax.random.fold_in(_gk, 2), (20000,), 0, 1250, jnp.int32)
        dst = jax.random.randint(jax.random.fold_in(_gk, 3), (20000,), 0, 1250, jnp.int32)
        _o = jnp.argsort(dst, stable=True)
        src = src[_o]
        dst = dst[_o]
        return (x, src, dst)
    x, src, dst = _rec_inputs()

    def _L0_gnn_setup():
        import jax, jax.numpy as jnp
        import numpy as np
        N = 1250
        D = 512
        H = 4 * D
        E = 20000
        K = 8
        DELTA = D // K

        def _gcn_conv(x, W, b, src, dst, norm, n):
            msgs = x[src] * norm[:, None]
            agg = jax.ops.segment_sum(msgs, dst, num_segments=n)
            return agg @ W + b
        key = jax.random.key(seed)
        k0, k1, k2, k3, k4, k5 = jax.random.split(key, 6)
        x_all = jax.random.normal(k0, (N, D), dtype=jnp.float32)
        edge_index = jax.random.randint(k1, (2, E), 0, N, dtype=jnp.int64)
        s1 = 1.0 / np.sqrt(D)
        s2 = 1.0 / np.sqrt(H)
        W1 = jax.random.uniform(k2, (D, H), jnp.float32, -s1, s1)
        b1 = jnp.zeros((H,), jnp.float32)
        W2 = jax.random.uniform(k3, (H, D), jnp.float32, -s2, s2)
        b2 = jnp.zeros((D,), jnp.float32)
        return {'x_all': x_all, 'max_iter': 10, 'ix': 0, 'edge_index': edge_index, 'aug_loss': 0, 'W1': W1, 'b1': b1, 'W2': W2, 'b2': b2}
    _L0_gnn_all = _L0_gnn_setup()
    _L0_gnn_in = {k: v for k, v in _L0_gnn_all.items() if k in ('W1', 'b1', 'W2', 'b2')}
    del _L0_gnn_all

    def _L0_ffn_setup():
        import jax, jax.numpy as jnp
        import numpy as np
        B, S, D, H, E = (4, 256, 512, 8, 8)
        FF = 4 * D
        HD = D // H
        EPS = 1e-05

        def _layernorm(x, g, b):
            mu = jnp.mean(x, axis=-1, keepdims=True)
            var = jnp.mean((x - mu) ** 2, axis=-1, keepdims=True)
            return (x - mu) * jax.lax.rsqrt(var + EPS) * g + b
        key = jax.random.key(seed)
        ks = jax.random.split(key, 16)
        s = 0.02
        return {'x': jax.random.normal(ks[0], (B, S, D), dtype=jnp.float32), 'ln1_g': jnp.ones((D,), jnp.float32), 'ln1_b': jnp.zeros((D,), jnp.float32), 'Wq': jax.random.normal(ks[1], (D, D), jnp.float32) * s, 'bq': jnp.zeros((D,), jnp.float32), 'Wk': jax.random.normal(ks[2], (D, D), jnp.float32) * s, 'bk': jnp.zeros((D,), jnp.float32), 'Wv': jax.random.normal(ks[3], (D, D), jnp.float32) * s, 'bv': jnp.zeros((D,), jnp.float32), 'Wo': jax.random.normal(ks[4], (D, D), jnp.float32) * s, 'bo': jnp.zeros((D,), jnp.float32), 'gate_W': jax.random.normal(ks[5], (D, E), jnp.float32) * s, 'gate_b': jnp.zeros((E,), jnp.float32), 'W1': jax.random.normal(ks[6], (E, D, FF), jnp.float32) * s, 'b1': jnp.zeros((E, FF), jnp.float32), 'W2': jax.random.normal(ks[7], (E, FF, D), jnp.float32) * s, 'b2': jnp.zeros((E, D), jnp.float32)}
    _L0_ffn_all = _L0_ffn_setup()
    _L0_ffn_in = {k: v for k, v in _L0_ffn_all.items() if k in ('ln1_g', 'ln1_b', 'Wq', 'bq', 'Wk', 'bk', 'Wv', 'bv', 'Wo', 'bo', 'gate_W', 'gate_b', 'W1', 'b1', 'W2', 'b2')}
    del _L0_ffn_all

    def _L1_gnn_setup():
        import jax, jax.numpy as jnp
        import numpy as np
        N_NODES = 4096
        N_EDGES = 32768
        D = 512
        NUM_EXPERTS = 4
        TOP_K = 2
        LAYERS = 2
        key = jax.random.key(seed)
        ks = jax.random.split(key, 8)
        x = jax.random.normal(ks[0], (N_NODES, D), dtype=jnp.float32)
        edge_index = jax.random.randint(ks[1], (2, N_EDGES), 0, N_NODES, dtype=jnp.int64)
        s = 1.0 / np.sqrt(D)
        gate_W = jax.random.uniform(ks[2], (D, NUM_EXPERTS), jnp.float32, -s, s)
        gate_b = jax.random.uniform(ks[3], (NUM_EXPERTS,), jnp.float32, -s, s)
        Wl = jax.random.uniform(ks[4], (NUM_EXPERTS, LAYERS, D, D), jnp.float32, -s, s)
        bl = jax.random.uniform(ks[5], (NUM_EXPERTS, LAYERS, D), jnp.float32, -s, s)
        Wr = jax.random.uniform(ks[6], (NUM_EXPERTS, LAYERS, D, D), jnp.float32, -s, s)
        return {'x': x, 'gate_W': gate_W, 'gate_b': gate_b, 'Wl': Wl, 'bl': bl, 'Wr': Wr, 'edge_index': edge_index}
    _L1_gnn_all = _L1_gnn_setup()
    _L1_gnn_in = {k: v for k, v in _L1_gnn_all.items() if k in ('gate_W', 'gate_b', 'Wl', 'bl', 'Wr')}
    del _L1_gnn_all

    def _L1_ffn_setup():
        import jax, jax.numpy as jnp
        import numpy as np
        B, S, D, F, E = (8, 512, 512, 256, 8)
        INIT_LAMBDA = 0.2
        LN_EPS = 1e-05
        LN_MERGE = 0.03
        key = jax.random.key(seed)
        ks = jax.random.split(key, 12)
        n = lambda k, shp, s=1.0: jax.random.normal(k, shp, dtype=jnp.float32) * s
        return {'hidden_states': n(ks[0], (B, S, D)), 'gfc1_w': n(ks[1], (D, D), 0.01), 'gfc1_b': jnp.zeros((D,), jnp.float32), 'gfc2_w': n(ks[2], (E, D), 0.01), 'gfc2_b': jnp.full((E,), INIT_LAMBDA, dtype=jnp.float32), 'W1': n(ks[3], (F, D), 0.02), 'b1': jnp.zeros((F,), jnp.float32), 'W2': n(ks[4], (D, F), 0.02), 'b2': jnp.zeros((D,), jnp.float32), 'ln_g': jnp.ones((D,), jnp.float32), 'ln_b': jnp.zeros((D,), jnp.float32), 'tv_W1': n(ks[5], (E, F, D), 0.02), 'tv_b1': n(ks[6], (E, F), 0.02), 'tv_W2': n(ks[7], (E, D, F), 0.02), 'tv_b2': n(ks[8], (E, D), 0.02), 'tv_ln_g': n(ks[9], (E, D), 0.02), 'tv_ln_b': n(ks[10], (E, D), 0.02)}
    _L1_ffn_all = _L1_ffn_setup()
    _L1_ffn_in = {k: v for k, v in _L1_ffn_all.items() if k in ('gfc1_w', 'gfc1_b', 'gfc2_w', 'gfc2_b', 'W1', 'b1', 'W2', 'b2', 'ln_g', 'ln_b', 'tv_W1', 'tv_b1', 'tv_W2', 'tv_b2', 'tv_ln_g', 'tv_ln_b')}
    del _L1_ffn_all
    return {'x': x, 'src': src, 'dst': dst, 'L0_gnn_W1': _L0_gnn_in['W1'], 'L0_gnn_b1': _L0_gnn_in['b1'], 'L0_gnn_W2': _L0_gnn_in['W2'], 'L0_gnn_b2': _L0_gnn_in['b2'], 'L0_ffn_ln1_g': _L0_ffn_in['ln1_g'], 'L0_ffn_ln1_b': _L0_ffn_in['ln1_b'], 'L0_ffn_Wq': _L0_ffn_in['Wq'], 'L0_ffn_bq': _L0_ffn_in['bq'], 'L0_ffn_Wk': _L0_ffn_in['Wk'], 'L0_ffn_bk': _L0_ffn_in['bk'], 'L0_ffn_Wv': _L0_ffn_in['Wv'], 'L0_ffn_bv': _L0_ffn_in['bv'], 'L0_ffn_Wo': _L0_ffn_in['Wo'], 'L0_ffn_bo': _L0_ffn_in['bo'], 'L0_ffn_gate_W': _L0_ffn_in['gate_W'], 'L0_ffn_gate_b': _L0_ffn_in['gate_b'], 'L0_ffn_W1': _L0_ffn_in['W1'], 'L0_ffn_b1': _L0_ffn_in['b1'], 'L0_ffn_W2': _L0_ffn_in['W2'], 'L0_ffn_b2': _L0_ffn_in['b2'], 'L1_gnn_gate_W': _L1_gnn_in['gate_W'], 'L1_gnn_gate_b': _L1_gnn_in['gate_b'], 'L1_gnn_Wl': _L1_gnn_in['Wl'], 'L1_gnn_bl': _L1_gnn_in['bl'], 'L1_gnn_Wr': _L1_gnn_in['Wr'], 'L1_ffn_gfc1_w': _L1_ffn_in['gfc1_w'], 'L1_ffn_gfc1_b': _L1_ffn_in['gfc1_b'], 'L1_ffn_gfc2_w': _L1_ffn_in['gfc2_w'], 'L1_ffn_gfc2_b': _L1_ffn_in['gfc2_b'], 'L1_ffn_W1': _L1_ffn_in['W1'], 'L1_ffn_b1': _L1_ffn_in['b1'], 'L1_ffn_W2': _L1_ffn_in['W2'], 'L1_ffn_b2': _L1_ffn_in['b2'], 'L1_ffn_ln_g': _L1_ffn_in['ln_g'], 'L1_ffn_ln_b': _L1_ffn_in['ln_b'], 'L1_ffn_tv_W1': _L1_ffn_in['tv_W1'], 'L1_ffn_tv_b1': _L1_ffn_in['tv_b1'], 'L1_ffn_tv_W2': _L1_ffn_in['tv_W2'], 'L1_ffn_tv_b2': _L1_ffn_in['tv_b2'], 'L1_ffn_tv_ln_g': _L1_ffn_in['tv_ln_g'], 'L1_ffn_tv_ln_b': _L1_ffn_in['tv_ln_b']}

def reference(x, src, dst, L0_gnn_W1, L0_gnn_b1, L0_gnn_W2, L0_gnn_b2, L0_ffn_ln1_g, L0_ffn_ln1_b, L0_ffn_Wq, L0_ffn_bq, L0_ffn_Wk, L0_ffn_bk, L0_ffn_Wv, L0_ffn_bv, L0_ffn_Wo, L0_ffn_bo, L0_ffn_gate_W, L0_ffn_gate_b, L0_ffn_W1, L0_ffn_b1, L0_ffn_W2, L0_ffn_b2, L1_gnn_gate_W, L1_gnn_gate_b, L1_gnn_Wl, L1_gnn_bl, L1_gnn_Wr, L1_ffn_gfc1_w, L1_ffn_gfc1_b, L1_ffn_gfc2_w, L1_ffn_gfc2_b, L1_ffn_W1, L1_ffn_b1, L1_ffn_W2, L1_ffn_b2, L1_ffn_ln_g, L1_ffn_ln_b, L1_ffn_tv_W1, L1_ffn_tv_b1, L1_ffn_tv_W2, L1_ffn_tv_b2, L1_ffn_tv_ln_g, L1_ffn_tv_ln_b):
    import jax
    import jax.numpy as jnp

    def _L0_gnn_ref(x_all, max_iter, ix, edge_index, aug_loss, W1, b1, W2, b2):
        import jax, jax.numpy as jnp
        import numpy as np
        N = 1250
        D = 512
        H = 4 * D
        E = 20000
        K = 8
        DELTA = D // K

        def _gcn_conv(x, W, b, src, dst, norm, n):
            msgs = x[src] * norm[:, None]
            agg = jax.ops.segment_sum(msgs, dst, num_segments=n)
            return agg @ W + b
        n = x_all.shape[0]
        loop = jnp.arange(n, dtype=edge_index.dtype)
        src = jnp.concatenate([edge_index[0], loop])
        dst = jnp.concatenate([edge_index[1], loop])
        deg = jax.ops.segment_sum(jnp.ones_like(src, dtype=x_all.dtype), dst, num_segments=n)
        dinv = jnp.where(deg > 0, jax.lax.rsqrt(deg), 0.0)
        norm = dinv[src] * dinv[dst]
        x = _gcn_conv(x_all, W1, b1, src, dst, norm, n)
        z = jax.nn.relu(x)
        z = _gcn_conv(z, W2, b2, src, dst, norm, n)
        zk = z.reshape(n, K, DELTA)
        nrm = jnp.sqrt(jnp.sum(zk * zk, axis=2, keepdims=True))
        zk = zk / jnp.maximum(nrm, 1e-12)
        return zk.reshape(n, D)

    def _L0_ffn_ref(x, ln1_g, ln1_b, Wq, bq, Wk, bk, Wv, bv, Wo, bo, gate_W, gate_b, W1, b1, W2, b2):
        import jax, jax.numpy as jnp
        import numpy as np
        B, S, D, H, E = (4, 256, 512, 8, 8)
        FF = 4 * D
        HD = D // H
        EPS = 1e-05

        def _layernorm(x, g, b):
            mu = jnp.mean(x, axis=-1, keepdims=True)
            var = jnp.mean((x - mu) ** 2, axis=-1, keepdims=True)
            return (x - mu) * jax.lax.rsqrt(var + EPS) * g + b
        b, s, d = x.shape
        q = (x @ Wq + bq).reshape(b, s, H, HD)
        k = (x @ Wk + bk).reshape(b, s, H, HD)
        v = (x @ Wv + bv).reshape(b, s, H, HD)
        scores = jnp.einsum('bqhd,bkhd->bhqk', q, k) / jnp.sqrt(jnp.float32(HD))
        attn = jax.nn.softmax(scores, axis=-1)
        o = jnp.einsum('bhqk,bkhd->bqhd', attn, v).reshape(b, s, d) @ Wo + bo
        h = _layernorm(x + o, ln1_g, ln1_b)
        t = h.reshape(b * s, d)
        probs = jax.nn.softmax(t @ gate_W + gate_b, axis=-1)
        idx = jnp.argmax(probs, axis=-1)
        gw = jnp.max(probs, axis=-1)
        hid = jax.nn.gelu(jnp.einsum('nd,edf->enf', t, W1) + b1[:, None, :])
        out_all = jnp.einsum('enf,efd->end', hid, W2) + b2[:, None, :]
        onehot = jax.nn.one_hot(idx, E, dtype=t.dtype)
        out = jnp.einsum('ne,end->nd', onehot, out_all)
        out = out * gw[:, None]
        return out.reshape(b, s, d)

    def _L1_gnn_ref(x, gate_W, gate_b, Wl, bl, Wr, edge_index):
        import jax, jax.numpy as jnp
        import numpy as np
        N_NODES = 4096
        N_EDGES = 32768
        D = 512
        NUM_EXPERTS = 4
        TOP_K = 2
        LAYERS = 2
        n = x.shape[0]
        src, dst = (edge_index[0], edge_index[1])
        gates = jax.nn.softmax(x @ gate_W + gate_b, axis=-1)
        top_v, top_i = jax.lax.top_k(gates, TOP_K)
        deg = jax.ops.segment_sum(jnp.ones((src.shape[0],), x.dtype), dst, num_segments=n)
        inv_deg = jnp.where(deg > 0, 1.0 / jnp.maximum(deg, 1.0), 0.0)[:, None]

        def sage_conv(h, W_l, b_l, W_r):
            aggr = jax.ops.segment_sum(h[src], dst, num_segments=n) * inv_deg
            return aggr @ W_l + b_l + h @ W_r
        expert_outs = []
        for e in range(NUM_EXPERTS):
            h = x
            for l in range(LAYERS):
                h = sage_conv(h, Wl[e, l], bl[e, l], Wr[e, l])
                h = jax.nn.relu(h)
            expert_outs.append(h)
        expert_outputs = jnp.stack(expert_outs, axis=1)
        sel = jnp.take_along_axis(expert_outputs, top_i[:, :, None], axis=1)
        out = jnp.sum(sel * top_v[:, :, None], axis=1)
        return out

    def _L1_ffn_ref(hidden_states, gfc1_w, gfc1_b, gfc2_w, gfc2_b, W1, b1, W2, b2, ln_g, ln_b, tv_W1, tv_b1, tv_W2, tv_b2, tv_ln_g, tv_ln_b):
        import jax, jax.numpy as jnp
        import numpy as np
        B, S, D, F, E = (8, 512, 512, 256, 8)
        INIT_LAMBDA = 0.2
        LN_EPS = 1e-05
        LN_MERGE = 0.03
        x = hidden_states
        gh = jax.nn.relu(jnp.einsum('bsd,hd->bsh', x, gfc1_w) + gfc1_b)
        g = (jnp.einsum('bsh,eh->bse', gh, gfc2_w) + gfc2_b).mean(axis=1)
        W1m = W1 + jnp.einsum('be,efd->bfd', g, tv_W1)
        b1m = b1 + g @ tv_b1
        W2m = W2 + jnp.einsum('be,edf->bdf', g, tv_W2)
        b2m = b2 + g @ tv_b2
        lng = ln_g + LN_MERGE * (tv_ln_g - ln_g).sum(axis=0)
        lnb = ln_b + LN_MERGE * (tv_ln_b - ln_b).sum(axis=0)
        h = jax.nn.relu(jnp.einsum('bsd,bfd->bsf', x, W1m) + b1m[:, None, :])
        out = jnp.einsum('bsf,bdf->bsd', h, W2m) + b2m[:, None, :]
        res = x + out
        mu = res.mean(axis=-1, keepdims=True)
        var = res.var(axis=-1, keepdims=True)
        return (res - mu) * jax.lax.rsqrt(var + LN_EPS) * lng + lnb
    edge_index = jnp.stack([src, dst])
    x = x + _L0_gnn_ref(_layernorm(x, axis=-1), 10, 0, edge_index, 0, L0_gnn_W1, L0_gnn_b1, L0_gnn_W2, L0_gnn_b2)
    x = x + _L0_ffn_ref(_layernorm(x, axis=-1)[None], L0_ffn_ln1_g, L0_ffn_ln1_b, L0_ffn_Wq, L0_ffn_bq, L0_ffn_Wk, L0_ffn_bk, L0_ffn_Wv, L0_ffn_bv, L0_ffn_Wo, L0_ffn_bo, L0_ffn_gate_W, L0_ffn_gate_b, L0_ffn_W1, L0_ffn_b1, L0_ffn_W2, L0_ffn_b2)[0]
    x = x + _L1_gnn_ref(_layernorm(x, axis=-1), L1_gnn_gate_W, L1_gnn_gate_b, L1_gnn_Wl, L1_gnn_bl, L1_gnn_Wr, edge_index)
    x = x + _L1_ffn_ref(_layernorm(x, axis=-1)[None], L1_ffn_gfc1_w, L1_ffn_gfc1_b, L1_ffn_gfc2_w, L1_ffn_gfc2_b, L1_ffn_W1, L1_ffn_b1, L1_ffn_W2, L1_ffn_b2, L1_ffn_ln_g, L1_ffn_ln_b, L1_ffn_tv_W1, L1_ffn_tv_b1, L1_ffn_tv_W2, L1_ffn_tv_b2, L1_ffn_tv_ln_g, L1_ffn_tv_ln_b)[0]
    return x

_drawn_inputs = setup_inputs


def setup_inputs(seed=0):
    import zlib

    import numpy as np

    out = dict(_drawn_inputs(seed))
    spreads = {'L0_gnn_b1': (0.0, 0.1),
     'L0_gnn_b2': (0.0, 0.1),
     'L0_ffn_ln1_g': (1.0, 0.2),
     'L0_ffn_ln1_b': (0.0, 0.44),
     'L0_ffn_bq': (0.0, 0.8),
     'L0_ffn_bk': (0.0, 2.0),
     'L0_ffn_bv': (0.0, 0.696),
     'L0_ffn_bo': (0.0, 1.281),
     'L0_ffn_gate_b': (0.0, 0.1),
     'L0_ffn_b1': (0.0, 0.611),
     'L0_ffn_b2': (0.0, 0.322),
     'L1_ffn_gfc1_b': (0.0, 0.8),
     'L1_ffn_gfc2_b': (0.20000000298023224, 0.6),
     'L1_ffn_b1': (0.0, 0.684),
     'L1_ffn_b2': (0.0, 0.366),
     'L1_ffn_ln_g': (1.0, 0.2),
     'L1_ffn_ln_b': (0.0, 0.1)}
    factors = {'L0_gnn_W1': 3.156,
     'L0_ffn_Wq': 8.0,
     'L0_ffn_Wk': 8.0,
     'L0_ffn_Wv': 7.21,
     'L0_ffn_Wo': 4.757,
     'L1_gnn_gate_b': 4.861,
     'L1_gnn_bl': 5.734,
     'L1_ffn_gfc1_w': 8.0,
     'L1_ffn_gfc2_w': 8.0,
     'L1_ffn_tv_b1': 8.0,
     'L1_ffn_tv_b2': 8.0,
     'L1_ffn_tv_ln_g': 48.037,
     'L1_ffn_tv_ln_b': 52.376}
    for name, (base, spread) in spreads.items():
        noise = np.random.default_rng([zlib.crc32(name.encode()), seed]).standard_normal(out[name].shape)
        drawn = base * np.exp(spread * noise) if base else spread * noise
        out[name] = jnp.asarray(drawn.astype(out[name].dtype))
    for name, factor in factors.items():
        out[name] = (out[name] * factor).astype(out[name].dtype)
    return out
```

```python
from contextlib import ExitStack

import concourse.bass as bass
from concourse import mybir

F32 = mybir.dt.float32
F32R = mybir.dt.float32r
F16 = mybir.dt.float16
I32 = mybir.dt.int32
U32 = mybir.dt.uint32
ALU = mybir.AluOpType
ACT = mybir.ActivationFunctionType
AX = mybir.AxisListType.X

N = 1250
NE = 20000
P = 125
NT = N // P
D = 512
KD = D // 128
FF = 2048
KF = FF // 128
HEADS, HD = 8, 64
EXPERTS = 8
SAGE = 4
MF = 256
KM = MF // 128
EPS = 1e-5
CHUNKS = [(0, 500), (500, 500), (1000, 250)]
TILES_OF = [range(0, 4), range(4, 8), range(8, 10)]
HALF = N // 2
FIELD = 4096.0
GROUP = 32
GROUPS = NE // P // GROUP
PACKED = HALF // P
DCH = 418
NDC = 3
ST = (N - EXPERTS) // 128 + EXPERTS
SLOT_ROWS = ST * 128
MOST = -(-N // 128)
NPAD = DCH * NDC
SLOTS = 8


class UnitPlan:

    def __init__(self, phases):
        self.at, units, v, a = {}, 0, 0, 0
        for name, owners, times in phases:
            self.at[name] = (units, v, a, owners)
            units += len(owners) * times
            v += owners.count("V") * times
            a += owners.count("A") * times

    def ready(self, name, k, i=0):
        units, _, _, owners = self.at[name]
        return i * len(owners) + (units + k + 1)

    def taken(self, name, k, i=0):
        _, v, a, owners = self.at[name]
        return (i * owners.count("V") + (v + owners[:k].count("V")),
                i * owners.count("A") + (a + owners[:k].count("A")))

    def size(self, name):
        return len(self.at[name][3])


def program(nc, t, out, spill, rows_x, rows_y):
    U = UnitPlan([
        ("degree", "AAAA", 1),
        ("agg1", "V" * 12, 1),
        ("gcn", ("VA" * 8 + "VV") * 5, 1),
        ("agg2", "V" * NT, 1),
        ("xt1", "VA" * 5, 1),
        ("qkv", "VA" * 12 + "V" * NT, 1),
        ("ot", "VA" * 5, 1),
        ("wo", "V" * NT, 1),
        ("ht", "VA" * 5, 1),
        ("gate", "VVV", 1),
        ("rows", "VA" * (ST // 2) + "V" * (ST % 2), 1),
        ("xt2", "VA" * 5, 1),
        ("gate2", "V", 1),
        ("degree2", "VVV", 1),
        ("agg3", "V" * 12, 1),
        ("sage", "V" * NT + "VVVVAAVV" * 5, SAGE),
        ("xt3", "VA" * 5, 1),
        ("gh", "A" * 12, 1),
        ("merge", "VVVVV", 1),
        ("up", "A" * 6, 1),
        ("down", "V" * NT, 1),
    ])

    ctx = ExitStack()
    with ctx:
        def sem(name):
            return ctx.enter_context(nc.semaphore(name))

        PS = ctx.enter_context(nc.psum_tensor("PS", [128, 8, 512], F32))

        BASE = 16512
        TOP = 229344

        def at(name, shape, dt, off):
            size = 2 if dt == F16 else 4
            for s in shape[1:]:
                size *= s
            assert BASE + off + size <= TOP, (name, BASE + off + size - TOP)
            return nc.alloc_sbuf_tensor_at(name, shape, dt, offset=BASE + off), off + (size + 31) // 32 * 32

        o = 0
        ident, o = at("ident", [128, 128], F32, o)
        identr, o = at("identr", [128, 128], F32R, o)
        onesr, o = at("onesr", [128, 128], F32R, o)
        eps, o = at("eps", [128, 1], F32, o)
        bnst, o = at("bnst", [P, NT, 6], F32, o)
        mv, o = at("mv", [P, NT, 2], F32, o)
        std, o = at("std", [P, NT], F32, o)
        rstd, o = at("rstd", [P, NT], F32, o)
        dcol, o = at("dcol", [P, NT], F32, o)
        l0b1, o = at("l0b1", [128, KF], F32, o)
        bq, o = at("bq", [128, KD], F32, o)
        bk, o = at("bk", [128, KD], F32, o)
        b1e, o = at("b1e", [128, EXPERTS + 2, KF], F32, o)
        b1c, o = at("b1c", [128, 2, KF], F32, o)
        tri, o = at("tri", [128, 128], F32, o)
        ones, o = at("ones", [128, 128], F32, o)
        before, o = at("before", [P, NT, EXPERTS], F32, o)
        inall, o = at("inall", [P, NT, EXPERTS], F32, o)
        count, o = at("count", [P, EXPERTS], F32, o)
        counti, o = at("counti", [P, EXPERTS], I32, o)
        tilesf, o = at("tilesf", [P, EXPERTS], F32, o)
        startf, o = at("startf", [P, EXPERTS], F32, o)
        start128, o = at("start128", [P, EXPERTS], F32, o)
        table, o = at("table", [P, 3 * EXPERTS], I32, o)
        slotf, o = at("slotf", [P, NT], F32, o)
        sloti, o = at("sloti", [P, NT], U32, o)
        topw, o = at("topw", [P, NT], F32, o)
        gbc, o = at("gbc", [128, EXPERTS], F32, o)
        ga, o = at("ga", [P, NT, EXPERTS], F32, o)
        gc, o = at("gc", [P, NT, SAGE], F32, o)
        gb, o = at("gb", [P, NT, EXPERTS], F32, o)
        wexp, o = at("wexp", [P, NT, EXPERTS], F32, o)
        gs, o = at("gs", [P, 4, NT], F32, o)
        idx8, o = at("idx8", [P, EXPERTS], F32, o)
        assert o <= 7680, o
        X, o = at("X", [P, NT, D], F32, 7680)
        A0 = o
        AT, o = at("AT", [P, NT, NPAD], F32R, A0)
        f0 = o
        aggT, _ = at("aggT", [128, KD, N], F32, 7680)
        zrow, _ = at("zrow", [128, D], F32, 7680)
        XS, _ = at("XS", [P, NT, D], F32, 7680)
        rowbc, o = at("rowbc", [128, NPAD], F32, f0)
        XH, oh = at("XH", [P, NT, D], F32R, o)
        XL, o2 = at("XL", [P, NT, D], F32R, oh)
        e0 = o
        srci, e0 = at("srci", [P, NE // P], I32, e0)
        dsti, e0 = at("dsti", [P, NE // P], I32, e0)
        srcf, e0 = at("srcf", [P, NE // P], F32, e0)
        dstf, e0 = at("dstf", [P, NE // P], F32, e0)
        srcw, e0 = at("srcw", [P, NE // P], F32, e0)
        srcq, e0 = at("srcq", [P, NE // P], F32, e0)
        edge, e0 = at("edge", [P, 3, GROUP], F32, e0)
        iota, e0 = at("iota", [P, NPAD], F16, e0)
        ohs, e0 = at("ohs", [P, SLOTS, HALF], F16, e0)
        ohd, e0 = at("ohd", [P, SLOTS, DCH], F16, e0)
        cnt, e0 = at("cnt", [P, PACKED, DCH], I32, e0)
        assert e0 <= o2, (e0, o2)
        W1, o3 = at("W1", [128, KD, FF], F32, o2)
        ZF, _ = at("ZF", [P, NT, D], F32, o2)
        b2bc, _ = at("b2bc", [P, D], F32, o2 + 20480)
        W2, o4 = at("W2", [128, KF, D], F32, o3)
        x0, _ = at("x0", [P, NT, D], F32, o3)
        cnthi, _ = at("cnthi", [P, PACKED, DCH], I32, o2)
        cntlo, _ = at("cntlo", [P, PACKED, DCH], I32, o2 + 8384)
        zT, o5 = at("zT", [128, KF, 250], F32, o4)
        zsq, _ = at("zsq", [P, 2, D], F32, o4)
        znr, _ = at("znr", [P, NT, 8], F32, o4 + 4096)
        XNT, o = at("XNT", [128, KD, N], F32, A0)
        O, o = at("O", [P, NT, D], F32, A0)
        XN, o = at("XN", [P, NT, D], F32, o)
        qT, oq = at("qT", [128, KD, N], F32, o)
        OT, _ = at("OT", [128, KD, N], F32, o)
        kT, o = at("kT", [128, KD, N], F32, oq)
        V, o = at("V", [P, NT, D], F32, o)
        Wq, o = at("Wq", [128, KD, D], F32, o)
        Wk, o = at("Wk", [128, KD, D], F32, o)
        Wv, o = at("Wv", [128, KD, D], F32, o)
        qs, o = at("qs", [HD, 2, N], F32, o)
        ks, o = at("ks", [HD, 2, N], F32, o)
        Pr, o = at("Pr", [P, 2, N], F32, o)
        PT, o = at("PT", [P, 2, NT, P], F32, o)
        bvbc, o = at("bvbc", [P, D], F32, o)
        bobc, o = at("bobc", [P, D], F32, o)
        lngbc, o = at("lngbc", [P, D], F32, o)
        lnbbc, o = at("lnbbc", [P, D], F32, o)
        smm, o = at("smm", [P, 2, 3], F32, o)
        smb, o = at("smb", [P, 2], F32, o)
        sms, o = at("sms", [P, 2, 3], F32, o)
        smr, o = at("smr", [P, 4], F32, o)
        rowsT, o = at("rowsT", [128, KD, SLOT_ROWS], F32, A0)
        outrow, o = at("outrow", [128, D], F32, o)
        b2s, o = at("b2s", [128, 2, D], F32, o)
        assert o <= A0 + 40960
        We, o = at("We", [128, 2, KD * FF + KF * D], F32, A0 + 40960)
        rows_in, _ = at("rows_in", [128, ST, D], F32, A0 + 40960 + 65536)
        hid, o = at("hid", [128, KF, 128], F32, o)
        W1e = We[:, :, 0:KD * FF].rearrange("p s (k n) -> p s k n", k=KD)
        W2e = We[:, :, KD * FF:].rearrange("p s (k n) -> p s k n", k=KF)
        gW, _ = at("gW", [128, KD, EXPERTS], F32, o)
        gbias, _ = at("gbias", [P, EXPERTS], F32, o + 128)
        back, _ = at("back", [P, NT, D], F32, f0)
        XNT3, o = at("XNT3", [128, KD, N], F32, f0)
        rowbc3, o = at("rowbc3", [128, NPAD], F32, o)
        agg0, o6 = at("agg0", [128, KD, N], F32, o)
        XN3, o = at("XN3", [P, NT, D], F32, o)
        o = max(o, o6)
        HH, o = at("HH", [P, NT, D], F32R, o)
        HL, o = at("HL", [P, NT, D], F32R, o)
        Wsl, o = at("Wsl", [128, 2, KD, D], F32, o)
        Wsr, o = at("Wsr", [128, 2, KD, D], F32, o)
        aggc, o = at("aggc", [128, KD, 250], F32, o)
        hTc, o = at("hTc", [128, KD, 2, 126], F32, o)
        blbc, o = at("blbc", [P, 2, D], F32, o)
        gW2, _ = at("gW2", [128, KD, SAGE], F32, o - 4096)
        gbias2, _ = at("gbias2", [P, SAGE], F32, o - 4096 + 64)
        XNT4, o = at("XNT4", [128, KD, N], F32, A0)
        XN4, o = at("XN4", [P, NT, D], F32, o)
        g1T, o = at("g1T", [128, KD, D], F32, o)
        g1b, o = at("g1b", [128, KD], F32, o)
        g2T, o = at("g2T", [128, KD, EXPERTS], F32, o)
        g2bbc, o = at("g2bbc", [128, EXPERTS], F32, o)
        g2bcol, o = at("g2bcol", [EXPERTS, 1], F32, o)
        W1m, o = at("W1m", [128, KD, MF], F32, o)
        W2m, o = at("W2m", [128, KM, D], F32, o)
        tv, o = at("tv", [128, 4, 1024], F32, o)
        m1b, o = at("m1b", [128, KM], F32, o)
        tvb1, o = at("tvb1", [128, KM, EXPERTS], F32, o)
        tvt, o = at("tvt", [128, KM, EXPERTS], F32, o)
        tvr, o = at("tvr", [128, KM], F32, o)
        tvb2, o = at("tvb2", [EXPERTS, D], F32, o)
        tvg, o = at("tvg", [EXPERTS, D], F32, o)
        tvb, o = at("tvb", [EXPERTS, D], F32, o)
        m2bc, o = at("m2bc", [P, D], F32, o)
        mgbc, o = at("mgbc", [P, D], F32, o)
        mbbc, o = at("mbbc", [P, D], F32, o)
        c03, o = at("c03", [EXPERTS, P], F32, o)
        ghs, o = at("ghs", [128, KD, 3], F32, o)
        ghm, o = at("ghm", [128, KD], F32, o)
        ghb, o = at("ghb", [128, KD, 128], F32, o)
        gT, o = at("gT", [EXPERTS, 128], F32, o)
        upT, o = at("upT", [128, KM, N], F32, o)

        names = """unit_ready taken_by_vector taken_by_scalar vector_step scalar_step
            edges_in x_in w1_in w2_in l0b_in xback_in qkvw_in attnb_in wo_in gate_in moeb_in
            w1e_in0 w1e_in1 w2e_in0 w2e_in1 table_ready slots_ready rows_scattered rows_loaded rows_stored rows_back
            hid_ready hid_done y_ready y_taken expert_done rows_zero rows_out_ready spilled unspilled gate2_in sl_in0 sl_in1 g1_in merge_in tv_in0 tv_in1 tv_in2 tv_in3
            out_stored iota_done ident_done adj_zero onehot_slots onehots_ready counts_by_scalar
            counts_by_vector fields_read adj_ready degree_root dinv_ready
            moments_ready std_ready norm_ready split_hi split_lo h2_hi znorm_sq znorm_sum znorm_root x_ready
            staged_by_vector staged_by_scalar scores_ready rowmax_ready exp_done pt_ready pt_by_vector pt_by_scalar
            pv_ready pv_taken gate_max gate_exp gates_ready
            bias_added relu_done h1_ready relu2_done row3_ready ghm_ready gate_bc w_merged tail_ready
            const_ready tv_used resid_ready edges_staged bias_staged""".split()
        S = {n: sem(n) for n in names}

        def ready(eng, name, k, i=0):
            eng.wait_ge(S["unit_ready"], U.ready(name, k, i))

        def taken(eng, name, k, i=0):
            v, a = U.taken(name, k, i)
            eng.wait_ge(S["taken_by_vector"], v)
            eng.wait_ge(S["taken_by_scalar"], a)

        def bank(name, k):
            return PS[:, k % 8, :]

        SAGE_V = U.at["sage"][3].count("V")
        block = ctx.enter_context(nc.Block())

        def bcast(v, n=P):
            return v.rearrange("(a d) -> a d", a=1).to_broadcast([n, v.shape[0]])

        def tiles(v):
            return v.rearrange("(t p) d -> p t d", p=P)

        def rows(v):
            return v.rearrange("(k p) n -> p k n", p=128)

        @block.sync
        def _(sp):
            sp.dma_start(srci[:], t["src"].rearrange("(p c) -> p c", p=P)).then_inc(S["edges_in"], 16)
            sp.dma_start(dsti[:], t["dst"].rearrange("(p c) -> p c", p=P)).then_inc(S["edges_in"], 16)
            sp.dma_start(x0[:], tiles(t["x"])).then_inc(S["x_in"], 16)
            sp.dma_start(l0b1[:], t["L0_gnn_b1"]).then_inc(S["l0b_in"], 16)
            sp.dma_start(bq[:], t["L0_ffn_bq"]).then_inc(S["l0b_in"], 16)
            sp.dma_start(bk[:], t["L0_ffn_bk"]).then_inc(S["l0b_in"], 16)
            sp.dma_start(b1e[:, 0:EXPERTS], t["L0_ffn_b1"]).then_inc(S["l0b_in"], 16)
            sp.wait_ge(S["adj_ready"], 1)
            sp.dma_start(W1[:], rows(t["L0_gnn_W1"])).then_inc(S["w1_in"], 16)
            sp.wait_ge(S["norm_ready"], NT)
            sp.dma_start(W2[:], rows(t["L0_gnn_W2"])).then_inc(S["w2_in"], 16)
            ready(sp, "gcn", U.size("gcn") - 1)
            sp.dma_start(X[:], tiles(t["x"])).then_inc(S["xback_in"], 16)
            sp.dma_start(b2bc[:], bcast(t["L0_gnn_b2"])).then_inc(S["xback_in"], 16)
            sp.dma_start(spill, AT[:].bitcast(F32)).then_inc(S["spilled"], 16)
            ready(sp, "agg2", NT - 1)
            sp.wait_ge(S["x_ready"], NT)
            for w, v in ((Wq, "L0_ffn_Wq"), (Wk, "L0_ffn_Wk"), (Wv, "L0_ffn_Wv")):
                sp.dma_start(w[:], rows(t[v])).then_inc(S["qkvw_in"], 16)
            for b, v in ((bvbc, "L0_ffn_bv"), (bobc, "L0_ffn_bo"), (lngbc, "L0_ffn_ln1_g"), (lnbbc, "L0_ffn_ln1_b")):
                sp.dma_start(b[:], bcast(t[v])).then_inc(S["attnb_in"], 16)
            ready(sp, "qkv", U.size("qkv") - 1)
            sp.dma_start(Wq[:], rows(t["L0_ffn_Wo"])).then_inc(S["wo_in"], 16)
            def expert_weights(e, s):
                w1 = t["L0_ffn_W1"][bass.ds(e, 1)].rearrange("a (k p) n -> p (a k) n", p=128)
                w2 = t["L0_ffn_W2"][bass.ds(e, 1)].rearrange("a (k p) n -> p (a k) n", p=128)
                sp.dma_start(W1e[:, s], w1).then_inc(S[f"w1e_in{s}"], 16)
                sp.dma_start(W2e[:, s], w2).then_inc(S[f"w2e_in{s}"], 16)
                sp.dma_start(b2s[:, s], t["L0_ffn_b2"][bass.ds(e, 1)].to_broadcast([128, D])).then_inc(S[f"w2e_in{s}"], 16)

            ready(sp, "wo", NT - 1)
            sp.dma_start(W1e[:, 0], rows(t["L0_ffn_W1"][0])).then_inc(S["w1e_in0"], 16)
            ready(sp, "ht", NT - 1)
            sp.wait_ge(S["norm_ready"], 3 * NT)
            sp.dma_start(gW[:], rows(t["L0_ffn_gate_W"])).then_inc(S["gate_in"], 16)
            sp.dma_start(gbias[:], bcast(t["L0_ffn_gate_b"])).then_inc(S["gate_in"], 16)
            sp.dma_start(W2e[:, 0], rows(t["L0_ffn_W2"][0])).then_inc(S["w2e_in0"], 16)
            sp.wait_ge(S["rows_scattered"], 16 * NT)
            sp.dma_start(rows_in[:], rows_x.rearrange("(i p) d -> p i d", p=128)).then_inc(S["rows_loaded"], 16)
            sp.dma_start(b2s[:, 0], bcast(t["L0_ffn_b2"][0], 128)).then_inc(S["w2e_in0"], 16)
            ready(sp, "rows", ST - 1)
            expert_weights(1, 1)
            with sp.Fori(1, EXPERTS // 2) as i:
                for s in range(2):
                    sp.wait_ge(S["expert_done"], i * 2 + (s + 1))
                    expert_weights(i * 2 + s, s)
            sp.wait_ge(S["expert_done"], EXPERTS + 2)
            sp.wait_ge(S["rows_out_ready"], 1)
            sp.dma_start(AT[:].bitcast(F32), spill).then_inc(S["unspilled"], 16)
            sp.dma_start(gW2[:], rows(t["L1_gnn_gate_W"])).then_inc(S["gate2_in"], 16)
            sp.dma_start(gbias2[:], bcast(t["L1_gnn_gate_b"])).then_inc(S["gate2_in"], 16)
            sp.wait_ge(S["gates_ready"], 2)
            with sp.Fori(0, SAGE) as i:
                for l in range(2):
                    if l == 0:
                        sp.wait_ge(S["taken_by_vector"], i * SAGE_V + (U.taken("sage", NT)[0] - SAGE_V))
                    else:
                        sp.wait_ge(S["taken_by_vector"], U.taken("sage", 0, i)[0])
                    sp.wait_ge(S["gates_ready"], 2)
                    wl = t["L1_gnn_Wl"][bass.ds(i, 1), l].rearrange("a (k p) n -> p (a k) n", p=128)
                    wr = t["L1_gnn_Wr"][bass.ds(i, 1), l].rearrange("a (k p) n -> p (a k) n", p=128)
                    sp.dma_start(Wsl[:, l], wl).then_inc(S[f"sl_in{l}"], 16)
                    sp.dma_start(Wsr[:, l], wr).then_inc(S[f"sl_in{l}"], 16)
                    sp.dma_start(blbc[:, l], t["L1_gnn_bl"][bass.ds(i, 1), l].to_broadcast([P, D])).then_inc(S[f"sl_in{l}"], 16)
            taken(sp, "xt3", 0)
            ready(sp, "sage", U.size("sage") - 1, SAGE - 1)
            sp.dma_start(g1T[:], rows(t["L1_ffn_gfc1_w"])).then_inc(S["g1_in"], 16)
            sp.dma_start(g1b[:], t["L1_ffn_gfc1_b"]).then_inc(S["g1_in"], 16)
            for dst, v in ((g2T, rows(t["L1_ffn_gfc2_w"])), (g2bbc, bcast(t["L1_ffn_gfc2_b"], 128)),
                           (g2bcol, t["L1_ffn_gfc2_b"].rearrange("(e a) -> e a", a=1)),
                           (W1m, rows(t["L1_ffn_W1"])), (W2m, rows(t["L1_ffn_W2"])), (m1b, t["L1_ffn_b1"]),
                           (tvb1, t["L1_ffn_tv_b1"]), (tvb2, t["L1_ffn_tv_b2"]), (tvg, t["L1_ffn_tv_ln_g"]),
                           (tvb, t["L1_ffn_tv_ln_b"]), (m2bc, bcast(t["L1_ffn_b2"])),
                           (mgbc, bcast(t["L1_ffn_ln_g"])), (mbbc, bcast(t["L1_ffn_ln_b"]))):
                sp.dma_start(dst[:], v).then_inc(S["merge_in"], 16)
            for n in range(2 * EXPERTS):
                e, second = n // 2, n % 2
                if n >= 4:
                    sp.wait_ge(S["tv_used"], n - 3)
                v = t["L1_ffn_tv_W2"][e] if second else t["L1_ffn_tv_W1"][e]
                k = KM if second else KD
                sp.dma_start(tv[:, n % 4].rearrange("p (k n) -> p k n", k=k), rows(v)).then_inc(S[f"tv_in{n % 4}"], 16)
            n = 0
            for i in range(NT):
                sp.wait_ge(S["tail_ready"], i + 1)
                sp.dma_start(tiles(out)[:, i], XN4[:, i]).then_inc(S["out_stored"], 16)
            sp.wait_ge(S["out_stored"], 16 * NT)

        @block.gpsimd
        def _(pool):
            pool.iota(iota[:], [[1, NPAD]], base=0, channel_multiplier=0, allow_small_or_imprecise_dtypes=True).then_inc(S["iota_done"], 1)
            pool.iota(idx8[:], [[-1, EXPERTS]], base=EXPERTS, channel_multiplier=0, allow_small_or_imprecise_dtypes=True).then_inc(S["iota_done"], 1)
            pool.memset(ident[:], 0.0).then_inc(S["ident_done"], 1)
            pool.memset(onesr[:].bitcast(F32), 1.0).then_inc(S["ident_done"], 1)
            pool.memset(eps[:], EPS).then_inc(S["ident_done"], 1)
            pool.memset(tri[:], 1.0).then_inc(S["ident_done"], 1)
            pool.memset(ones[:], 1.0).then_inc(S["ident_done"], 1)
            pool.memset(b1e[:, EXPERTS:EXPERTS + 2], 0.0).then_inc(S["ident_done"], 1)
            pool.memset(zrow[:], 0.0).then_inc(S["ident_done"], 1)
            pool.wait_ge(S["ident_done"], 7)
            pool.affine_select(out=tri[:], in_=tri[:], compare_op=ALU.is_gt, fill=0.0, base=0,
                               pattern=[[1, 128]], channel_multiplier=-1).then_inc(S["ident_done"], 1)
            for v, done in ((rows_x, "rows_zero"), (rows_y, "rows_stored")):
                pool.dma_start(v.rearrange("(i p) d -> p i d", p=128),
                               zrow[:].rearrange("p (a d) -> p a d", a=1).to_broadcast([128, ST, D])).then_inc(S[done], 16)
            pool.affine_select(out=ident[:], in_=ident[:], compare_op=ALU.not_equal, fill=1.0, base=0,
                               pattern=[[-1, 128]], channel_multiplier=1).then_inc(S["ident_done"], 1)
            pool.memset(AT[:].bitcast(F32), 0.0).then_inc(S["adj_zero"], 1)
            pool.wait_ge(S["adj_zero"], 1)
            pool.memset(cnt[:, 0:3], 0).then_inc(S["counts_by_scalar"], 1)
            pool.memset(cnt[:, 3:PACKED], 0).then_inc(S["counts_by_vector"], 1)
            pool.memset(cntlo[:], 0).then_inc(S["fields_read"], 1)
            pool.wait_ge(S["attnb_in"], 64)
            ready(pool, "xt1", NT - 1)
            for i in range(NT):
                pool.tensor_tensor(XN[:, i], XN[:, i], bobc[:], ALU.add).then_inc(S["resid_ready"], 1)
            pool.wait_ge(S["slots_ready"], 1)
            pool.wait_ge(S["norm_ready"], 3 * NT)
            pool.wait_ge(S["rows_zero"], 16)
            for i in range(NT):
                pool.indirect_dma_start(rows_x[:, :], bass.IndirectOffsetOnAxis(ap=sloti[:, i:i + 1], axis=0), XN[:, i], None).then_inc(S["rows_scattered"], 16)
            pool.wait_ge(S["table_ready"], 1)
            with pool.Fori(0, EXPERTS) as e:
                n = pool.value_load(table[0:1, bass.ds(e, 1)], min_val=0, max_val=MOST)
                start = pool.value_load(table[0:1, bass.ds(e + EXPERTS, 1)], min_val=0, max_val=ST)
                with pool.Fori(0, MOST) as m:
                    with pool.If(m < n):
                        i = nc.s_assert_within(start + m, 0, ST - 1, skip_runtime_bounds_check_because="the experts' tiles add up to at most ST")
                        pool.wait_ge(S["y_taken"], i + 2)
                        pool.dma_start(rows_y[bass.ds(i * 128, 128), :], outrow[:]).then_inc(S["rows_stored"], 16)
            pool.wait_ge(S["rows_out_ready"], 1)
            for i in range(NT):
                pool.indirect_dma_start(back[:, i], None, rows_y[:, :], bass.IndirectOffsetOnAxis(ap=sloti[:, i:i + 1], axis=0)).then_inc(S["rows_back"], 16)

        def pt_out_scalar(act, b, i):
            act.wait_ge(S["pt_ready"], b * 60 + (3 * i + 2))
            if i >= 2:
                act.wait_ge(S["pv_ready"], b * 20 + (i - 1))
            act.activation(PT[:, i % 2, 4:8, :], PS[0:P, 4 + (3 * i + 1) % 3, 0:500].rearrange("p (k n) -> p k n", n=P),
                           ACT.Copy).then_inc(S["pt_by_scalar"], 1)

        @block.scalar
        def _(act):
            TV, TA = S["taken_by_vector"], S["taken_by_scalar"]
            def root(k):
                act.wait_ge(S["moments_ready"], NT * (k + 1))
                if k:
                    act.wait_ge(S["std_ready"], k)
                act.activation(std[:], mv[:, :, 1], ACT.Sqrt, bias=eps[0:P, :]).then_inc(S["std_ready"], 1)

            act.wait_ge(S["ident_done"], 9)
            root(0)
            with act.Fori(0, GROUPS) as g:
                for j in range(NDC):
                    act.wait_ge(S["onehot_slots"], g * (NDC * GROUP) + (SLOTS + (j + 1) * GROUP))
                    act.wait_ge(S["fields_read"], g * NDC + (j + 1))
                    for r in range(3):
                        ins = act.activation(cnt[:, r], PS[0:P, r, 0:DCH], ACT.Copy)
                    ins.then_inc(S["counts_by_scalar"], 1)
            for k in range(3):
                ready(act, "degree", k)
                act.activation(rowbc[:, k * DCH:(k + 1) * DCH], bank("degree", k)[:, 0:DCH], ACT.Sqrt).then_inc(TA, 1)
            ready(act, "degree", 3)
            act.activation(dcol[:], bank("degree", 3)[0:P, 0:2 * NT].rearrange("p (t a) -> p t a", a=2)[:, :, 0], ACT.Sqrt).then_inc(TA, 1)
            for i in range(NT):
                act.wait_ge(S["norm_ready"], i + 1)
                act.activation(XH[:, i], XS[:, i], ACT.Copy).then_inc(S["split_hi"], 1)
            act.wait_ge(S["l0b_in"], 64)
            for c in range(5):
                for f in range(1, KF, 2):
                    k = 18 * c + f
                    ready(act, "gcn", k)
                    act.activation(zT[:, f], bank("gcn", k)[:, 0:250], ACT.Relu, bias=l0b1[:, f:f + 1]).then_inc(TA, 1)
                for i in range(2):
                    k, tt = 18 * c + KF + i, 2 * c + i
                    ready(act, "gcn", k)
                    act.activation(XH[:, tt], bank("gcn", k)[0:P, :], ACT.Copy, scale=dcol[:, tt:tt + 1]).then_inc(S["h2_hi"], 1)
            for i in range(NT):
                taken(act, "agg2", i + 1)
                if i >= 2:
                    act.wait_ge(S["znorm_sum"], i - 1)
                act.activation(zsq[:, i % 2], ZF[:, i], ACT.Square).then_inc(S["znorm_sq"], 1)
            act.wait_ge(S["znorm_sum"], NT)
            act.activation(znr[:], znr[:], ACT.Sqrt).then_inc(S["znorm_root"], 1)
            root(1)

            def transposed(name, dst, stride=P):
                for i in range(1, NT, 2):
                    ready(act, name, i)
                    act.activation(dst[:, :, i * P:(i + 1) * P], bank(name, i)[:, 0:KD * P].rearrange("p (k n) -> p k n", k=KD),
                                   ACT.Copy).then_inc(TA, 1)

            transposed("xt1", XNT)
            for n in range(1, 24, 2):
                f, c = (n % 12) // 3, n % 3
                lo, w = CHUNKS[c]
                ready(act, "qkv", n)
                if n < 12:
                    act.wait_ge(S["const_ready"], 1)
                    act.activation(qT[:, f, lo:lo + w], bank("qkv", n)[:, 0:w], ACT.Identity, bias=bq[:, f:f + 1], scale=-0.125).then_inc(TA, 1)
                else:
                    act.activation(kT[:, f, lo:lo + w], bank("qkv", n)[:, 0:w], ACT.Identity, bias=bk[:, f:f + 1]).then_inc(TA, 1)
            with act.Fori(0, HEADS // 2) as b:
                taken(act, "qkv", U.size("qkv"))
                for hh in range(2):
                    act.activation(ks[:, hh:hh + 1], kT[64 * hh:64 * hh + 64, bass.ds(b, 1)], ACT.Copy).then_inc(S["staged_by_scalar"], 1)
                for i in range(20):
                    act.wait_ge(S["rowmax_ready"], b * 20 + (i + 1))
                    if i >= 2:
                        act.wait_ge(S["pt_ready"], b * 60 + 3 * (i - 1))
                    for k, (lo, w) in enumerate(CHUNKS):
                        act.activation(Pr[:, i % 2, lo:lo + w], PS[0:P, (3 * i + k) % 4, 0:w], ACT.Exp, bias=smb[:, i % 2:i % 2 + 1],
                                       scale=-1.0, accum_out=sms[:, i % 2, k:k + 1]).then_inc(S["exp_done"], 1)
                    if i:
                        pt_out_scalar(act, b, i - 1)
                pt_out_scalar(act, b, 19)
            transposed("ot", OT)
            root(2)
            transposed("ht", XNT)
            act.wait_ge(S["gate_max"], 1)
            act.activation(ga[:], ga[:], ACT.Exp).then_inc(S["gate_exp"], 1)
            for i in range(1, ST, 2):
                ready(act, "rows", i)
                act.activation(rowsT[:, :, i * 128:(i + 1) * 128], bank("rows", i).rearrange("p (k n) -> p k n", k=KD), ACT.Copy).then_inc(TA, 1)
            act.wait_ge(S["table_ready"], 1)
            with act.Fori(0, EXPERTS // 2) as e2:
                for s in range(2):
                    n = act.value_load(table[0:1, bass.ds(e2 * 2 + s, 1)], min_val=0, max_val=MOST)
                    start = act.value_load(table[0:1, bass.ds(e2 * 2 + (s + EXPERTS), 1)], min_val=0, max_val=ST)
                    act.wait_ge(S["expert_done"], e2 * 2 + (s + 1))
                    with act.Fori(0, MOST) as m:
                        with act.If(m < n):
                            i = nc.s_assert_within(start + m, 0, ST - 1, skip_runtime_bounds_check_because="the experts' tiles add up to at most ST")
                            for f in range(KF):
                                act.wait_ge(S["hid_ready"], i * KF + (f + 1))
                                act.activation(hid[:, f], PS[:, f % 6, 0:128], ACT.Gelu_apprx_tanh, bias=b1c[:, s, f:f + 1]).then_inc(S["hid_done"], 1)
            root(3)
            transposed("xt2", XNT3)
            for i in range(NT):
                act.wait_ge(S["norm_ready"], 3 * NT + i + 1)
                act.activation(HH[:, i], XN3[:, i], ACT.Copy).then_inc(S["split_hi"], 1)
            act.wait_ge(S["gate_max"], 2)
            act.activation(ga[:, :, 0:SAGE], ga[:, :, 0:SAGE], ACT.Exp).then_inc(S["gate_exp"], 1)
            with act.Fori(0, SAGE) as e:
                for i in range(NT):
                    act.wait_ge(S["bias_added"], e * (2 * NT) + (i + 1))
                    act.activation(HH[:, i], bank("sage", i)[0:P, :], ACT.Relu).then_inc(S["relu_done"], 1)
                for c in range(5):
                    for i in range(2):
                        k = NT + 8 * c + 4 + i
                        ready(act, "sage", k, e)
                        act.activation(hTc[:, :, i, :], bank("sage", k)[:, 0:KD * 126].rearrange("p (k n) -> p k n", k=KD), ACT.Copy).then_inc(TA, 1)
                    for i in range(2):
                        k, tt = NT + 8 * c + 6 + i, 2 * c + i
                        act.wait_ge(S["bias_added"], e * (2 * NT) + (NT + tt + 1))
                        act.activation(bank("sage", k)[0:P, :], bank("sage", k)[0:P, :], ACT.Relu).then_inc(S["relu2_done"], 1)
            root(4)
            transposed("xt3", XNT4)
            act.wait_ge(S["g1_in"], 32)
            for n in range(12):
                f, c = n // 3, n % 3
                ready(act, "gh", n)
                w = CHUNKS[c][1]
                act.activation(bank("gh", n)[:, 0:w], bank("gh", n)[:, 0:w], ACT.Relu, bias=g1b[:, f:f + 1],
                               accum_out=ghs[:, f, c:c + 1]).then_inc(TA, 1)
            act.wait_ge(S["w_merged"], 1)
            for n in range(6):
                f, c = n // 3, n % 3
                lo, w = CHUNKS[c]
                ready(act, "up", n)
                act.activation(upT[:, f, lo:lo + w], bank("up", n)[:, 0:w], ACT.Relu, bias=m1b[:, f:f + 1]).then_inc(TA, 1)
            root(5)

        @block.vector
        def _(dve):
            TV, TA = S["taken_by_vector"], S["taken_by_scalar"]
            steps = [0]

            def did(ins):
                ins.then_inc(S["vector_step"], 1)
                steps[0] += 1
                return steps[0]

            def own(n, extra=0):
                dve.wait_ge(S["vector_step"], extra + n)

            def moments(i, src):
                own(did(dve.bn_stats(bnst[:, i], src)))
                dve.bn_aggr(mv[:, i], bnst[:, i]).then_inc(S["moments_ready"], 1)

            def inverse(k):
                dve.wait_ge(S["std_ready"], k + 1)
                own(did(dve.reciprocal(rstd[:], std[:])))

            def normalized(i, dst, src):
                return dve.tensor_scalar(dst, src, mv[:, i, 0:1], rstd[:, i:i + 1], ALU.subtract, ALU.mult)

            dve.wait_ge(S["edges_in"], 32)
            did(dve.tensor_copy(srcf[:], srci[:]))
            own(did(dve.tensor_copy(dstf[:], dsti[:])))
            own(did(dve.tensor_scalar(srcq[:], srcf[:], float(HALF), None, ALU.is_ge)))
            did(dve.tensor_scalar(srcw[:], srcq[:], FIELD - 1.0, 1.0, ALU.mult, ALU.add))
            own(did(dve.scalar_tensor_tensor(out=srcf[:], in0=srcq[:], scalar=-float(HALF), in1=srcf[:], op0=ALU.mult, op1=ALU.add)))
            dve.wait_ge(S["x_in"], 16)
            for i in range(NT):
                moments(i, x0[:, i])
            dve.wait_ge(S["iota_done"], 2)
            dve.wait_ge(S["adj_zero"], 1)
            dve.memset(ohs[:], 0.0).then_inc(S["onehot_slots"], SLOTS)

            def field(n, j, part):
                cols = slice(j * DCH, (j + 1) * DCH)
                if part == 0:
                    dve.wait_ge(S["counts_by_scalar"], n + 1)
                    dve.wait_ge(S["counts_by_vector"], n + 1)
                    dve.tensor_scalar(cnthi[:], cnt[:], 12, None, ALU.arith_shift_right)
                elif part == 1:
                    dve.tensor_scalar(cntlo[:], cnt[:], 4095, None, ALU.bitwise_and).then_inc(S["fields_read"], 1)
                elif part == 2:
                    dve.wait_ge(S["fields_read"], n + 1)
                    dve.tensor_tensor(AT[:, PACKED:NT, cols], AT[:, PACKED:NT, cols].bitcast(F32), cnthi[:], ALU.add)
                else:
                    dve.tensor_tensor(AT[:, 0:PACKED, cols], AT[:, 0:PACKED, cols].bitcast(F32), cntlo[:], ALU.add)

            def counts(n):
                dve.wait_ge(S["onehot_slots"], n * GROUP + SLOTS)
                for r in range(3, PACKED):
                    ins = dve.tensor_copy(cnt[:, r], PS[0:P, r, 0:DCH])
                ins.then_inc(S["counts_by_vector"], 1)

            def onehots(g, first):
                cols = bass.ds(g * GROUP, GROUP)
                if not first:
                    dve.wait_ge(S["onehots_ready"], g * (NDC * GROUP))
                for m, v in enumerate((srcf, srcw, dstf)):
                    ins = dve.tensor_copy(edge[:, m], v[:, cols])
                ins.then_inc(S["edges_staged"], 1)
                dve.wait_ge(S["edges_staged"], g + 1)
                for j in range(NDC):
                    n = g * NDC + j
                    for c in range(GROUP):
                        dve.wait_ge(S["onehot_slots"], g * (NDC * GROUP) + (j * GROUP + c + 1))
                        dve.tensor_scalar(ohs[:, c % SLOTS], iota[:, 0:HALF], edge[:, 0, c:c + 1], edge[:, 1, c:c + 1], ALU.is_equal, ALU.mult)
                        dve.tensor_scalar(ohd[:, c % SLOTS], iota[:, j * DCH:(j + 1) * DCH], edge[:, 2, c:c + 1], None, ALU.is_equal).then_inc(S["onehots_ready"], 1)
                        if first and j == 0:
                            continue
                        if c == SLOTS - 1:
                            counts(n)
                        if c in (8, 12, 16, 20):
                            field(n, (j - 1) % NDC, (c - 8) // 4)

            onehots(0, True)
            with dve.Fori(1, GROUPS) as g:
                onehots(g, False)
            counts(NDC * GROUPS)
            for part in range(4):
                field(NDC * GROUPS, NDC - 1, part)
            dve.wait_ge(S["ident_done"], 9)
            own(did(dve.tensor_copy(identr[:], ident[:])))
            for i in range(NT):
                blk = AT[:, i, i * P:(i + 1) * P]
                ins = dve.tensor_tensor(blk, blk.bitcast(F32), ident[0:P, 0:P], ALU.add)
            ins.then_inc(S["adj_ready"], 1)
            taken(dve, "degree", 4)
            did(dve.reciprocal(rowbc[:, 0:N], rowbc[:, 0:N]))
            own(did(dve.reciprocal(dcol[:], dcol[:])))
            inverse(0)
            own(did(dve.tensor_tensor(rstd[:], rstd[:], dcol[:], ALU.mult)))
            dve.wait_ge(S["rows_zero"], 16)
            dve.wait_ge(S["rows_stored"], 16)
            for i in range(NT):
                normalized(i, XS[:, i], x0[:, i]).then_inc(S["norm_ready"], 1)
            for i in range(NT):
                dve.wait_ge(S["split_hi"], i + 1)
                dve.tensor_tensor(XL[:, i], XS[:, i], XH[:, i].bitcast(F32), ALU.subtract).then_inc(S["split_lo"], 1)
            for k in range(12):
                c, f = k // KD, k % KD
                lo, w = CHUNKS[c]
                ready(dve, "agg1", k)
                dve.tensor_tensor(aggT[:, f, lo:lo + w], bank("agg1", k)[:, 0:w], rowbc[:, lo:lo + w], ALU.mult).then_inc(TV, 1)
            dve.wait_ge(S["l0b_in"], 64)
            dve.tensor_scalar(bq[:], bq[:], -0.125, None, ALU.mult).then_inc(S["const_ready"], 1)
            for c in range(5):
                for f in range(0, KF, 2):
                    k = 18 * c + f
                    ready(dve, "gcn", k)
                    dve.tensor_scalar(zT[:, f], bank("gcn", k)[:, 0:250], l0b1[:, f:f + 1], 0.0, ALU.add, ALU.max).then_inc(TV, 1)
                for i in range(2):
                    k, tt = 18 * c + KF + i, 2 * c + i
                    dve.wait_ge(S["h2_hi"], tt + 1)
                    dve.scalar_tensor_tensor(out=XL[:, tt], in0=bank("gcn", k)[0:P, :], scalar=dcol[:, tt:tt + 1],
                                             in1=XH[:, tt].bitcast(F32), op0=ALU.mult, op1=ALU.subtract).then_inc(TV, 1)
            dve.wait_ge(S["xback_in"], 32)

            def groupsum(i):
                dve.wait_ge(S["znorm_sq"], i + 1)
                dve.tensor_reduce(znr[:, i], zsq[:, i % 2].rearrange("p (g d) -> p g d", g=8), AX, ALU.add).then_inc(S["znorm_sum"], 1)

            for i in range(NT):
                ready(dve, "agg2", i)
                dve.scalar_tensor_tensor(out=ZF[:, i], in0=bank("agg2", i)[0:P, :], scalar=dcol[:, i:i + 1],
                                         in1=b2bc[:], op0=ALU.mult, op1=ALU.add).then_inc(TV, 1)
                if i:
                    groupsum(i - 1)
            groupsum(NT - 1)
            dve.wait_ge(S["znorm_root"], 1)
            own(did(dve.tensor_scalar(znr[:], znr[:], 1e-12, None, ALU.max)))
            own(did(dve.reciprocal(znr[:], znr[:])))
            for i in range(NT):
                z = ZF[:, i].rearrange("p (g d) -> p g d", g=8)
                scaled = did(dve.tensor_tensor(z, z, znr[:, i].rearrange("p (g a) -> p g a", a=1).to_broadcast([P, 8, 64]), ALU.mult))
            own(scaled)
            for i in range(NT):
                dve.tensor_tensor(X[:, i], X[:, i], ZF[:, i], ALU.add).then_inc(S["x_ready"], 1)
            for i in range(NT):
                dve.wait_ge(S["x_ready"], i + 1)
                moments(i, X[:, i])
            inverse(1)
            dve.wait_ge(S["spilled"], 16)
            for i in range(NT):
                normalized(i, XN[:, i], X[:, i]).then_inc(S["norm_ready"], 1)

            def transposed(name, dst):
                for i in range(0, NT, 2):
                    ready(dve, name, i)
                    dve.tensor_copy(dst[:, :, i * P:(i + 1) * P], bank(name, i)[:, 0:KD * P].rearrange("p (k n) -> p k n", k=KD)).then_inc(TV, 1)

            transposed("xt1", XNT)
            dve.wait_ge(S["const_ready"], 1)
            for n in range(0, 24, 2):
                f, c = (n % 12) // 3, n % 3
                lo, w = CHUNKS[c]
                ready(dve, "qkv", n)
                if n < 12:
                    dve.tensor_scalar(qT[:, f, lo:lo + w], bank("qkv", n)[:, 0:w], -0.125, bq[:, f:f + 1], ALU.mult, ALU.add).then_inc(TV, 1)
                else:
                    dve.tensor_scalar(kT[:, f, lo:lo + w], bank("qkv", n)[:, 0:w], bk[:, f:f + 1], None, ALU.add).then_inc(TV, 1)
            dve.wait_ge(S["attnb_in"], 64)
            for i in range(NT):
                ready(dve, "qkv", 24 + i)
                dve.tensor_tensor(V[:, i], bank("qkv", 24 + i)[0:P, :], bvbc[:], ALU.add).then_inc(TV, 1)

            per = 60
            with dve.Fori(0, HEADS // 2) as b:
                base = steps[0]
                taken(dve, "qkv", U.size("qkv"))
                for hh in range(2):
                    dve.tensor_copy(qs[:, hh:hh + 1], qT[64 * hh:64 * hh + 64, bass.ds(b, 1)]).then_inc(S["staged_by_vector"], 1)

                def rowmax(i):
                    for k, (lo, w) in enumerate(CHUNKS):
                        dve.wait_ge(S["scores_ready"], b * 60 + (3 * i + k + 1))
                        ins = dve.tensor_reduce(smm[:, i % 2, k:k + 1], PS[0:P, (3 * i + k) % 4, 0:w], AX, ALU.min)
                    own(did(ins), b * per)
                    dve.scalar_tensor_tensor(out=smb[:, i % 2:i % 2 + 1], in0=smm[:, i % 2, 0:1], scalar=smm[:, i % 2, 1:2],
                                             in1=smm[:, i % 2, 2:3], op0=ALU.min, op1=ALU.min).then_inc(S["rowmax_ready"], 1)

                def weighted(i):
                    hh, tt = i // NT, i % NT
                    dve.wait_ge(S["pv_ready"], b * 20 + (i + 1))
                    dve.tensor_scalar(O[:, tt, bass.ds(b * 128 + hh * 64, 64)], PS[0:P, 7, 64 * (i % 2):64 * (i % 2) + 64],
                                      smr[:, i % 2:i % 2 + 1], None, ALU.mult).then_inc(S["pv_taken"], 1)

                rowmax(0)
                for i in range(20):
                    if i < 19:
                        rowmax(i + 1)
                    for k in (0, 2):
                        nb = 4 if k == 0 else 2
                        dve.wait_ge(S["pt_ready"], b * 60 + (3 * i + k + 1))
                        if i >= 2:
                            dve.wait_ge(S["pv_ready"], b * 20 + (i - 1))
                        dve.tensor_copy(PT[:, i % 2, 4 * k:4 * k + nb, :], PS[0:P, 4 + (3 * i + k) % 3, 0:nb * P].rearrange("p (k n) -> p k n", n=P)).then_inc(S["pt_by_vector"], 1)
                    if i:
                        weighted(i - 1)
                    dve.wait_ge(S["exp_done"], b * 60 + 3 * i + 3)
                    own(did(dve.scalar_tensor_tensor(out=smr[:, 2 + i % 2:3 + i % 2], in0=sms[:, i % 2, 0:1], scalar=sms[:, i % 2, 1:2],
                                                     in1=sms[:, i % 2, 2:3], op0=ALU.add, op1=ALU.add)), b * per)
                    own(did(dve.reciprocal(smr[:, i % 2:i % 2 + 1], smr[:, 2 + i % 2:3 + i % 2])), b * per)
                weighted(19)
                assert steps[0] - base == per
            steps[0] = base + per * (HEADS // 2)
            transposed("ot", OT)
            dve.wait_ge(S["resid_ready"], NT)
            for i in range(NT):
                ready(dve, "wo", i)
                dve.tensor_tensor(XN[:, i], bank("wo", i)[0:P, :], XN[:, i], ALU.add).then_inc(TV, 1)
                dve.wait_ge(TV, U.taken("wo", i + 1)[0])
                moments(i, XN[:, i])
            inverse(2)
            for i in range(NT):
                n1 = did(normalized(i, XN[:, i], XN[:, i]))
            own(n1)
            for i in range(NT):
                n1 = did(dve.tensor_tensor(XN[:, i], XN[:, i], lngbc[:], ALU.mult))
            own(n1)
            for i in range(NT):
                dve.tensor_tensor(XN[:, i], XN[:, i], lnbbc[:], ALU.add).then_inc(S["norm_ready"], 1)
            transposed("ht", XNT)

            def over_experts(v, n):
                return v.rearrange("p (t a) -> p t a", a=1).to_broadcast([P, NT, n])

            def first_hot(hot, src, top, n):
                own(did(dve.tensor_reduce(top, src, AX, ALU.max)))
                own(did(dve.tensor_tensor(hot, src, over_experts(top, n), ALU.is_equal)))
                order = idx8[:, 0:n].rearrange("p (a e) -> p a e", a=1).to_broadcast([P, NT, n])
                own(did(dve.tensor_tensor(hot, hot, order, ALU.mult)))
                own(did(dve.tensor_reduce(gs[:, 3], hot, AX, ALU.max)))
                ins = dve.tensor_tensor(hot, hot, over_experts(gs[:, 3], n), ALU.is_equal)
                return ins

            def probabilities(name, bias, n, time):
                g = ga[:, :, 0:n]
                ready(dve, name, 0)
                dve.tensor_tensor(g, bank(name, 0)[0:P, 0:NT * n].rearrange("p (t e) -> p t e", e=n),
                                  bias[:].rearrange("p (a e) -> p a e", a=1).to_broadcast([P, NT, n]), ALU.add).then_inc(TV, 1)
                dve.wait_ge(TV, U.taken(name, 1)[0])
                own(did(dve.tensor_reduce(gs[:, 0], g, AX, ALU.max)))
                dve.tensor_tensor(g, g, over_experts(gs[:, 0], n), ALU.subtract).then_inc(S["gate_max"], 1)
                dve.wait_ge(S["gate_exp"], time)
                own(did(dve.tensor_reduce(gs[:, 1], g, AX, ALU.add)))
                own(did(dve.reciprocal(gs[:, 2], gs[:, 1])))
                own(did(dve.tensor_tensor(g, g, over_experts(gs[:, 2], n), ALU.mult)))

            dve.wait_ge(S["gate_in"], 32)
            probabilities("gate", gbias, EXPERTS, 1)
            first_hot(gb[:], ga[:], gs[:, 0], EXPERTS).then_inc(S["gates_ready"], 1)
            ready(dve, "gate", 2)
            own(did(dve.tensor_copy(inall[:], bank("gate", 2)[0:P, 0:NT * EXPERTS].rearrange("p (t e) -> p t e", e=EXPERTS))))
            own(did(dve.memset(before[:, 0], 0.0)))
            for i in range(1, NT):
                own(did(dve.tensor_tensor(before[:, i], before[:, i - 1], inall[:, i - 1], ALU.add)))
            own(did(dve.tensor_tensor(count[:], before[:, NT - 1], inall[:, NT - 1], ALU.add)))
            own(did(dve.tensor_scalar(counti[:], count[:], 127.0, None, ALU.add)))
            own(did(dve.tensor_scalar(table[:, 0:EXPERTS], counti[:], 7, None, ALU.arith_shift_right)))
            did(dve.memset(startf[:, 0:1], 0.0))
            own(did(dve.tensor_copy(tilesf[:], table[:, 0:EXPERTS])))
            for e in range(1, EXPERTS):
                own(did(dve.tensor_tensor(startf[:, e:e + 1], startf[:, e - 1:e], tilesf[:, e - 1:e], ALU.add)))
            did(dve.tensor_tensor(table[:, 2 * EXPERTS:2 * EXPERTS + 1], startf[:, EXPERTS - 1:EXPERTS], tilesf[:, EXPERTS - 1:EXPERTS], ALU.add))
            did(dve.tensor_scalar(start128[:], startf[:], 128.0, None, ALU.mult))
            dve.tensor_copy(table[:, EXPERTS:2 * EXPERTS], startf[:]).then_inc(S["table_ready"], 1)
            dve.wait_ge(S["table_ready"], 1)
            own(did(dve.tensor_tensor(before[:], before[:], start128[:].rearrange("p (a e) -> p a e", a=1).to_broadcast([P, NT, EXPERTS]), ALU.add)))
            dve.tensor_tensor(before[:], bank("gate", 1)[0:P, 0:NT * EXPERTS].rearrange("p (t e) -> p t e", e=EXPERTS), before[:], ALU.add).then_inc(TV, 1)
            dve.wait_ge(TV, U.taken("gate", 2)[0])
            dve.tensor_tensor(before[:], before[:], gb[:], ALU.mult).then_inc(TV, 1)
            dve.wait_ge(TV, U.taken("gate", 3)[0])
            own(did(dve.tensor_reduce(slotf[:], before[:], AX, ALU.add)))
            dve.tensor_copy(sloti[:], slotf[:]).then_inc(S["slots_ready"], 1)
            for s in range(2):
                dve.tensor_copy(b1c[:, s], b1e[:, s]).then_inc(S["expert_done"], 1)
            dve.tensor_copy(startf[:], tilesf[:]).then_inc(S["y_taken"], 1)
            for i in range(0, ST, 2):
                ready(dve, "rows", i)
                dve.tensor_copy(rowsT[:, :, i * 128:(i + 1) * 128], bank("rows", i).rearrange("p (k n) -> p k n", k=KD)).then_inc(TV, 1)
            with dve.Fori(0, EXPERTS // 2) as e2:
                for s in range(2):
                    n = dve.value_load(table[0:1, bass.ds(e2 * 2 + s, 1)], min_val=0, max_val=MOST)
                    start = dve.value_load(table[0:1, bass.ds(e2 * 2 + (s + EXPERTS), 1)], min_val=0, max_val=ST)
                    with dve.Fori(0, MOST) as m:
                        with dve.If(m < n):
                            i = nc.s_assert_within(start + m, 0, ST - 1, skip_runtime_bounds_check_because="the experts' tiles add up to at most ST")
                            dve.wait_ge(S["rows_stored"], i * 16 + 16)
                            dve.wait_ge(S[f"w2e_in{s}"], e2 * 32 + 32)
                            dve.wait_ge(S["y_ready"], i + 1)
                            dve.tensor_tensor(outrow[:], PS[:, 6, :], b2s[:, s], ALU.add).then_inc(S["y_taken"], 1)
                    dve.wait_ge(S[f"w1e_in{s}"], e2 * 16 + 16)
                    dve.wait_ge(S[f"w2e_in{s}"], e2 * 32 + 32)
                    dve.tensor_scalar(b1c[:, s:s + 1], b1e[:, bass.ds(e2 * 2 + (s + 2), 1)], 1.0, None, ALU.mult).then_inc(S["expert_done"], 1)
            last = dve.value_load(table[0:1, 2 * EXPERTS:2 * EXPERTS + 1], min_val=1, max_val=ST)
            dve.wait_ge(S["rows_stored"], last * 16 + 16)
            dve.tensor_scalar(topw[:], gs[:, 0], 1.0, None, ALU.mult).then_inc(S["rows_out_ready"], 1)
            dve.wait_ge(S["rows_out_ready"], 1)
            dve.wait_ge(S["rows_back"], 16 * NT)
            for i in range(NT):
                own(did(dve.scalar_tensor_tensor(out=X[:, i], in0=back[:, i], scalar=topw[:, i:i + 1], in1=X[:, i], op0=ALU.mult, op1=ALU.add)))
            taken(dve, "xt2", 0)
            for i in range(NT):
                moments(i, X[:, i])
            inverse(3)
            for i in range(NT):
                normalized(i, XN3[:, i], X[:, i]).then_inc(S["norm_ready"], 1)
            transposed("xt2", XNT3)
            for i in range(NT):
                dve.wait_ge(S["split_hi"], NT + i + 1)
                dve.tensor_tensor(HL[:, i], XN3[:, i], HH[:, i].bitcast(F32), ALU.subtract).then_inc(S["split_lo"], 1)
            dve.wait_ge(S["gate2_in"], 32)
            probabilities("gate2", gbias2, SAGE, 2)
            p, w4, hot = ga[:, :, 0:SAGE], wexp[:, :, 0:SAGE], gb[:, :, 0:SAGE]
            own(did(first_hot(w4, p, gs[:, 0], SAGE)))
            own(did(dve.scalar_tensor_tensor(out=gc[:], in0=w4, scalar=-2.0, in1=p, op0=ALU.mult, op1=ALU.add)))
            own(did(first_hot(hot, gc[:], gs[:, 1], SAGE)))
            own(did(dve.tensor_tensor(w4, w4, hot, ALU.add)))
            dve.tensor_tensor(w4, w4, p, ALU.mult).then_inc(S["gates_ready"], 1)
            dve.wait_ge(S["gates_ready"], 2)
            dve.wait_ge(S["unspilled"], 16)
            for i in range(NT):
                blk = AT[:, i, i * P:(i + 1) * P]
                ins = dve.tensor_tensor(blk, blk.bitcast(F32), ident[0:P, 0:P], ALU.subtract)
            ins.then_inc(S["adj_ready"], 1)
            for k in range(3):
                ready(dve, "degree2", k)
                r = rowbc3[:, k * DCH:(k + 1) * DCH]
                deg = bank("degree2", k)[:, 0:DCH]
                own(did(dve.tensor_scalar(r, deg, 1.0, None, ALU.max)))
                own(did(dve.reciprocal(r, r)))
                dve.scalar_tensor_tensor(out=r, in0=deg, scalar=1.0, in1=r, op0=ALU.min, op1=ALU.mult).then_inc(TV, 1)
            taken(dve, "agg3", 0)
            for k in range(12):
                c, f = k // KD, k % KD
                lo, w = CHUNKS[c]
                ready(dve, "agg3", k)
                dve.tensor_tensor(agg0[:, f, lo:lo + w], bank("agg3", k)[:, 0:w], rowbc3[:, lo:lo + w], ALU.mult).then_inc(TV, 1)
            with dve.Fori(0, SAGE) as e:
                dve.wait_ge(S["sl_in0"], e * 48 + 48)

                def low_part(i):
                    dve.wait_ge(S["relu_done"], e * NT + (i + 1))
                    dve.scalar_tensor_tensor(out=HL[:, i], in0=bank("sage", i)[0:P, :], scalar=0.0,
                                             in1=HH[:, i].bitcast(F32), op0=ALU.max, op1=ALU.subtract).then_inc(TV, 1)

                for i in range(NT):
                    ready(dve, "sage", i, e)
                    dve.tensor_tensor(bank("sage", i)[0:P, :], bank("sage", i)[0:P, :], blbc[:, 0], ALU.add).then_inc(S["bias_added"], 1)
                    if i:
                        low_part(i - 1)
                low_part(NT - 1)
                dve.wait_ge(S["sl_in1"], e * 48 + 48)
                for c in range(5):
                    for f in range(KD):
                        k = NT + 8 * c + f
                        ready(dve, "sage", k, e)
                        dve.tensor_tensor(aggc[:, f], bank("sage", k)[:, 0:250], rowbc3[:, c * 250:(c + 1) * 250], ALU.mult).then_inc(TV, 1)
                    for i in range(2):
                        k = NT + 8 * c + 6 + i
                        ready(dve, "sage", k, e)
                        dve.tensor_tensor(bank("sage", k)[0:P, :], bank("sage", k)[0:P, :], blbc[:, 1], ALU.add).then_inc(S["bias_added"], 1)
                    for i in range(2):
                        k, tt = NT + 8 * c + 6 + i, 2 * c + i
                        dve.wait_ge(S["relu2_done"], e * NT + (tt + 1))
                        dve.wait_ge(TV, U.taken("sage", 0, e)[0])
                        dve.scalar_tensor_tensor(out=X[:, tt], in0=bank("sage", k)[0:P, :], scalar=wexp[:, tt, bass.ds(e, 1)],
                                                 in1=X[:, tt], op0=ALU.mult, op1=ALU.add).then_inc(TV, 1)
            taken(dve, "xt3", 0)
            for i in range(NT):
                moments(i, X[:, i])
            inverse(4)
            for i in range(NT):
                normalized(i, XN4[:, i], X[:, i]).then_inc(S["norm_ready"], 1)
            transposed("xt3", XNT4)
            own(did(dve.memset(c03[:], 0.03)))
            taken(dve, "merge", 0)
            own(did(dve.tensor_reduce(ghm[:], ghs[:], AX, ALU.add)))
            own(did(dve.tensor_scalar(ghm[:], ghm[:], 1.0 / N, None, ALU.mult)))
            dve.tensor_copy(ghb[:], ghm[:].rearrange("p (k a) -> p k a", a=1).to_broadcast([128, KD, 128])).then_inc(S["ghm_ready"], 1)
            dve.wait_ge(S["merge_in"], 13 * 16)
            ready(dve, "merge", 0)
            dve.tensor_tensor(gbc[:], bank("merge", 0)[:, 0:EXPERTS], g2bbc[:], ALU.add).then_inc(TV, 1)
            ready(dve, "merge", 1)
            dve.tensor_scalar(gT[:], bank("merge", 1)[0:EXPERTS, 0:128], g2bcol[:], None, ALU.add).then_inc(TV, 1)
            ready(dve, "merge", 2)
            dve.tensor_tensor(m2bc[:], m2bc[:], bank("merge", 2)[0:P, :], ALU.add).then_inc(TV, 1)
            for k, v in ((3, mgbc), (4, mbbc)):
                ready(dve, "merge", k)
                dve.scalar_tensor_tensor(out=v[:], in0=v[:], scalar=1.0 - 0.03 * EXPERTS, in1=bank("merge", k)[0:P, :],
                                         op0=ALU.mult, op1=ALU.add).then_inc(TV, 1)
            dve.wait_ge(TV, U.taken("merge", 5)[0])
            own(did(dve.tensor_tensor(tvt[:], tvb1[:], gbc[:].rearrange("p (a e) -> p a e", a=1).to_broadcast([128, KM, EXPERTS]), ALU.mult)))
            own(did(dve.tensor_reduce(tvr[:], tvt[:], AX, ALU.add)))
            own(did(dve.tensor_tensor(m1b[:], m1b[:], tvr[:], ALU.add)))
            for n in range(2 * EXPERTS):
                e, m = n // 2, (W1m, W2m)[n % 2]
                dve.wait_ge(S[f"tv_in{n % 4}"], 16 * (n // 4 + 1))
                if n >= 2:
                    dve.wait_ge(S["tv_used"], n - 1)
                flat = m[:].rearrange("p k n -> p (k n)")
                dve.scalar_tensor_tensor(out=flat, in0=tv[:, n % 4], scalar=gbc[:, e:e + 1], in1=flat, op0=ALU.mult, op1=ALU.add).then_inc(S["tv_used"], 1)
            dve.wait_ge(S["tv_used"], 2 * EXPERTS)
            for i in range(NT):
                ins = dve.tensor_tensor(XN4[:, i], XN4[:, i], m2bc[:], ALU.add)
            ins.then_inc(S["w_merged"], 1)
            for i in range(NT):
                ready(dve, "down", i)
                dve.tensor_tensor(XN4[:, i], bank("down", i)[0:P, :], XN4[:, i], ALU.add).then_inc(TV, 1)
                dve.wait_ge(TV, U.taken("down", i + 1)[0])
                moments(i, XN4[:, i])
            inverse(5)
            for i in range(NT):
                n1 = did(normalized(i, XN4[:, i], XN4[:, i]))
            own(n1)
            for i in range(NT):
                n1 = did(dve.tensor_tensor(XN4[:, i], XN4[:, i], mgbc[:], ALU.mult))
            own(n1)
            for i in range(NT):
                n1 = did(dve.tensor_tensor(XN4[:, i], XN4[:, i], mbbc[:], ALU.add))
            own(n1)
            for i in range(NT):
                dve.tensor_tensor(XN4[:, i], XN4[:, i], X[:, i], ALU.add).then_inc(S["tail_ready"], 1)

        @block.tensor
        def _(pe):
            UR = S["unit_ready"]

            def free(name, k, i=0):
                if k == 0:
                    taken(pe, name, 0, i)
                elif k >= 8:
                    taken(pe, name, k - 7, i)

            def product(dst, lhs, rhs):
                for n, (a, b) in enumerate(zip(lhs, rhs)):
                    ins = pe.matmul(dst, a, b, start=(n == 0), stop=(n == len(lhs) - 1))
                return ins

            def transposes(name, src, wait, base):
                for i in range(NT):
                    pe.wait_ge(S[wait], base + i + 1)
                    free(name, i)
                    for k in range(KD):
                        ins = pe.transpose(bank(name, i)[:, k * P:(k + 1) * P], src[:, i, k * 128:(k + 1) * 128], ident[0:P, 0:P])
                    ins.then_inc(UR, 1)

            def blocks(m, lo, w):
                return [m[:, k, lo:lo + w] for k in range(m.shape[1])]

            with pe.Fori(0, GROUPS) as g:
                for j in range(NDC):
                    pe.wait_ge(S["counts_by_scalar"], g * NDC + (j + 1))
                    for c in range(GROUP):
                        pe.wait_ge(S["onehots_ready"], g * (NDC * GROUP) + (j * GROUP + c + 1))
                        for r in range(PACKED):
                            if c == 0 and r == 3:
                                pe.wait_ge(S["counts_by_vector"], g * NDC + (j + 1))
                            ins = pe.matmul(PS[0:P, r, 0:DCH], ohs[:, c % SLOTS, r * P:(r + 1) * P], ohd[:, c % SLOTS],
                                            start=(c == 0), stop=(c == GROUP - 1))
                        ins.then_inc(S["onehot_slots"], 1)
            pe.wait_ge(S["adj_ready"], 1)
            for k in range(3):
                product(bank("degree", k)[:, 0:DCH], [onesr[0:P, :]] * NT, [AT[:, s, k * DCH:(k + 1) * DCH] for s in range(NT)]).then_inc(UR, 1)
            for i in range(NT):
                ins = product(bank("degree", 3)[0:P, 2 * i:2 * i + 2], [AT[:, s, i * P:(i + 1) * P] for s in range(NT)], [onesr[0:P, 0:2]] * NT)
            ins.then_inc(UR, 1)

            def aggregate(name, k0, hi, lo_, c, cols, i=0):
                lo, w = cols
                for f in range(KD):
                    free(name, k0 + f, i)
                    lhs = [h[:, s, f * 128:(f + 1) * 128] for h in (hi, lo_) for s in range(NT)]
                    rhs = [AT[:, s, lo:lo + w] for _ in range(2) for s in range(NT)]
                    product(bank(name, k0 + f)[:, 0:w], lhs, rhs).then_inc(UR, 1)

            pe.wait_ge(S["split_lo"], NT)
            for c in range(3):
                aggregate("agg1", KD * c, XH, XL, c, CHUNKS[c])
            pe.wait_ge(S["w1_in"], 16)
            taken(pe, "agg1", 12)
            for c in range(5):
                for f in range(KF):
                    k = 18 * c + f
                    free("gcn", k)
                    product(bank("gcn", k)[:, 0:250], blocks(W1, f * 128, 128), blocks(aggT, 250 * c, 250)).then_inc(UR, 1)
                pe.wait_ge(S["w2_in"], 16)
                taken(pe, "gcn", 18 * c + KF)
                for i in range(2):
                    k = 18 * c + KF + i
                    product(bank("gcn", k)[0:P, :], blocks(zT, i * P, P), blocks(W2, 0, D)).then_inc(UR, 1)
            taken(pe, "gcn", U.size("gcn"))
            for i in range(NT):
                free("agg2", i)
                product(bank("agg2", i)[0:P, :], [AT[:, s, i * P:(i + 1) * P] for _ in range(2) for s in range(NT)],
                        [h[:, s, :] for h in (XH, XL) for s in range(NT)]).then_inc(UR, 1)
            transposes("xt1", XN, "norm_ready", NT)
            taken(pe, "xt1", NT)
            pe.wait_ge(S["qkvw_in"], 48)
            for n in range(24):
                f, c = (n % 12) // 3, n % 3
                free("qkv", n)
                product(bank("qkv", n)[:, 0:CHUNKS[c][1]], blocks((Wq, Wk)[n // 12], f * 128, 128), blocks(XNT, *CHUNKS[c])).then_inc(UR, 1)
            for i in range(NT):
                free("qkv", 24 + i)
                product(bank("qkv", 24 + i)[0:P, :], blocks(XNT, i * P, P), blocks(Wv, 0, D)).then_inc(UR, 1)
            taken(pe, "qkv", U.size("qkv"))
            with pe.Fori(0, HEADS // 2) as b:
                def scores(i):
                    hh, tt = i // NT, i % NT
                    pe.wait_ge(S["staged_by_vector"], b * 2 + (hh + 1))
                    pe.wait_ge(S["staged_by_scalar"], b * 2 + (hh + 1))
                    for k, (lo, w) in enumerate(CHUNKS):
                        n = 3 * i + k
                        if n >= 4:
                            pe.wait_ge(S["exp_done"], b * 60 + (n - 3))
                        pe.matmul(PS[0:P, n % 4, 0:w], qs[:, hh, tt * P:(tt + 1) * P], ks[:, hh, lo:lo + w], start=True, stop=True).then_inc(S["scores_ready"], 1)

                def transpose_p(i):
                    for k, (lo, w) in enumerate(CHUNKS):
                        pe.wait_ge(S["exp_done"], b * 60 + (3 * i + k + 1))
                        if i:
                            if k == 1:
                                pe.wait_ge(S["pt_by_scalar"], b * 20 + i)
                            else:
                                pe.wait_ge(S["pt_by_vector"], b * 40 + (2 * i - (1 if k == 0 else 0)))
                        for m in range(w // P):
                            ins = pe.transpose(PS[0:P, 4 + (3 * i + k) % 3, m * P:(m + 1) * P], Pr[:, i % 2, lo + m * P:lo + (m + 1) * P], ident[0:P, 0:P])
                        ins.then_inc(S["pt_ready"], 1)

                def values(i):
                    hh = i // NT
                    pe.wait_ge(S["pt_by_vector"], b * 40 + 2 * (i + 1))
                    pe.wait_ge(S["pt_by_scalar"], b * 20 + (i + 1))
                    if i:
                        pe.wait_ge(S["pv_taken"], b * 20 + i)
                    for s in range(NT):
                        ins = pe.matmul(PS[0:P, 7, 64 * (i % 2):64 * (i % 2) + 64], PT[:, i % 2, s, :], V[:, s, bass.ds(b * 128 + hh * 64, 64)],
                                        start=(s == 0), stop=(s == NT - 1))
                    ins.then_inc(S["pv_ready"], 1)

                scores(0)
                for i in range(20):
                    if i < 19:
                        scores(i + 1)
                    transpose_p(i)
                    if i:
                        values(i - 1)
                values(19)
            pe.wait_ge(S["pv_taken"], HEADS * NT)
            pe.wait_ge(S["pt_by_scalar"], HEADS * NT)
            transposes("ot", O, "pv_taken", HEADS * NT - NT)
            taken(pe, "ot", NT)
            pe.wait_ge(S["wo_in"], 16)
            for i in range(NT):
                free("wo", i)
                product(bank("wo", i)[0:P, :], blocks(OT, i * P, P), blocks(Wq, 0, D)).then_inc(UR, 1)
            transposes("ht", XN, "norm_ready", 2 * NT)
            taken(pe, "gate", 0)
            pe.wait_ge(S["gate_in"], 32)
            for i in range(NT):
                ins = product(bank("gate", 0)[0:P, EXPERTS * i:EXPERTS * (i + 1)], blocks(XNT, i * P, P), blocks(gW, 0, EXPERTS))
            ins.then_inc(UR, 1)
            pe.wait_ge(S["gates_ready"], 1)
            for m, k in ((tri, 1), (ones, 2)):
                pe.matmul(bank("gate", k)[0:P, 0:NT * EXPERTS], m[0:P, 0:P], gb[:].rearrange("p t e -> p (t e)"), start=True, stop=True).then_inc(UR, 1)
            taken(pe, "gate", 3)
            pe.wait_ge(S["rows_loaded"], 16)
            for i in range(ST):
                free("rows", i)
                for k in range(KD):
                    ins = pe.transpose(bank("rows", i)[:, k * 128:(k + 1) * 128], rows_in[:, i, k * 128:(k + 1) * 128], ident[:])
                ins.then_inc(UR, 1)
            taken(pe, "rows", ST)
            pe.wait_ge(S["table_ready"], 1)
            with pe.Fori(0, EXPERTS // 2) as e2:
                for s in range(2):
                    n = pe.value_load(table[0:1, bass.ds(e2 * 2 + s, 1)], min_val=0, max_val=MOST)
                    start = pe.value_load(table[0:1, bass.ds(e2 * 2 + (s + EXPERTS), 1)], min_val=0, max_val=ST)
                    with pe.Fori(0, MOST) as m:
                        with pe.If(m < n):
                            i = nc.s_assert_within(start + m, 0, ST - 1, skip_runtime_bounds_check_because="the experts' tiles add up to at most ST")
                            pe.wait_ge(S[f"w1e_in{s}"], e2 * 16 + 16)
                            for f in range(KF):
                                if f >= 6:
                                    pe.wait_ge(S["hid_done"], i * KF + (f - 5))
                                product(PS[:, f % 6, 0:128], [W1e[:, s, k, f * 128:(f + 1) * 128] for k in range(KD)],
                                        [rowsT[:, k, bass.ds(i * 128, 128)] for k in range(KD)]).then_inc(S["hid_ready"], 1)
                            pe.wait_ge(S["y_taken"], i + 1)
                            pe.wait_ge(S[f"w2e_in{s}"], e2 * 32 + 32)
                            for k in range(KF):
                                pe.wait_ge(S["hid_done"], i * KF + (k + 1))
                                ins = pe.matmul(PS[:, 6, :], hid[:, k], W2e[:, s, k, :], start=(k == 0), stop=(k == KF - 1))
                            ins.then_inc(S["y_ready"], 1)
            transposes("xt2", XN3, "norm_ready", 3 * NT)
            taken(pe, "xt2", NT)
            pe.wait_ge(S["gate2_in"], 32)
            for i in range(NT):
                ins = product(bank("gate2", 0)[0:P, SAGE * i:SAGE * (i + 1)], blocks(XNT3, i * P, P), blocks(gW2, 0, SAGE))
            ins.then_inc(UR, 1)
            taken(pe, "degree2", 0)
            pe.wait_ge(S["adj_ready"], 2)
            for k in range(3):
                product(bank("degree2", k)[:, 0:DCH], [onesr[0:P, :]] * NT, [AT[:, s, k * DCH:(k + 1) * DCH] for s in range(NT)]).then_inc(UR, 1)
            pe.wait_ge(S["split_lo"], 2 * NT)
            for c in range(3):
                aggregate("agg3", KD * c, HH, HL, c, CHUNKS[c])
            with pe.Fori(0, SAGE) as e:
                taken(pe, "sage", 0, e)
                pe.wait_ge(S["sl_in0"], e * 48 + 48)
                for i in range(NT):
                    free("sage", i, e)
                    product(bank("sage", i)[0:P, :], blocks(agg0, i * P, P) + blocks(XNT3, i * P, P),
                            [Wsl[:, 0, k, :] for k in range(KD)] + [Wsr[:, 0, k, :] for k in range(KD)]).then_inc(UR, 1)
                taken(pe, "sage", NT, e)
                for c in range(5):
                    k0 = NT + 8 * c
                    aggregate("sage", k0, HH, HL, c, (250 * c, 250), e)
                    for i in range(2):
                        tt = 2 * c + i
                        free("sage", k0 + 4 + i, e)
                        for k in range(KD):
                            blk = slice(k * 128, (k + 1) * 128)
                            ins = product(bank("sage", k0 + 4 + i)[:, k * 126:(k + 1) * 126], [HH[:, tt, blk], HL[:, tt, blk]], [identr[0:P, 0:126]] * 2)
                        ins.then_inc(UR, 1)
                    if c == 0:
                        pe.wait_ge(S["sl_in1"], e * 48 + 48)
                    taken(pe, "sage", k0 + 6, e)
                    for i in range(2):
                        free("sage", k0 + 6 + i, e)
                        product(bank("sage", k0 + 6 + i)[0:P, :], blocks(aggc, i * P, P) + [hTc[:, k, i, 0:P] for k in range(KD)],
                                [Wsl[:, 1, k, :] for k in range(KD)] + [Wsr[:, 1, k, :] for k in range(KD)]).then_inc(UR, 1)
            transposes("xt3", XN4, "norm_ready", 4 * NT)
            taken(pe, "xt3", NT)
            pe.wait_ge(S["g1_in"], 32)
            for n in range(12):
                f, c = n // 3, n % 3
                free("gh", n)
                product(bank("gh", n)[:, 0:CHUNKS[c][1]], blocks(g1T, f * 128, 128), blocks(XNT4, *CHUNKS[c])).then_inc(UR, 1)
            taken(pe, "merge", 0)
            pe.wait_ge(S["merge_in"], 13 * 16)
            pe.wait_ge(S["ghm_ready"], 1)
            product(bank("merge", 0)[:, 0:EXPERTS], blocks(ghb, 0, 128), blocks(g2T, 0, EXPERTS)).then_inc(UR, 1)
            product(bank("merge", 1)[0:EXPERTS, 0:128], blocks(g2T, 0, EXPERTS), blocks(ghb, 0, 128)).then_inc(UR, 1)
            taken(pe, "merge", 2)
            pe.matmul(bank("merge", 2)[0:P, :], gT[:, 0:P], tvb2[:], start=True, stop=True).then_inc(UR, 1)
            for k, v in ((3, tvg), (4, tvb)):
                pe.matmul(bank("merge", k)[0:P, :], c03[:], v[:], start=True, stop=True).then_inc(UR, 1)
            taken(pe, "merge", 5)
            pe.wait_ge(S["w_merged"], 1)
            for n in range(6):
                f, c = n // 3, n % 3
                product(bank("up", n)[:, 0:CHUNKS[c][1]], blocks(W1m, f * 128, 128), blocks(XNT4, *CHUNKS[c])).then_inc(UR, 1)
            taken(pe, "up", 6)
            for i in range(NT):
                free("down", i)
                product(bank("down", i)[0:P, :], blocks(upT, i * P, P), blocks(W2m, 0, D)).then_inc(UR, 1)


_IN = ["x", "src", "dst", "L0_gnn_W1", "L0_gnn_b1", "L0_gnn_W2", "L0_gnn_b2", "L0_ffn_ln1_g", "L0_ffn_ln1_b",
       "L0_ffn_Wq", "L0_ffn_bq", "L0_ffn_Wk", "L0_ffn_bk", "L0_ffn_Wv", "L0_ffn_bv", "L0_ffn_Wo", "L0_ffn_bo",
       "L0_ffn_gate_W", "L0_ffn_gate_b", "L0_ffn_W1", "L0_ffn_b1", "L0_ffn_W2", "L0_ffn_b2", "L1_gnn_gate_W",
       "L1_gnn_gate_b", "L1_gnn_Wl", "L1_gnn_bl", "L1_gnn_Wr", "L1_ffn_gfc1_w", "L1_ffn_gfc1_b", "L1_ffn_gfc2_w",
       "L1_ffn_gfc2_b", "L1_ffn_W1", "L1_ffn_b1", "L1_ffn_W2", "L1_ffn_b2", "L1_ffn_ln_g", "L1_ffn_ln_b",
       "L1_ffn_tv_W1", "L1_ffn_tv_b1", "L1_ffn_tv_W2", "L1_ffn_tv_b2", "L1_ffn_tv_ln_g", "L1_ffn_tv_ln_b"]


def _laid_out(inputs):
    import numpy as np

    a = {k: np.asarray(inputs[k]) for k in _IN}
    for k in ("L0_gnn_b1", "L0_ffn_bq", "L0_ffn_bk", "L1_ffn_gfc1_b", "L1_ffn_b1"):
        a[k] = a[k].reshape(-1, 128).T
    a["L0_ffn_b1"] = a["L0_ffn_b1"].reshape(EXPERTS, KF, 128).transpose(2, 0, 1)
    a["L1_ffn_tv_b1"] = a["L1_ffn_tv_b1"].reshape(EXPERTS, KM, 128).transpose(2, 1, 0)
    for k in ("L1_ffn_gfc1_w", "L1_ffn_gfc2_w", "L1_ffn_W1", "L1_ffn_W2"):
        a[k] = a[k].T
    for k in ("L1_ffn_tv_W1", "L1_ffn_tv_W2"):
        a[k] = a[k].transpose(0, 2, 1)
    return {k: np.ascontiguousarray(v) for k, v in a.items()}


def build(nc, arrays):
    t = {k: nc.dram_tensor(f"in_{k}", v.shape, mybir.dt.from_np(v.dtype), kind="ExternalInput").ap() for k, v in arrays.items()}
    out = nc.dram_tensor("out_0", (N, D), F32, kind="ExternalOutput").ap()
    rows_x = nc.dram_tensor("rows_by_expert", (SLOT_ROWS, D), F32, kind="Internal").ap()
    rows_y = nc.dram_tensor("rows_out_by_expert", (SLOT_ROWS, D), F32, kind="Internal").ap()
    spill = nc.dram_tensor("adjacency_spill", (P, NT, NPAD), F32, kind="Internal").ap()
    program(nc, t, out, spill, rows_x, rows_y)


def kernel(**inputs):
    import concourse.bacc as _bacc
    from concourse.bass_utils import run_bass_kernel_spmd as _run

    arrays = _laid_out(inputs)
    nc = _bacc.Bacc("TRN2", target_bir_lowering=False, num_devices=1)
    build(nc, arrays)
    r = _run(nc, [{f"in_{k}": v for k, v in arrays.items()}], core_ids=[0])
    return r.results[0]["out_0"]
```

```python
from contextlib import ExitStack

import concourse.bass as bass
from concourse import mybir

F32 = mybir.dt.float32
F32R = mybir.dt.float32r
F16 = mybir.dt.float16
I32 = mybir.dt.int32
U32 = mybir.dt.uint32
ALU = mybir.AluOpType
ACT = mybir.ActivationFunctionType
AX = mybir.AxisListType.X

N = 1250
NE = 20000
P = 125
NT = N // P
D = 512
KD = D // 128
FF = 2048
KF = FF // 128
HEADS, HD = 8, 64
EXPERTS = 8
SAGE = 4
MF = 256
KM = MF // 128
EPS = 1e-5
CHUNKS = [(0, 500), (500, 500), (1000, 250)]
TILES_OF = [range(0, 4), range(4, 8), range(8, 10)]
HALF = N // 2
FIELD = 4096.0
GROUP = 8
GROUPS = NE // P // GROUP
EROWS = 80
PACKED = HALF // P
DCH = 418
NDC = 3
ST = (N - EXPERTS) // 128 + EXPERTS
SLOT_ROWS = ST * 128
MOST = -(-N // 128)
NPAD = DCH * NDC


class UnitPlan:

    def __init__(self, phases):
        self.at, units, v, a = {}, 0, 0, 0
        for name, owners, times in phases:
            self.at[name] = (units, v, a, owners)
            units += len(owners) * times
            v += owners.count("V") * times
            a += owners.count("A") * times

    def ready(self, name, k, i=0):
        units, _, _, owners = self.at[name]
        return i * len(owners) + (units + k + 1)

    def taken(self, name, k, i=0):
        _, v, a, owners = self.at[name]
        return (i * owners.count("V") + (v + owners[:k].count("V")),
                i * owners.count("A") + (a + owners[:k].count("A")))

    def size(self, name):
        return len(self.at[name][3])


def program(nc, t, out, spill, rows_x, rows_y):
    U = UnitPlan([
        ("edges", "VVV", 1),
        ("degree", "AAAA", 1),
        ("agg1", "V" * 12, 1),
        ("gcn", ("VA" * 8 + "VV") * 5, 1),
        ("agg2", "V" * NT, 1),
        ("xt1", "V" * NT, 1),
        ("qkv", "VA" * 12 + "V" * NT, 1),
        ("ot", "VA" * 5, 1),
        ("wo", "V" * NT, 1),
        ("ht", "VA" * 5, 1),
        ("gate", "VVV", 1),
        ("rows", "VA" * (ST // 2) + "V" * (ST % 2), 1),
        ("xt2", "VA" * 5, 1),
        ("gate2", "V", 1),
        ("degree2", "VVV", 1),
        ("agg3", "V" * 12, 1),
        ("sage", "V" * NT + "VVVVAAVV" * 5, SAGE),
        ("xt3", "VA" * 5, 1),
        ("gh", "A" * 12, 1),
        ("merge", "VVVVV", 1),
        ("up", "A" * 6, 1),
        ("down", "V" * NT, 1),
    ])

    ctx = ExitStack()
    with ctx:
        def sem(name):
            return ctx.enter_context(nc.semaphore(name))

        PS = ctx.enter_context(nc.psum_tensor("PS", [128, 8, 512], F32))

        BASE = 16512
        TOP = 229344

        def at(name, shape, dt, off):
            size = 2 if dt == F16 else 4
            for s in shape[1:]:
                size *= s
            assert BASE + off + size <= TOP, (name, BASE + off + size - TOP)
            return nc.alloc_sbuf_tensor_at(name, shape, dt, offset=BASE + off), off + (size + 31) // 32 * 32

        o = 0
        ident, o = at("ident", [128, 128], F32, o)
        identr, o = at("identr", [128, 128], F32R, o)
        onesr, o = at("onesr", [128, 128], F32R, o)
        eps, o = at("eps", [128, 1], F32, o)
        bnst, o = at("bnst", [P, NT, 6], F32, o)
        mv, o = at("mv", [P, NT, 2], F32, o)
        std, o = at("std", [P, NT], F32, o)
        rstd, o = at("rstd", [P, NT], F32, o)
        dcol, o = at("dcol", [P, NT], F32, o)
        l0b1, o = at("l0b1", [128, KF], F32, o)
        bq, o = at("bq", [128, KD], F32, o)
        bk, o = at("bk", [128, KD], F32, o)
        b1e, o = at("b1e", [128, EXPERTS + 2, KF], F32, o)
        b1c, o = at("b1c", [128, 2, KF], F32, o)
        tri, o = at("tri", [128, 128], F32, o)
        ones, o = at("ones", [128, 128], F32, o)
        before, o = at("before", [P, NT, EXPERTS], F32, o)
        inall, o = at("inall", [P, NT, EXPERTS], F32, o)
        count, o = at("count", [P, EXPERTS], F32, o)
        counti, o = at("counti", [P, EXPERTS], I32, o)
        tilesf, o = at("tilesf", [P, EXPERTS], F32, o)
        startf, o = at("startf", [P, EXPERTS], F32, o)
        start128, o = at("start128", [P, EXPERTS], F32, o)
        table, o = at("table", [P, 3 * EXPERTS], I32, o)
        slotf, o = at("slotf", [P, NT], F32, o)
        sloti, o = at("sloti", [P, NT], U32, o)
        topw, o = at("topw", [P, NT], F32, o)
        gbc, o = at("gbc", [128, EXPERTS], F32, o)
        ga, o = at("ga", [P, NT, EXPERTS], F32, o)
        gc, o = at("gc", [P, NT, SAGE], F32, o)
        gb, o = at("gb", [P, NT, EXPERTS], F32, o)
        wexp, o = at("wexp", [P, NT, EXPERTS], F32, o)
        gs, o = at("gs", [P, 4, NT], F32, o)
        idx8, o = at("idx8", [P, EXPERTS], F32, o)
        assert o <= 7680, o
        X, o = at("X", [P, NT, D], F32, 7680)
        A0 = o
        AT, o = at("AT", [P, NT, NPAD], F32R, A0)
        f0 = o
        aggT, _ = at("aggT", [128, KD, N], F32, 7680)
        zrow, _ = at("zrow", [128, D], F32, 7680)
        XS, _ = at("XS", [P, NT, D], F32, 7680)
        rowbc, o = at("rowbc", [128, NPAD], F32, f0)
        XH, oh = at("XH", [P, NT, D], F32R, o)
        XL, o2 = at("XL", [P, NT, D], F32R, oh)
        e0 = o
        edgei, e0 = at("edgei", [EROWS, 2, 2 * P], I32, e0)
        edgef, e0 = at("edgef", [EROWS, 2, 2 * P], F32, e0)
        srcf, e0 = at("srcf", [P, NE // P], F32, e0)
        dstf, e0 = at("dstf", [P, NE // P], F32, e0)
        srcw, e0 = at("srcw", [P, NE // P], F32, e0)
        srcq, e0 = at("srcq", [P, NE // P], F32, e0)
        above, e0 = at("above", [P, NT - 1, NE // P], F32, e0)
        aboves, e0 = at("aboves", [P, NT - 1, GROUPS], F32, e0)
        within, e0 = at("within", [P, 2, NT - 1, GROUPS], F32, e0)
        spanf, e0 = at("spanf", [P, 2, GROUPS], F32, e0)
        span, e0 = at("span", [P, 2 * GROUPS], I32, e0)
        edge, e0 = at("edge", [P, 3, GROUP], F32, e0)
        iota, e0 = at("iota", [P, NPAD], F16, e0)
        iotaj, e0 = at("iotaj", [P, P], F16, e0)
        ohs, e0 = at("ohs", [P, GROUP, HALF], F16, e0)
        ohd, e0 = at("ohd", [P, GROUP, P], F16, e0)
        cnt, e0 = at("cnt", [P, 2, PACKED, P], F32, e0)
        assert e0 <= o2, (e0, o2)
        W1, o3 = at("W1", [128, KD, FF], F32, o2)
        ZF, _ = at("ZF", [P, NT, D], F32, o2)
        b2bc, _ = at("b2bc", [P, D], F32, o2 + 20480)
        W2, o4 = at("W2", [128, KF, D], F32, o3)
        x0, _ = at("x0", [P, NT, D], F32, o3)
        cnthi, _ = at("cnthi", [P, 2, PACKED, P], I32, o2)
        cntlo, _ = at("cntlo", [P, 2, PACKED, P], F32, o2 + 8384)
        cnthf, _ = at("cnthf", [P, 2, PACKED, P], F32, o2 + 16768)
        zT, o5 = at("zT", [128, KF, 250], F32, o4)
        zsq, _ = at("zsq", [P, 2, D], F32, o4)
        znr, _ = at("znr", [P, NT, 8], F32, o4 + 4096)
        XNT, o = at("XNT", [128, KD, N], F32, A0)
        O, o = at("O", [P, NT, D], F32, A0)
        XN, o = at("XN", [P, NT, D], F32, o)
        qT, oq = at("qT", [128, KD, N], F32, o)
        OT, _ = at("OT", [128, KD, N], F32, o)
        kT, o = at("kT", [128, KD, N], F32, oq)
        V, o = at("V", [P, NT, D], F32, o)
        Wq, o = at("Wq", [128, KD, D], F32, o)
        o += 2 * 8192
        XNTh, oh = at("XNTh", [128, KD, N], F32R, o)
        XNTl, _ = at("XNTl", [128, KD, N], F32R, A0)
        Wh, oh = at("Wh", [128, 3, KD, D], F32R, oh)
        Wl, _ = at("Wl", [128, 3, KD, D], F32R, o - 3 * 8192)
        Wf, _ = at("Wf", [128, 3, KD, D], F32, o - 3 * 8192)
        qs, o = at("qs", [128, 2, N], F32R, o)
        ks, o = at("ks", [128, 2, N], F32R, o)
        kl, o = at("kl", [128, N], F32R, o)
        Pr, o = at("Pr", [P, 2, N], F32, o)
        PT, o = at("PT", [P, 2, NT, P], F32, o)
        assert oh <= o
        bvbc, o = at("bvbc", [P, D], F32, o)
        bobc, o = at("bobc", [P, D], F32, o)
        lngbc, o = at("lngbc", [P, D], F32, o)
        lnbbc, o = at("lnbbc", [P, D], F32, o)
        smm, o = at("smm", [P, 2, 3], F32, o)
        smb, o = at("smb", [P, 2], F32, o)
        sms, o = at("sms", [P, 2, 3], F32, o)
        smr, o = at("smr", [P, 4], F32, o)
        rowsT, o = at("rowsT", [128, KD, SLOT_ROWS], F32, A0)
        outrow, o = at("outrow", [128, D], F32, o)
        b2s, o = at("b2s", [128, 2, D], F32, o)
        assert o <= A0 + 40960
        We, o = at("We", [128, 2, KD * FF + KF * D], F32, A0 + 40960)
        rows_in, _ = at("rows_in", [128, ST, D], F32, A0 + 40960 + 65536)
        hid, o = at("hid", [128, KF, 128], F32, o)
        W1e = We[:, :, 0:KD * FF].rearrange("p s (k n) -> p s k n", k=KD)
        W2e = We[:, :, KD * FF:].rearrange("p s (k n) -> p s k n", k=KF)
        gW, _ = at("gW", [128, KD, EXPERTS], F32, o)
        gbias, _ = at("gbias", [P, EXPERTS], F32, o + 128)
        back, _ = at("back", [P, NT, D], F32, f0)
        XNT3, o = at("XNT3", [128, KD, N], F32, f0)
        rowbc3, o = at("rowbc3", [128, NPAD], F32, o)
        agg0, o6 = at("agg0", [128, KD, N], F32, o)
        XN3, o = at("XN3", [P, NT, D], F32, o)
        o = max(o, o6)
        HH, o = at("HH", [P, NT, D], F32R, o)
        HL, o = at("HL", [P, NT, D], F32R, o)
        Wsl, o = at("Wsl", [128, 2, KD, D], F32, o)
        Wsr, o = at("Wsr", [128, 2, KD, D], F32, o)
        aggc, o = at("aggc", [128, KD, 250], F32, o)
        hTc, o = at("hTc", [128, KD, 2, 126], F32, o)
        blbc, o = at("blbc", [P, 2, D], F32, o)
        gW2, _ = at("gW2", [128, KD, SAGE], F32, o - 4096)
        gbias2, _ = at("gbias2", [P, SAGE], F32, o - 4096 + 64)
        XNT4, o = at("XNT4", [128, KD, N], F32, A0)
        XN4, o = at("XN4", [P, NT, D], F32, o)
        g1T, o = at("g1T", [128, KD, D], F32, o)
        g1b, o = at("g1b", [128, KD], F32, o)
        g2T, o = at("g2T", [128, KD, EXPERTS], F32, o)
        g2bbc, o = at("g2bbc", [128, EXPERTS], F32, o)
        g2bcol, o = at("g2bcol", [EXPERTS, 1], F32, o)
        W1m, o = at("W1m", [128, KD, MF], F32, o)
        W2m, o = at("W2m", [128, KM, D], F32, o)
        tv, o = at("tv", [128, 4, 1024], F32, o)
        m1b, o = at("m1b", [128, KM], F32, o)
        tvb1, o = at("tvb1", [128, KM, EXPERTS], F32, o)
        tvt, o = at("tvt", [128, KM, EXPERTS], F32, o)
        tvr, o = at("tvr", [128, KM], F32, o)
        tvb2, o = at("tvb2", [EXPERTS, D], F32, o)
        tvg, o = at("tvg", [EXPERTS, D], F32, o)
        tvb, o = at("tvb", [EXPERTS, D], F32, o)
        m2bc, o = at("m2bc", [P, D], F32, o)
        mgbc, o = at("mgbc", [P, D], F32, o)
        mbbc, o = at("mbbc", [P, D], F32, o)
        c03, o = at("c03", [EXPERTS, P], F32, o)
        ghs, o = at("ghs", [128, KD, 3], F32, o)
        ghm, o = at("ghm", [128, KD], F32, o)
        ghb, o = at("ghb", [128, KD, 128], F32, o)
        gT, o = at("gT", [EXPERTS, 128], F32, o)
        upT, o = at("upT", [128, KM, N], F32, o)

        names = """unit_ready taken_by_vector taken_by_scalar vector_step scalar_step
            edges_in x_in w1_in w2_in l0b_in xback_in qkvw_in attnb_in wo_in gate_in moeb_in
            w1e_in0 w1e_in1 w2e_in0 w2e_in1 table_ready slots_ready rows_scattered rows_loaded rows_stored rows_back
            hid_ready hid_done y_ready y_taken expert_done rows_zero rows_out_ready spilled unspilled gate2_in sl_in0 sl_in1 g1_in merge_in tv_in0 tv_in1 tv_in2 tv_in3
            out_stored iota_done ident_done adj_zero onehots_used onehots_ready counts_read0 counts_read1 counts_added0 counts_added1 high_ready low_ready fields_ready pairs_added
            edges_ready span_ready dcol_ready chunk_staged adj_ready
            moments_ready std_ready norm_ready split_hi split_lo h2_hi znorm_sq znorm_sum znorm_root x_ready
            staged_by_vector staged_by_scalar weights_hi weights_lo xt_hi scores_ready rowmax_ready exp_done pt_ready pt_by_vector pt_by_scalar
            pv_ready pv_taken gate_max gate_exp gates_ready
            bias_added relu_done h1_ready relu2_done row3_ready ghm_ready gate_bc bias_in_residual tail_ready bias_in_x std_of_tile2 std_of_tile5
            const_ready tv_used resid_ready bias_staged""".split()
        S = {n: sem(n) for n in names}

        def ready(eng, name, k, i=0):
            eng.wait_ge(S["unit_ready"], U.ready(name, k, i))

        def taken(eng, name, k, i=0):
            v, a = U.taken(name, k, i)
            for who, n in (("taken_by_vector", v), ("taken_by_scalar", a)):
                if not (isinstance(n, int) and n == 0):
                    eng.wait_ge(S[who], n)

        def bank(name, k):
            return PS[:, k % 8, :]

        STD_BEFORE = [0, 1, 2, 2, 3, 4]
        SAGE_V = U.at["sage"][3].count("V")

        def up_to(eng, n, most, body, sure=False):
            def step(m):
                if m == 2:
                    with eng.Fori(2, most) as m:
                        with eng.If(m < n):
                            body(m)
                    return
                body(m)
                with eng.If(n > m + 1):
                    step(m + 1)

            if sure:
                step(0)
            else:
                with eng.If(n > 0):
                    step(0)

        def pairs(eng, body, start_group=None):
            name = eng.engine.name
            done, uses = eng.alloc_register(f"pairs_{name}"), [eng.alloc_register(f"set_{s}_{name}") for s in range(2)]
            for r in [done] + uses:
                eng.reg_mov(r, 0)
            eng.wait_ge(S["span_ready"], 1)
            with eng.Fori(0, GROUPS // 2) as g2:
                for half in range(2):
                    g = g2 * 2 + half
                    n = eng.value_load(span[0:1, bass.ds(g, 1)], min_val=1, max_val=NT)
                    first = eng.value_load(span[0:1, bass.ds(g + GROUPS, 1)], min_val=0, max_val=NT - 1)
                    if start_group:
                        start_group(g, eng.snap(done))

                    def pair(m):
                        s = (half + m) % 2 if isinstance(m, int) else 0
                        j = nc.s_assert_within(first + m, 0, NT - 1, skip_runtime_bounds_check_because="a group's chunks lie between its first and last destination")
                        body(eng.snap(done), j, s, [eng.snap(v) for v in uses])
                        eng.reg_add(done, done, 1)
                        eng.reg_add(uses[s], uses[s], 1)

                    up_to(eng, n, NT, pair, sure=True)

        block = ctx.enter_context(nc.Block())

        def bcast(v, n=P):
            return v.rearrange("(a d) -> a d", a=1).to_broadcast([n, v.shape[0]])

        def tiles(v):
            return v.rearrange("(t p) d -> p t d", p=P)

        def rows(v):
            return v.rearrange("(k p) n -> p k n", p=128)

        @block.sync
        def _(sp):
            sp.dma_start(edgei[:, 0], t["src"].rearrange("(r n) -> r n", r=EROWS)).then_inc(S["edges_in"], 16)
            sp.dma_start(edgei[:, 1], t["dst"].rearrange("(r n) -> r n", r=EROWS)).then_inc(S["edges_in"], 16)
            sp.dma_start(x0[:], tiles(t["x"])).then_inc(S["x_in"], 16)
            sp.dma_start(l0b1[:], t["L0_gnn_b1"]).then_inc(S["l0b_in"], 16)
            sp.dma_start(bq[:], t["L0_ffn_bq"]).then_inc(S["l0b_in"], 16)
            sp.dma_start(bk[:], t["L0_ffn_bk"]).then_inc(S["l0b_in"], 16)
            sp.dma_start(b1e[:, 0:EXPERTS], t["L0_ffn_b1"]).then_inc(S["l0b_in"], 16)
            sp.wait_ge(S["adj_ready"], 1)
            sp.dma_start(W1[:], rows(t["L0_gnn_W1"])).then_inc(S["w1_in"], 16)
            sp.wait_ge(S["norm_ready"], NT)
            sp.dma_start(W2[:], rows(t["L0_gnn_W2"])).then_inc(S["w2_in"], 16)
            ready(sp, "gcn", U.size("gcn") - 1)
            sp.dma_start(X[:], tiles(t["x"])).then_inc(S["xback_in"], 16)
            sp.dma_start(b2bc[:], bcast(t["L0_gnn_b2"])).then_inc(S["xback_in"], 16)
            sp.dma_start(spill, AT[:].bitcast(F32)).then_inc(S["spilled"], 16)
            ready(sp, "agg2", NT - 1)
            sp.wait_ge(S["x_ready"], NT)
            for m, v in enumerate(("L0_ffn_Wq", "L0_ffn_Wk", "L0_ffn_Wv")):
                sp.dma_start(Wf[:, m], rows(t[v])).then_inc(S["qkvw_in"], 16)
            for b, v in ((bvbc, "L0_ffn_bv"), (bobc, "L0_ffn_bo"), (lngbc, "L0_ffn_ln1_g"), (lnbbc, "L0_ffn_ln1_b")):
                sp.dma_start(b[:], bcast(t[v])).then_inc(S["attnb_in"], 16)
            ready(sp, "qkv", U.size("qkv") - 1)
            sp.dma_start(Wq[:], rows(t["L0_ffn_Wo"])).then_inc(S["wo_in"], 16)
            def expert_weights(e, s):
                w1 = t["L0_ffn_W1"][bass.ds(e, 1)].rearrange("a (k p) n -> p (a k) n", p=128)
                w2 = t["L0_ffn_W2"][bass.ds(e, 1)].rearrange("a (k p) n -> p (a k) n", p=128)
                sp.dma_start(W1e[:, s], w1).then_inc(S[f"w1e_in{s}"], 16)
                sp.dma_start(W2e[:, s], w2).then_inc(S[f"w2e_in{s}"], 16)
                sp.dma_start(b2s[:, s], t["L0_ffn_b2"][bass.ds(e, 1)].to_broadcast([128, D])).then_inc(S[f"w2e_in{s}"], 16)

            ready(sp, "wo", NT - 1)
            sp.dma_start(W1e[:, 0], rows(t["L0_ffn_W1"][0])).then_inc(S["w1e_in0"], 16)
            ready(sp, "ht", NT - 1)
            sp.wait_ge(S["norm_ready"], 3 * NT)
            sp.dma_start(gW[:], rows(t["L0_ffn_gate_W"])).then_inc(S["gate_in"], 16)
            sp.dma_start(gbias[:], bcast(t["L0_ffn_gate_b"])).then_inc(S["gate_in"], 16)
            sp.dma_start(W2e[:, 0], rows(t["L0_ffn_W2"][0])).then_inc(S["w2e_in0"], 16)
            sp.wait_ge(S["rows_scattered"], 16 * NT)
            sp.dma_start(rows_in[:], rows_x.rearrange("(i p) d -> p i d", p=128)).then_inc(S["rows_loaded"], 16)
            sp.dma_start(b2s[:, 0], bcast(t["L0_ffn_b2"][0], 128)).then_inc(S["w2e_in0"], 16)
            ready(sp, "rows", ST - 1)
            expert_weights(1, 1)
            with sp.Fori(1, EXPERTS // 2) as i:
                for s in range(2):
                    sp.wait_ge(S["expert_done"], i * 2 + (s + 1))
                    expert_weights(i * 2 + s, s)
            sp.wait_ge(S["expert_done"], EXPERTS + 2)
            sp.wait_ge(S["rows_back"], 16 * NT)
            sp.dma_start(AT[:].bitcast(F32), spill).then_inc(S["unspilled"], 16)
            sp.dma_start(gW2[:], rows(t["L1_gnn_gate_W"])).then_inc(S["gate2_in"], 16)
            sp.dma_start(gbias2[:], bcast(t["L1_gnn_gate_b"])).then_inc(S["gate2_in"], 16)
            sp.wait_ge(S["gates_ready"], 2)
            with sp.Fori(0, SAGE) as i:
                for l in range(2):
                    if l == 0:
                        sp.wait_ge(S["taken_by_vector"], i * SAGE_V + (U.taken("sage", NT)[0] - SAGE_V))
                    else:
                        sp.wait_ge(S["taken_by_vector"], U.taken("sage", 0, i)[0])
                    sp.wait_ge(S["gates_ready"], 2)
                    wl = t["L1_gnn_Wl"][bass.ds(i, 1), l].rearrange("a (k p) n -> p (a k) n", p=128)
                    wr = t["L1_gnn_Wr"][bass.ds(i, 1), l].rearrange("a (k p) n -> p (a k) n", p=128)
                    sp.dma_start(Wsl[:, l], wl).then_inc(S[f"sl_in{l}"], 16)
                    sp.dma_start(Wsr[:, l], wr).then_inc(S[f"sl_in{l}"], 16)
                    sp.dma_start(blbc[:, l], t["L1_gnn_bl"][bass.ds(i, 1), l].to_broadcast([P, D])).then_inc(S[f"sl_in{l}"], 16)
            taken(sp, "xt3", 0)
            ready(sp, "sage", U.size("sage") - 1, SAGE - 1)
            sp.dma_start(g1T[:], rows(t["L1_ffn_gfc1_w"])).then_inc(S["g1_in"], 16)
            sp.dma_start(g1b[:], t["L1_ffn_gfc1_b"]).then_inc(S["g1_in"], 16)
            for dst, v in ((g2T, rows(t["L1_ffn_gfc2_w"])), (g2bbc, bcast(t["L1_ffn_gfc2_b"], 128)),
                           (g2bcol, t["L1_ffn_gfc2_b"].rearrange("(e a) -> e a", a=1)),
                           (W1m, rows(t["L1_ffn_W1"])), (W2m, rows(t["L1_ffn_W2"])), (m1b, t["L1_ffn_b1"]),
                           (tvb1, t["L1_ffn_tv_b1"]), (tvb2, t["L1_ffn_tv_b2"]), (tvg, t["L1_ffn_tv_ln_g"]),
                           (tvb, t["L1_ffn_tv_ln_b"]), (m2bc, bcast(t["L1_ffn_b2"])),
                           (mgbc, bcast(t["L1_ffn_ln_g"])), (mbbc, bcast(t["L1_ffn_ln_b"]))):
                sp.dma_start(dst[:], v).then_inc(S["merge_in"], 16)
            for n in range(2 * EXPERTS):
                e, second = n % EXPERTS, n // EXPERTS
                if n >= 4:
                    sp.wait_ge(S["tv_used"], n - 3)
                v = t["L1_ffn_tv_W2"][e] if second else t["L1_ffn_tv_W1"][e]
                k = KM if second else KD
                sp.dma_start(tv[:, n % 4].rearrange("p (k n) -> p k n", k=k), rows(v)).then_inc(S[f"tv_in{n % 4}"], 16)
            n = 0
            for i in range(NT):
                sp.wait_ge(S["tail_ready"], i + 1)
                sp.dma_start(tiles(out)[:, i], XN4[:, i]).then_inc(S["out_stored"], 16)
            sp.wait_ge(S["out_stored"], 16 * NT)

        @block.gpsimd
        def _(pool):
            pool.iota(iota[:], [[1, NPAD]], base=0, channel_multiplier=0, allow_small_or_imprecise_dtypes=True).then_inc(S["iota_done"], 1)
            pool.iota(idx8[:], [[-1, EXPERTS]], base=EXPERTS, channel_multiplier=0, allow_small_or_imprecise_dtypes=True).then_inc(S["iota_done"], 1)
            pool.memset(ident[:], 0.0).then_inc(S["ident_done"], 1)
            pool.memset(onesr[:].bitcast(F32), 1.0).then_inc(S["ident_done"], 1)
            pool.memset(eps[:], EPS).then_inc(S["ident_done"], 1)
            pool.memset(tri[:], 1.0).then_inc(S["ident_done"], 1)
            pool.memset(ones[:], 1.0).then_inc(S["ident_done"], 1)
            pool.memset(b1e[:, EXPERTS:EXPERTS + 2], 0.0).then_inc(S["ident_done"], 1)
            pool.memset(zrow[:], 0.0).then_inc(S["ident_done"], 1)
            pool.wait_ge(S["ident_done"], 7)
            pool.affine_select(out=tri[:], in_=tri[:], compare_op=ALU.is_gt, fill=0.0, base=0,
                               pattern=[[1, 128]], channel_multiplier=-1).then_inc(S["ident_done"], 1)
            pool.affine_select(out=ident[:], in_=ident[:], compare_op=ALU.not_equal, fill=1.0, base=0,
                               pattern=[[-1, 128]], channel_multiplier=1).then_inc(S["ident_done"], 1)
            pool.memset(AT[:].bitcast(F32), 0.0).then_inc(S["adj_zero"], 1)
            for s in range(2):
                pool.memset(cnt[:, s], 0.0).then_inc(S[f"counts_read{s}"], 1)
                pool.memset(cnthi[:, s], 0).then_inc(S[f"counts_added{s}"], 1)
            pool.wait_ge(S["adj_zero"], 1)
            for v, done in ((rows_x, "rows_zero"), (rows_y, "rows_stored")):
                pool.dma_start(v.rearrange("(i p) d -> p i d", p=128),
                               zrow[:].rearrange("p (a d) -> p a d", a=1).to_broadcast([128, ST, D])).then_inc(S[done], 16)
            def fields(q, j, s, u):
                cols = bass.ds(j * P, P)
                for m in range(2):
                    pool.wait_ge(S[f"counts_added{m}"], u[m] + 1)
                pool.wait_ge(S["fields_ready"], q + 1)
                pool.tensor_tensor(cntlo[:, s], cnt[:, s], cntlo[:, s], ALU.add).then_inc(S["low_ready"], 1)
                pool.tensor_tensor(AT[:, PACKED:NT, cols], AT[:, PACKED:NT, cols].bitcast(F32), cnthf[:, s], ALU.add)
                pool.wait_ge(S["low_ready"], q + 1)
                pool.tensor_tensor(AT[:, 0:PACKED, cols], AT[:, 0:PACKED, cols].bitcast(F32), cntlo[:, s], ALU.add).then_inc(S[f"counts_added{s}"], 1)

            pairs(pool, fields)
            pool.memset(cnt[:, 0, 0, 0:1], 0.0).then_inc(S["pairs_added"], 1)
            pool.wait_ge(S["qkvw_in"], 48)
            for m in range(3):
                pool.wait_ge(S["weights_hi"], m + 1)
                pool.tensor_tensor(Wl[:, m], Wf[:, m], Wh[:, m].bitcast(F32), ALU.subtract).then_inc(S["weights_lo"], 1)
            pool.wait_ge(S["attnb_in"], 64)
            ready(pool, "xt1", NT - 1)
            for i in range(NT):
                pool.tensor_tensor(XN[:, i], XN[:, i], bobc[:], ALU.add).then_inc(S["resid_ready"], 1)
            pool.wait_ge(S["slots_ready"], 1)
            pool.wait_ge(S["norm_ready"], 3 * NT)
            pool.wait_ge(S["rows_zero"], 16)
            for i in range(NT):
                pool.indirect_dma_start(rows_x[:, :], bass.IndirectOffsetOnAxis(ap=sloti[:, i:i + 1], axis=0), XN[:, i], None).then_inc(S["rows_scattered"], 16)
            pool.wait_ge(S["table_ready"], 1)
            with pool.Fori(0, EXPERTS) as e:
                n = pool.value_load(table[0:1, bass.ds(e, 1)], min_val=0, max_val=MOST)
                start = pool.value_load(table[0:1, bass.ds(e + EXPERTS, 1)], min_val=0, max_val=ST)

                def tile(m):
                    i = nc.s_assert_within(start + m, 0, ST - 1, skip_runtime_bounds_check_because="the experts' tiles add up to at most ST")
                    pool.wait_ge(S["y_taken"], i + 2)
                    pool.dma_start(rows_y[bass.ds(i * 128, 128), :], outrow[:]).then_inc(S["rows_stored"], 16)

                up_to(pool, n, MOST, tile)
            pool.wait_ge(S["rows_out_ready"], 1)
            for i in range(NT):
                pool.indirect_dma_start(back[:, i], None, rows_y[:, :], bass.IndirectOffsetOnAxis(ap=sloti[:, i:i + 1], axis=0)).then_inc(S["rows_back"], 16)
            taken(pool, "merge", 5)
            for i in range(NT):
                pool.tensor_tensor(XN4[:, i], XN4[:, i], m2bc[:], ALU.add).then_inc(S["bias_in_residual"], 1)
            for i in range(NT):
                pool.tensor_tensor(X[:, i], X[:, i], mbbc[:], ALU.add).then_inc(S["bias_in_x"], 1)

        OWN = [slice(0, HD), slice(HD, 2 * HD)]

        def pt_out_scalar(act, b, i):
            act.wait_ge(S["pt_ready"], b * 60 + (3 * i + 2))
            if i >= 2:
                act.wait_ge(S["pv_ready"], b * 20 + (i - 1))
            act.activation(PT[:, i % 2, 4:8, :], PS[0:P, 4 + (3 * i + 1) % 3, 0:500].rearrange("p (k n) -> p k n", n=P),
                           ACT.Copy).then_inc(S["pt_by_scalar"], 1)

        @block.scalar
        def _(act):
            TV, TA = S["taken_by_vector"], S["taken_by_scalar"]
            def root(k):
                act.wait_ge(S["moments_ready"], NT * (k + 1))
                if k:
                    act.wait_ge(S["std_ready"], STD_BEFORE[k])
                act.activation(std[:], mv[:, :, 1], ACT.Sqrt, bias=eps[0:P, :]).then_inc(S["std_ready"], 1)

            def roots(k):
                act.wait_ge(S["std_ready"], STD_BEFORE[k])
                for i in range(NT):
                    act.wait_ge(S["moments_ready"], NT * k + i + 1)
                    act.activation(std[:, i:i + 1], mv[:, i, 1:2], ACT.Sqrt, bias=eps[0:P, :]).then_inc(S[f"std_of_tile{k}"], 1)

            act.wait_ge(S["ident_done"], 9)
            def counts(q, j, s, u):
                act.wait_ge(S["onehots_used"], q * GROUP + 2 * GROUP)
                act.wait_ge(S[f"counts_added{s}"], u[s] + 1)
                for dst, scale, done in ((cnthi, 1.0 / FIELD, "high_ready"), (cnt, 1.0, f"counts_read{s}")):
                    act.activation(dst[:, s, 0:4], PS[0:P, 2 * s, 0:4 * P].rearrange("p (k n) -> p k n", n=P), ACT.Copy, scale=scale)
                    act.activation(dst[:, s, 4], PS[0:P, 2 * s + 1, 0:P], ACT.Copy, scale=scale).then_inc(S[done], 1)
                act.wait_ge(S["high_ready"], q + 1)
                act.activation(cnthf[:, s], cnthi[:, s], ACT.Copy)
                act.activation(cntlo[:, s], cnthi[:, s], ACT.Copy, scale=-FIELD).then_inc(S["fields_ready"], 1)

            pairs(act, counts)
            for k in range(3):
                ready(act, "degree", k)
                act.activation(rowbc[:, k * DCH:(k + 1) * DCH], bank("degree", k)[:, 0:DCH], ACT.Sqrt).then_inc(TA, 1)
            ready(act, "degree", 3)
            act.activation(dcol[:], bank("degree", 3)[0:P, 0:2 * NT].rearrange("p (t a) -> p t a", a=2)[:, :, 0], ACT.Sqrt).then_inc(TA, 1)
            root(0)
            act.wait_ge(S["dcol_ready"], 1)
            for i in range(NT):
                act.wait_ge(S["norm_ready"], i + 1)
                act.activation(XH[:, i], XS[:, i], ACT.Copy, scale=dcol[:, i:i + 1]).then_inc(S["split_hi"], 1)
            act.wait_ge(S["l0b_in"], 64)
            for c in range(5):
                for f in range(1, KF, 2):
                    k = 18 * c + f
                    ready(act, "gcn", k)
                    act.activation(zT[:, f], bank("gcn", k)[:, 0:250], ACT.Relu, bias=l0b1[:, f:f + 1]).then_inc(TA, 1)
                for i in range(2):
                    k, tt = 18 * c + KF + i, 2 * c + i
                    ready(act, "gcn", k)
                    act.activation(XH[:, tt], bank("gcn", k)[0:P, :], ACT.Copy, scale=dcol[:, tt:tt + 1]).then_inc(S["h2_hi"], 1)
            for i in range(NT):
                taken(act, "agg2", i + 1)
                act.activation(zsq[:, i % 2], ZF[:, i], ACT.Square).then_inc(S["znorm_sq"], 1)
                act.wait_ge(S["znorm_sum"], i + 1)
                act.activation(znr[:, i], znr[:, i], ACT.Sqrt).then_inc(S["znorm_root"], 1)
            root(1)
            act.wait_ge(S["qkvw_in"], 48)
            for m in range(3):
                act.activation(Wh[:, m], Wf[:, m], ACT.Copy).then_inc(S["weights_hi"], 1)
            for i in range(NT):
                ready(act, "xt1", i)
                act.activation(XNTh[:, :, i * P:(i + 1) * P], bank("xt1", i)[:, 0:KD * P].rearrange("p (k n) -> p k n", k=KD),
                               ACT.Copy).then_inc(S["xt_hi"], 1)

            def transposed(name, dst, stride=P):
                for i in range(1, NT, 2):
                    ready(act, name, i)
                    act.activation(dst[:, :, i * P:(i + 1) * P], bank(name, i)[:, 0:KD * P].rearrange("p (k n) -> p k n", k=KD),
                                   ACT.Copy).then_inc(TA, 1)

            for n in range(1, 24, 2):
                f, c = (n % 12) // 3, n % 3
                lo, w = CHUNKS[c]
                ready(act, "qkv", n)
                if n < 12:
                    act.wait_ge(S["const_ready"], 1)
                    act.activation(qT[:, f, lo:lo + w], bank("qkv", n)[:, 0:w], ACT.Identity, bias=bq[:, f:f + 1], scale=-0.125).then_inc(TA, 1)
                else:
                    act.activation(kT[:, f, lo:lo + w], bank("qkv", n)[:, 0:w], ACT.Identity, bias=bk[:, f:f + 1]).then_inc(TA, 1)
            taken(act, "qkv", U.size("qkv"))

            def upper_bits(b, hh, m):
                src, dst = ((qT, qs[OWN[hh], hh:hh + 1]), (kT, ks[OWN[hh], hh:hh + 1]), (kT, ks[OWN[1 - hh], hh:hh + 1]))[m]
                act.activation(dst, src[OWN[hh], bass.ds(b, 1)], ACT.Copy).then_inc(S["staged_by_scalar"], 1)

            def exponentials(b, i):
                act.wait_ge(S["rowmax_ready"], b * 20 + (i + 1))
                if i >= 2:
                    act.wait_ge(S["pt_ready"], b * 60 + 3 * (i - 1))
                for k, (lo, w) in enumerate(CHUNKS):
                    act.activation(Pr[:, i % 2, lo:lo + w], PS[0:P, (3 * i + k) % 4, 0:w], ACT.Exp, bias=smb[:, i % 2:i % 2 + 1],
                                   scale=-1.0, accum_out=sms[:, i % 2, k:k + 1]).then_inc(S["exp_done"], 1)

            def head_pair(b, last):
                for i in range(20):
                    if i < 19 or not last:
                        exponentials(b, i + 1)
                    pt_out_scalar(act, b, i)
                    if i in (1, 3, 5):
                        upper_bits(b, 1, i // 2)
                    if i in (11, 13, 15) and not last:
                        upper_bits(b + 1, 0, i // 2 - 5)

            for m in range(3):
                upper_bits(0, 0, m)
            exponentials(0, 0)
            with act.Fori(0, HEADS // 2 - 1) as b:
                head_pair(b, False)
            head_pair(HEADS // 2 - 1, True)
            transposed("ot", OT)
            roots(2)
            transposed("ht", XNT)
            act.wait_ge(S["gate_max"], 1)
            act.activation(ga[:], ga[:], ACT.Exp).then_inc(S["gate_exp"], 1)
            for i in range(1, ST, 2):
                ready(act, "rows", i)
                act.activation(rowsT[:, :, i * 128:(i + 1) * 128], bank("rows", i).rearrange("p (k n) -> p k n", k=KD), ACT.Copy).then_inc(TA, 1)
            act.wait_ge(S["table_ready"], 1)
            with act.Fori(0, EXPERTS // 2) as e2:
                for s in range(2):
                    n = act.value_load(table[0:1, bass.ds(e2 * 2 + s, 1)], min_val=0, max_val=MOST)
                    start = act.value_load(table[0:1, bass.ds(e2 * 2 + (s + EXPERTS), 1)], min_val=0, max_val=ST)

                    def tile(m):
                        act.wait_ge(S["expert_done"], e2 * 2 + (s + 1))
                        i = nc.s_assert_within(start + m, 0, ST - 1, skip_runtime_bounds_check_because="the experts' tiles add up to at most ST")
                        for f in range(KF):
                            act.wait_ge(S["hid_ready"], i * KF + (f + 1))
                            act.activation(hid[:, f], PS[:, f % 6, 0:128], ACT.Gelu_apprx_tanh, bias=b1c[:, s, f:f + 1]).then_inc(S["hid_done"], 1)

                    up_to(act, n, MOST, tile)
            root(3)
            transposed("xt2", XNT3)
            for i in range(NT):
                act.wait_ge(S["norm_ready"], 3 * NT + i + 1)
                act.activation(HH[:, i], XN3[:, i], ACT.Copy).then_inc(S["split_hi"], 1)
            act.wait_ge(S["gate_max"], 2)
            act.activation(ga[:, :, 0:SAGE], ga[:, :, 0:SAGE], ACT.Exp).then_inc(S["gate_exp"], 1)
            with act.Fori(0, SAGE) as e:
                for i in range(NT):
                    act.wait_ge(S["bias_added"], e * (2 * NT) + (i + 1))
                    act.activation(HH[:, i], bank("sage", i)[0:P, :], ACT.Relu).then_inc(S["relu_done"], 1)
                for c in range(5):
                    for i in range(2):
                        k = NT + 8 * c + 4 + i
                        ready(act, "sage", k, e)
                        act.activation(hTc[:, :, i, :], bank("sage", k)[:, 0:KD * 126].rearrange("p (k n) -> p k n", k=KD), ACT.Copy).then_inc(TA, 1)
                    for i in range(2):
                        k, tt = NT + 8 * c + 6 + i, 2 * c + i
                        act.wait_ge(S["bias_added"], e * (2 * NT) + (NT + tt + 1))
                        act.activation(bank("sage", k)[0:P, :], bank("sage", k)[0:P, :], ACT.Relu).then_inc(S["relu2_done"], 1)
            root(4)
            transposed("xt3", XNT4)
            act.wait_ge(S["g1_in"], 32)
            for n in range(12):
                f, c = n // 3, n % 3
                ready(act, "gh", n)
                w = CHUNKS[c][1]
                act.activation(bank("gh", n)[:, 0:w], bank("gh", n)[:, 0:w], ACT.Relu, bias=g1b[:, f:f + 1],
                               accum_out=ghs[:, f, c:c + 1]).then_inc(TA, 1)
            act.wait_ge(S["tv_used"], EXPERTS)
            for n in range(6):
                f, c = n // 3, n % 3
                lo, w = CHUNKS[c]
                ready(act, "up", n)
                act.activation(upT[:, f, lo:lo + w], bank("up", n)[:, 0:w], ACT.Relu, bias=m1b[:, f:f + 1]).then_inc(TA, 1)
            roots(5)

        @block.vector
        def _(dve):
            TV, TA = S["taken_by_vector"], S["taken_by_scalar"]
            steps = [0]

            def did(ins):
                ins.then_inc(S["vector_step"], 1)
                steps[0] += 1
                return steps[0]

            def own(n, extra=0):
                dve.wait_ge(S["vector_step"], extra + n)

            def moments(i, src):
                own(did(dve.bn_stats(bnst[:, i], src)))
                dve.bn_aggr(mv[:, i], bnst[:, i]).then_inc(S["moments_ready"], 1)

            def inverse(k):
                dve.wait_ge(S["std_ready"], STD_BEFORE[k] + 1)
                own(did(dve.reciprocal(rstd[:], std[:])))

            def inverse_of(i, k):
                dve.wait_ge(S[f"std_of_tile{k}"], i + 1)
                own(did(dve.reciprocal(rstd[:, i:i + 1], std[:, i:i + 1])))

            def normalized(i, dst, src):
                return dve.tensor_scalar(dst, src, mv[:, i, 0:1], rstd[:, i:i + 1], ALU.subtract, ALU.mult)

            dve.wait_ge(S["edges_in"], 32)
            dve.tensor_copy(edgef[:], edgei[:]).then_inc(S["edges_ready"], 1)
            for k, v in enumerate((srcf, dstf)):
                ready(dve, "edges", k)
                dve.tensor_copy(v[:].rearrange("p (r h) -> p h r", h=2), bank("edges", k)[0:P, 0:2 * EROWS].rearrange("p (h r) -> p h r", h=2)).then_inc(TV, 1)
            dve.wait_ge(TV, 2)
            for j in range(1, NT):
                n = did(dve.tensor_scalar(above[:, j - 1], dstf[:], float(j * P), None, ALU.is_ge))
            own(n)
            dve.tensor_reduce(aboves[:], above[:].rearrange("p j (g c) -> p j g c", c=GROUP), AX, ALU.add).then_inc(S["edges_ready"], 1)
            own(did(dve.tensor_scalar(srcq[:], srcf[:], float(HALF), None, ALU.is_ge)))
            did(dve.tensor_scalar(srcw[:], srcq[:], FIELD - 1.0, 1.0, ALU.mult, ALU.add))
            own(did(dve.scalar_tensor_tensor(out=srcf[:], in0=srcq[:], scalar=-float(HALF), in1=srcf[:], op0=ALU.mult, op1=ALU.add)))
            ready(dve, "edges", 2)
            cum = bank("edges", 2)[0:P, 0:(NT - 1) * GROUPS].rearrange("p (j g) -> p j g", g=GROUPS)
            did(dve.tensor_scalar(within[:, 0], cum, 1.0, None, ALU.is_ge))
            dve.tensor_scalar(within[:, 1], cum, float(GROUP * P), None, ALU.is_ge).then_inc(TV, 1)
            own(steps[0])
            dve.wait_ge(TV, 3)
            own(did(dve.tensor_reduce(spanf[:], within[:].rearrange("p a j g -> p a g j"), AX, ALU.add)))
            did(dve.tensor_copy(span[:, GROUPS:2 * GROUPS], spanf[:, 1]))
            own(did(dve.tensor_tensor(spanf[:, 0], spanf[:, 0], spanf[:, 1], ALU.subtract)))
            dve.tensor_scalar(span[:, 0:GROUPS], spanf[:, 0], 1.0, None, ALU.add).then_inc(S["span_ready"], 1)
            dve.wait_ge(S["iota_done"], 2)
            dve.wait_ge(S["adj_zero"], 1)
            dve.memset(ohs[:], 0.0).then_inc(S["onehots_used"], GROUP)
            dve.memset(ohd[:], 0.0).then_inc(S["onehots_ready"], 1)
            def stage_edges(g, done):
                dve.wait_ge(S["onehots_ready"], done * GROUP + 1)
                for m, v in enumerate((srcf, srcw, dstf)):
                    dve.tensor_copy(edge[:, m], v[:, bass.ds(g * GROUP, GROUP)])

            def onehots(q, j, s, u):
                dve.wait_ge(S["onehots_ready"], q * GROUP + 1)
                dve.tensor_copy(iotaj[:], iota[:, bass.ds(j * P, P)]).then_inc(S["chunk_staged"], 1)
                dve.wait_ge(S["chunk_staged"], q + 1)
                for c in range(GROUP):
                    dve.wait_ge(S["onehots_used"], q * GROUP + (c + 1))
                    dve.tensor_scalar(ohs[:, c], iota[:, 0:HALF], edge[:, 0, c:c + 1], edge[:, 1, c:c + 1], ALU.is_equal, ALU.mult)
                    dve.tensor_scalar(ohd[:, c], iotaj[:], edge[:, 2, c:c + 1], None, ALU.is_equal).then_inc(S["onehots_ready"], 1)

            pairs(dve, onehots, stage_edges)
            dve.wait_ge(S["ident_done"], 9)
            own(did(dve.tensor_copy(identr[:], ident[:])))
            dve.wait_ge(S["pairs_added"], 1)
            for i in range(NT):
                blk = AT[:, i, i * P:(i + 1) * P]
                ins = dve.tensor_tensor(blk, blk.bitcast(F32), ident[0:P, 0:P], ALU.add)
            ins.then_inc(S["adj_ready"], 1)
            dve.wait_ge(S["x_in"], 16)
            for i in range(NT):
                moments(i, x0[:, i])
            inverse(0)
            dve.wait_ge(S["rows_zero"], 16)
            dve.wait_ge(S["rows_stored"], 16)
            for i in range(NT):
                normalized(i, XS[:, i], x0[:, i]).then_inc(S["norm_ready"], 1)
            taken(dve, "degree", 4)
            dve.reciprocal(dcol[:], dcol[:]).then_inc(S["dcol_ready"], 1)
            own(did(dve.reciprocal(rowbc[:, 0:N], rowbc[:, 0:N])))
            for i in range(NT):
                dve.wait_ge(S["split_hi"], i + 1)
                dve.scalar_tensor_tensor(out=XL[:, i], in0=XS[:, i], scalar=dcol[:, i:i + 1], in1=XH[:, i].bitcast(F32),
                                         op0=ALU.mult, op1=ALU.subtract).then_inc(S["split_lo"], 1)
            for k in range(12):
                c, f = k // KD, k % KD
                lo, w = CHUNKS[c]
                ready(dve, "agg1", k)
                dve.tensor_tensor(aggT[:, f, lo:lo + w], bank("agg1", k)[:, 0:w], rowbc[:, lo:lo + w], ALU.mult).then_inc(TV, 1)
            dve.wait_ge(S["l0b_in"], 64)
            dve.tensor_scalar(bq[:], bq[:], -0.125, None, ALU.mult).then_inc(S["const_ready"], 1)
            for c in range(5):
                for f in range(0, KF, 2):
                    k = 18 * c + f
                    ready(dve, "gcn", k)
                    dve.tensor_scalar(zT[:, f], bank("gcn", k)[:, 0:250], l0b1[:, f:f + 1], 0.0, ALU.add, ALU.max).then_inc(TV, 1)
                for i in range(2):
                    k, tt = 18 * c + KF + i, 2 * c + i
                    dve.wait_ge(S["h2_hi"], tt + 1)
                    dve.scalar_tensor_tensor(out=XL[:, tt], in0=bank("gcn", k)[0:P, :], scalar=dcol[:, tt:tt + 1],
                                             in1=XH[:, tt].bitcast(F32), op0=ALU.mult, op1=ALU.subtract).then_inc(TV, 1)
            dve.wait_ge(S["xback_in"], 32)

            def groupsum(i):
                dve.wait_ge(S["znorm_sq"], i + 1)
                dve.tensor_reduce(znr[:, i], zsq[:, i % 2].rearrange("p (g d) -> p g d", g=8), AX, ALU.add).then_inc(S["znorm_sum"], 1)

            def groupnorm(i):
                dve.wait_ge(S["znorm_root"], i + 1)
                own(did(dve.tensor_scalar(znr[:, i], znr[:, i], 1e-12, None, ALU.max)))
                own(did(dve.reciprocal(znr[:, i], znr[:, i])))
                z = ZF[:, i].rearrange("p (g d) -> p g d", g=8)
                own(did(dve.tensor_tensor(z, z, znr[:, i].rearrange("p (g a) -> p g a", a=1).to_broadcast([P, 8, 64]), ALU.mult)))
                dve.tensor_tensor(X[:, i], X[:, i], ZF[:, i], ALU.add).then_inc(S["x_ready"], 1)
                dve.wait_ge(S["x_ready"], i + 1)
                moments(i, X[:, i])

            for i in range(NT):
                ready(dve, "agg2", i)
                dve.scalar_tensor_tensor(out=ZF[:, i], in0=bank("agg2", i)[0:P, :], scalar=dcol[:, i:i + 1],
                                         in1=b2bc[:], op0=ALU.mult, op1=ALU.add).then_inc(TV, 1)
                if i:
                    groupnorm(i - 1)
                groupsum(i)
            groupnorm(NT - 1)
            inverse(1)
            dve.wait_ge(S["spilled"], 16)
            for i in range(NT):
                normalized(i, XN[:, i], X[:, i]).then_inc(S["norm_ready"], 1)

            def transposed(name, dst):
                for i in range(0, NT, 2):
                    ready(dve, name, i)
                    dve.tensor_copy(dst[:, :, i * P:(i + 1) * P], bank(name, i)[:, 0:KD * P].rearrange("p (k n) -> p k n", k=KD)).then_inc(TV, 1)

            for i in range(NT):
                ready(dve, "xt1", i)
                dve.wait_ge(S["xt_hi"], i + 1)
                dve.tensor_tensor(XNTl[:, :, i * P:(i + 1) * P], bank("xt1", i)[:, 0:KD * P].rearrange("p (k n) -> p k n", k=KD),
                                  XNTh[:, :, i * P:(i + 1) * P].bitcast(F32), ALU.subtract).then_inc(TV, 1)
            dve.wait_ge(S["const_ready"], 1)
            for n in range(0, 24, 2):
                f, c = (n % 12) // 3, n % 3
                lo, w = CHUNKS[c]
                ready(dve, "qkv", n)
                if n < 12:
                    dve.tensor_scalar(qT[:, f, lo:lo + w], bank("qkv", n)[:, 0:w], -0.125, bq[:, f:f + 1], ALU.mult, ALU.add).then_inc(TV, 1)
                else:
                    dve.tensor_scalar(kT[:, f, lo:lo + w], bank("qkv", n)[:, 0:w], bk[:, f:f + 1], None, ALU.add).then_inc(TV, 1)
            dve.wait_ge(S["attnb_in"], 64)
            for i in range(NT):
                ready(dve, "qkv", 24 + i)
                dve.tensor_tensor(V[:, i], bank("qkv", 24 + i)[0:P, :], bvbc[:], ALU.add).then_inc(TV, 1)

            per = 60
            taken(dve, "qkv", U.size("qkv"))

            def lower_bits(b, hh, m):
                own_, other = OWN[hh], OWN[1 - hh]
                src, hi = ((qT, qs), (kT, ks))[m]
                dst = kl[own_] if m else qs[other, hh]
                dve.wait_ge(S["staged_by_scalar"], b * 6 + (3 * hh + m + 1))
                dve.tensor_tensor(dst, src[own_, bass.ds(b, 1)].rearrange("p a n -> p (a n)"), hi[own_, hh].bitcast(F32), ALU.subtract).then_inc(S["staged_by_vector"], 1)

            def rowmax(b, i):
                for k, (lo, w) in enumerate(CHUNKS):
                    dve.wait_ge(S["scores_ready"], b * 60 + (3 * i + k + 1))
                    ins = dve.tensor_reduce(smm[:, i % 2, k:k + 1], PS[0:P, (3 * i + k) % 4, 0:w], AX, ALU.min)
                own(did(ins), b * per)
                dve.scalar_tensor_tensor(out=smb[:, i % 2:i % 2 + 1], in0=smm[:, i % 2, 0:1], scalar=smm[:, i % 2, 1:2],
                                         in1=smm[:, i % 2, 2:3], op0=ALU.min, op1=ALU.min).then_inc(S["rowmax_ready"], 1)

            def weighted(b, i):
                hh, tt = i // NT, i % NT
                dve.wait_ge(S["pv_ready"], b * 20 + (i + 1))
                dve.tensor_scalar(O[:, tt, bass.ds(b * 128 + hh * 64, 64)], PS[0:P, 7, 64 * (i % 2):64 * (i % 2) + 64],
                                  smr[:, i % 2:i % 2 + 1], None, ALU.mult).then_inc(S["pv_taken"], 1)

            def head_pair(b, last):
                for i in range(20):
                    if i < 19 or not last:
                        rowmax(b, i + 1)
                    for k in (0, 2):
                        nb = 4 if k == 0 else 2
                        dve.wait_ge(S["pt_ready"], b * 60 + (3 * i + k + 1))
                        if i >= 2:
                            dve.wait_ge(S["pv_ready"], b * 20 + (i - 1))
                        dve.tensor_copy(PT[:, i % 2, 4 * k:4 * k + nb, :], PS[0:P, 4 + (3 * i + k) % 3, 0:nb * P].rearrange("p (k n) -> p k n", n=P)).then_inc(S["pt_by_vector"], 1)
                    if i:
                        weighted(b, i - 1)
                    dve.wait_ge(S["exp_done"], b * 60 + (3 * i + 3))
                    own(did(dve.scalar_tensor_tensor(out=smr[:, 2 + i % 2:3 + i % 2], in0=sms[:, i % 2, 0:1], scalar=sms[:, i % 2, 1:2],
                                                     in1=sms[:, i % 2, 2:3], op0=ALU.add, op1=ALU.add)), b * per)
                    own(did(dve.reciprocal(smr[:, i % 2:i % 2 + 1], smr[:, 2 + i % 2:3 + i % 2])), b * per)
                    if i in (2, 4):
                        lower_bits(b, 1, i // 2 - 1)
                    if i in (12, 14) and not last:
                        lower_bits(b + 1, 0, i // 2 - 6)
                weighted(b, 19)

            for m in range(2):
                lower_bits(0, 0, m)
            rowmax(0, 0)
            base = steps[0]
            with dve.Fori(0, HEADS // 2 - 1) as b:
                head_pair(b, False)
                assert steps[0] - base == per
            steps[0] = base
            dve_last = HEADS // 2 - 1
            head_pair(dve_last, True)
            steps[0] += per * dve_last
            transposed("ot", OT)
            dve.wait_ge(S["resid_ready"], NT)
            def post_norm(i):
                inverse_of(i, 2)
                own(did(normalized(i, XN[:, i], XN[:, i])))
                own(did(dve.tensor_tensor(XN[:, i], XN[:, i], lngbc[:], ALU.mult)))
                dve.tensor_tensor(XN[:, i], XN[:, i], lnbbc[:], ALU.add).then_inc(S["norm_ready"], 1)

            for i in range(NT):
                ready(dve, "wo", i)
                dve.tensor_tensor(XN[:, i], bank("wo", i)[0:P, :], XN[:, i], ALU.add).then_inc(TV, 1)
                dve.wait_ge(TV, U.taken("wo", i + 1)[0])
                moments(i, XN[:, i])
                if i:
                    post_norm(i - 1)
            post_norm(NT - 1)
            transposed("ht", XNT)

            def over_experts(v, n):
                return v.rearrange("p (t a) -> p t a", a=1).to_broadcast([P, NT, n])

            def first_hot(hot, src, top, n):
                own(did(dve.tensor_reduce(top, src, AX, ALU.max)))
                own(did(dve.tensor_tensor(hot, src, over_experts(top, n), ALU.is_equal)))
                order = idx8[:, 0:n].rearrange("p (a e) -> p a e", a=1).to_broadcast([P, NT, n])
                own(did(dve.tensor_tensor(hot, hot, order, ALU.mult)))
                own(did(dve.tensor_reduce(gs[:, 3], hot, AX, ALU.max)))
                ins = dve.tensor_tensor(hot, hot, over_experts(gs[:, 3], n), ALU.is_equal)
                return ins

            def probabilities(name, bias, n, time):
                g = ga[:, :, 0:n]
                ready(dve, name, 0)
                dve.tensor_tensor(g, bank(name, 0)[0:P, 0:NT * n].rearrange("p (t e) -> p t e", e=n),
                                  bias[:].rearrange("p (a e) -> p a e", a=1).to_broadcast([P, NT, n]), ALU.add).then_inc(TV, 1)
                dve.wait_ge(TV, U.taken(name, 1)[0])
                own(did(dve.tensor_reduce(gs[:, 0], g, AX, ALU.max)))
                dve.tensor_tensor(g, g, over_experts(gs[:, 0], n), ALU.subtract).then_inc(S["gate_max"], 1)
                dve.wait_ge(S["gate_exp"], time)
                own(did(dve.tensor_reduce(gs[:, 1], g, AX, ALU.add)))
                own(did(dve.reciprocal(gs[:, 2], gs[:, 1])))
                own(did(dve.tensor_tensor(g, g, over_experts(gs[:, 2], n), ALU.mult)))

            dve.wait_ge(S["gate_in"], 32)
            probabilities("gate", gbias, EXPERTS, 1)
            first_hot(gb[:], ga[:], gs[:, 0], EXPERTS).then_inc(S["gates_ready"], 1)
            ready(dve, "gate", 2)
            own(did(dve.tensor_copy(inall[:], bank("gate", 2)[0:P, 0:NT * EXPERTS].rearrange("p (t e) -> p t e", e=EXPERTS))))
            own(did(dve.memset(before[:, 0], 0.0)))
            for i in range(1, NT):
                own(did(dve.tensor_tensor(before[:, i], before[:, i - 1], inall[:, i - 1], ALU.add)))
            own(did(dve.tensor_tensor(count[:], before[:, NT - 1], inall[:, NT - 1], ALU.add)))
            own(did(dve.tensor_scalar(counti[:], count[:], 127.0, None, ALU.add)))
            own(did(dve.tensor_scalar(table[:, 0:EXPERTS], counti[:], 7, None, ALU.arith_shift_right)))
            did(dve.memset(startf[:, 0:1], 0.0))
            own(did(dve.tensor_copy(tilesf[:], table[:, 0:EXPERTS])))
            for e in range(1, EXPERTS):
                own(did(dve.tensor_tensor(startf[:, e:e + 1], startf[:, e - 1:e], tilesf[:, e - 1:e], ALU.add)))
            did(dve.tensor_tensor(table[:, 2 * EXPERTS:2 * EXPERTS + 1], startf[:, EXPERTS - 1:EXPERTS], tilesf[:, EXPERTS - 1:EXPERTS], ALU.add))
            did(dve.tensor_scalar(start128[:], startf[:], 128.0, None, ALU.mult))
            dve.tensor_copy(table[:, EXPERTS:2 * EXPERTS], startf[:]).then_inc(S["table_ready"], 1)
            dve.wait_ge(S["table_ready"], 1)
            own(did(dve.tensor_tensor(before[:], before[:], start128[:].rearrange("p (a e) -> p a e", a=1).to_broadcast([P, NT, EXPERTS]), ALU.add)))
            dve.tensor_tensor(before[:], bank("gate", 1)[0:P, 0:NT * EXPERTS].rearrange("p (t e) -> p t e", e=EXPERTS), before[:], ALU.add).then_inc(TV, 1)
            dve.wait_ge(TV, U.taken("gate", 2)[0])
            dve.tensor_tensor(before[:], before[:], gb[:], ALU.mult).then_inc(TV, 1)
            dve.wait_ge(TV, U.taken("gate", 3)[0])
            own(did(dve.tensor_reduce(slotf[:], before[:], AX, ALU.add)))
            dve.tensor_copy(sloti[:], slotf[:]).then_inc(S["slots_ready"], 1)
            for s in range(2):
                dve.tensor_copy(b1c[:, s], b1e[:, s]).then_inc(S["expert_done"], 1)
            dve.tensor_copy(startf[:], tilesf[:]).then_inc(S["y_taken"], 1)
            for i in range(0, ST, 2):
                ready(dve, "rows", i)
                dve.tensor_copy(rowsT[:, :, i * 128:(i + 1) * 128], bank("rows", i).rearrange("p (k n) -> p k n", k=KD)).then_inc(TV, 1)
            with dve.Fori(0, EXPERTS // 2) as e2:
                for s in range(2):
                    n = dve.value_load(table[0:1, bass.ds(e2 * 2 + s, 1)], min_val=0, max_val=MOST)
                    start = dve.value_load(table[0:1, bass.ds(e2 * 2 + (s + EXPERTS), 1)], min_val=0, max_val=ST)

                    def tile(m):
                        i = nc.s_assert_within(start + m, 0, ST - 1, skip_runtime_bounds_check_because="the experts' tiles add up to at most ST")
                        dve.wait_ge(S["rows_stored"], i * 16 + 16)
                        dve.wait_ge(S[f"w2e_in{s}"], e2 * 32 + 32)
                        dve.wait_ge(S["y_ready"], i + 1)
                        dve.tensor_tensor(outrow[:], PS[:, 6, :], b2s[:, s], ALU.add).then_inc(S["y_taken"], 1)

                    up_to(dve, n, MOST, tile)
                    dve.wait_ge(S[f"w1e_in{s}"], e2 * 16 + 16)
                    dve.wait_ge(S[f"w2e_in{s}"], e2 * 32 + 32)
                    dve.tensor_scalar(b1c[:, s:s + 1], b1e[:, bass.ds(e2 * 2 + (s + 2), 1)], 1.0, None, ALU.mult).then_inc(S["expert_done"], 1)
            last = dve.value_load(table[0:1, 2 * EXPERTS:2 * EXPERTS + 1], min_val=1, max_val=ST)
            dve.wait_ge(S["rows_stored"], last * 16 + 16)
            dve.tensor_scalar(topw[:], gs[:, 0], 1.0, None, ALU.mult).then_inc(S["rows_out_ready"], 1)
            dve.wait_ge(S["rows_out_ready"], 1)
            dve.wait_ge(S["rows_back"], 16 * NT)
            for i in range(NT):
                own(did(dve.scalar_tensor_tensor(out=X[:, i], in0=back[:, i], scalar=topw[:, i:i + 1], in1=X[:, i], op0=ALU.mult, op1=ALU.add)))
            taken(dve, "xt2", 0)
            for i in range(NT):
                moments(i, X[:, i])
            inverse(3)
            for i in range(NT):
                normalized(i, XN3[:, i], X[:, i]).then_inc(S["norm_ready"], 1)
            transposed("xt2", XNT3)
            for i in range(NT):
                dve.wait_ge(S["split_hi"], NT + i + 1)
                dve.tensor_tensor(HL[:, i], XN3[:, i], HH[:, i].bitcast(F32), ALU.subtract).then_inc(S["split_lo"], 1)
            dve.wait_ge(S["gate2_in"], 32)
            probabilities("gate2", gbias2, SAGE, 2)
            p, w4, hot = ga[:, :, 0:SAGE], wexp[:, :, 0:SAGE], gb[:, :, 0:SAGE]
            own(did(first_hot(w4, p, gs[:, 0], SAGE)))
            own(did(dve.scalar_tensor_tensor(out=gc[:], in0=w4, scalar=-2.0, in1=p, op0=ALU.mult, op1=ALU.add)))
            own(did(first_hot(hot, gc[:], gs[:, 1], SAGE)))
            own(did(dve.tensor_tensor(w4, w4, hot, ALU.add)))
            dve.tensor_tensor(w4, w4, p, ALU.mult).then_inc(S["gates_ready"], 1)
            dve.wait_ge(S["gates_ready"], 2)
            dve.wait_ge(S["unspilled"], 16)
            for i in range(NT):
                blk = AT[:, i, i * P:(i + 1) * P]
                ins = dve.tensor_tensor(blk, blk.bitcast(F32), ident[0:P, 0:P], ALU.subtract)
            ins.then_inc(S["adj_ready"], 1)
            for k in range(3):
                ready(dve, "degree2", k)
                r = rowbc3[:, k * DCH:(k + 1) * DCH]
                deg = bank("degree2", k)[:, 0:DCH]
                own(did(dve.tensor_scalar(r, deg, 1.0, None, ALU.max)))
                own(did(dve.reciprocal(r, r)))
                dve.scalar_tensor_tensor(out=r, in0=deg, scalar=1.0, in1=r, op0=ALU.min, op1=ALU.mult).then_inc(TV, 1)
            taken(dve, "agg3", 0)
            for k in range(12):
                c, f = k // KD, k % KD
                lo, w = CHUNKS[c]
                ready(dve, "agg3", k)
                dve.tensor_tensor(agg0[:, f, lo:lo + w], bank("agg3", k)[:, 0:w], rowbc3[:, lo:lo + w], ALU.mult).then_inc(TV, 1)
            with dve.Fori(0, SAGE) as e:
                dve.wait_ge(S["sl_in0"], e * 48 + 48)

                def low_part(i):
                    dve.wait_ge(S["relu_done"], e * NT + (i + 1))
                    dve.scalar_tensor_tensor(out=HL[:, i], in0=bank("sage", i)[0:P, :], scalar=0.0,
                                             in1=HH[:, i].bitcast(F32), op0=ALU.max, op1=ALU.subtract).then_inc(TV, 1)

                for i in range(NT):
                    ready(dve, "sage", i, e)
                    dve.tensor_tensor(bank("sage", i)[0:P, :], bank("sage", i)[0:P, :], blbc[:, 0], ALU.add).then_inc(S["bias_added"], 1)
                    if i:
                        low_part(i - 1)
                low_part(NT - 1)
                dve.wait_ge(S["sl_in1"], e * 48 + 48)
                for c in range(5):
                    for f in range(KD):
                        k = NT + 8 * c + f
                        ready(dve, "sage", k, e)
                        dve.tensor_tensor(aggc[:, f], bank("sage", k)[:, 0:250], rowbc3[:, c * 250:(c + 1) * 250], ALU.mult).then_inc(TV, 1)
                    for i in range(2):
                        k = NT + 8 * c + 6 + i
                        ready(dve, "sage", k, e)
                        dve.tensor_tensor(bank("sage", k)[0:P, :], bank("sage", k)[0:P, :], blbc[:, 1], ALU.add).then_inc(S["bias_added"], 1)
                    for i in range(2):
                        k, tt = NT + 8 * c + 6 + i, 2 * c + i
                        dve.wait_ge(S["relu2_done"], e * NT + (tt + 1))
                        dve.wait_ge(TV, U.taken("sage", 0, e)[0])
                        dve.scalar_tensor_tensor(out=X[:, tt], in0=bank("sage", k)[0:P, :], scalar=wexp[:, tt, bass.ds(e, 1)],
                                                 in1=X[:, tt], op0=ALU.mult, op1=ALU.add).then_inc(TV, 1)
            taken(dve, "xt3", 0)
            for i in range(NT):
                moments(i, X[:, i])
            inverse(4)
            for i in range(NT):
                normalized(i, XN4[:, i], X[:, i]).then_inc(S["norm_ready"], 1)
            transposed("xt3", XNT4)
            own(did(dve.memset(c03[:], 0.03)))
            taken(dve, "merge", 0)
            own(did(dve.tensor_reduce(ghm[:], ghs[:], AX, ALU.add)))
            own(did(dve.tensor_scalar(ghm[:], ghm[:], 1.0 / N, None, ALU.mult)))
            dve.tensor_copy(ghb[:], ghm[:].rearrange("p (k a) -> p k a", a=1).to_broadcast([128, KD, 128])).then_inc(S["ghm_ready"], 1)
            dve.wait_ge(S["merge_in"], 13 * 16)
            ready(dve, "merge", 0)
            dve.tensor_tensor(gbc[:], bank("merge", 0)[:, 0:EXPERTS], g2bbc[:], ALU.add).then_inc(TV, 1)
            ready(dve, "merge", 1)
            dve.tensor_scalar(gT[:], bank("merge", 1)[0:EXPERTS, 0:128], g2bcol[:], None, ALU.add).then_inc(TV, 1)
            ready(dve, "merge", 2)
            dve.tensor_tensor(m2bc[:], m2bc[:], bank("merge", 2)[0:P, :], ALU.add).then_inc(TV, 1)
            for k, v in ((3, mgbc), (4, mbbc)):
                ready(dve, "merge", k)
                dve.scalar_tensor_tensor(out=v[:], in0=v[:], scalar=1.0 - 0.03 * EXPERTS, in1=bank("merge", k)[0:P, :],
                                         op0=ALU.mult, op1=ALU.add).then_inc(TV, 1)
            dve.wait_ge(TV, U.taken("merge", 5)[0])
            own(did(dve.tensor_tensor(tvt[:], tvb1[:], gbc[:].rearrange("p (a e) -> p a e", a=1).to_broadcast([128, KM, EXPERTS]), ALU.mult)))
            own(did(dve.tensor_reduce(tvr[:], tvt[:], AX, ALU.add)))
            own(did(dve.tensor_tensor(m1b[:], m1b[:], tvr[:], ALU.add)))
            for n in range(2 * EXPERTS):
                e, m = n % EXPERTS, (W1m, W2m)[n // EXPERTS]
                dve.wait_ge(S[f"tv_in{n % 4}"], 16 * (n // 4 + 1))
                if n:
                    dve.wait_ge(S["tv_used"], n)
                flat = m[:].rearrange("p k n -> p (k n)")
                dve.scalar_tensor_tensor(out=flat, in0=tv[:, n % 4], scalar=gbc[:, e:e + 1], in1=flat, op0=ALU.mult, op1=ALU.add).then_inc(S["tv_used"], 1)

            def last_norm(i):
                inverse_of(i, 5)
                own(did(normalized(i, XN4[:, i], XN4[:, i])))
                own(did(dve.tensor_tensor(XN4[:, i], XN4[:, i], mgbc[:], ALU.mult)))
                dve.wait_ge(S["bias_in_x"], i + 1)
                dve.tensor_tensor(XN4[:, i], XN4[:, i], X[:, i], ALU.add).then_inc(S["tail_ready"], 1)

            for i in range(NT):
                ready(dve, "down", i)
                dve.wait_ge(S["bias_in_residual"], i + 1)
                dve.tensor_tensor(XN4[:, i], bank("down", i)[0:P, :], XN4[:, i], ALU.add).then_inc(TV, 1)
                dve.wait_ge(TV, U.taken("down", i + 1)[0])
                moments(i, XN4[:, i])
                if i:
                    last_norm(i - 1)
            last_norm(NT - 1)

        @block.tensor
        def _(pe):
            UR = S["unit_ready"]

            def free(name, k, i=0):
                if k == 0:
                    taken(pe, name, 0, i)
                elif k >= 8:
                    taken(pe, name, k - 7, i)

            def product(dst, lhs, rhs):
                for n, (a, b) in enumerate(zip(lhs, rhs)):
                    ins = pe.matmul(dst, a, b, start=(n == 0), stop=(n == len(lhs) - 1))
                return ins

            def transposes(name, src, wait, base):
                for i in range(NT):
                    pe.wait_ge(S[wait], base + i + 1)
                    free(name, i)
                    for k in range(KD):
                        ins = pe.transpose(bank(name, i)[:, k * P:(k + 1) * P], src[:, i, k * 128:(k + 1) * 128], ident[0:P, 0:P])
                    ins.then_inc(UR, 1)

            def blocks(m, lo, w):
                return [m[:, k, lo:lo + w] for k in range(m.shape[1])]

            def three(a, cols_a, b, cols_b):
                return ([x for m in (0, 1, 0) for x in blocks(a[m], *cols_a)],
                        [x for m in (0, 0, 1) for x in blocks(b[m], *cols_b)])

            pe.wait_ge(S["ident_done"], 9)
            pe.wait_ge(S["edges_ready"], 1)
            for k in range(2):
                for h in range(2):
                    ins = pe.transpose(bank("edges", k)[0:P, h * EROWS:(h + 1) * EROWS], edgef[:, k, h * P:(h + 1) * P], ident[0:EROWS, 0:EROWS])
                ins.then_inc(UR, 1)
            pe.wait_ge(S["edges_ready"], 2)
            pe.matmul(bank("edges", 2)[0:P, 0:(NT - 1) * GROUPS], ones[0:P, 0:P], aboves[:].rearrange("p j g -> p (j g)"), start=True, stop=True).then_inc(UR, 1)
            taken(pe, "edges", 3)

            def count(q, j, s, u):
                pe.wait_ge(S[f"counts_read{s}"], u[s] + 1)
                for c in range(GROUP):
                    pe.wait_ge(S["onehots_ready"], q * GROUP + (c + 2))
                    for r in range(PACKED):
                        ins = pe.matmul(PS[0:P, 2 * s + r // 4, (r % 4) * P:(r % 4 + 1) * P], ohs[:, c, r * P:(r + 1) * P], ohd[:, c],
                                        start=(c == 0 and r % 4 == 0), stop=(c == GROUP - 1 and r >= 3))
                    ins.then_inc(S["onehots_used"], 1)

            pairs(pe, count)
            pe.wait_ge(S["adj_ready"], 1)
            for k in range(3):
                product(bank("degree", k)[:, 0:DCH], [onesr[0:P, :]] * NT, [AT[:, s, k * DCH:(k + 1) * DCH] for s in range(NT)]).then_inc(UR, 1)
            for i in range(NT):
                ins = product(bank("degree", 3)[0:P, 2 * i:2 * i + 2], [AT[:, s, i * P:(i + 1) * P] for s in range(NT)], [onesr[0:P, 0:2]] * NT)
            ins.then_inc(UR, 1)

            def aggregate(name, k0, hi, lo_, c, cols, i=0):
                lo, w = cols
                for f in range(KD):
                    free(name, k0 + f, i)
                    lhs = [h[:, s, f * 128:(f + 1) * 128] for h in (hi, lo_) for s in range(NT)]
                    rhs = [AT[:, s, lo:lo + w] for _ in range(2) for s in range(NT)]
                    product(bank(name, k0 + f)[:, 0:w], lhs, rhs).then_inc(UR, 1)

            pe.wait_ge(S["split_lo"], NT)
            for c in range(3):
                aggregate("agg1", KD * c, XH, XL, c, CHUNKS[c])
            pe.wait_ge(S["w1_in"], 16)
            taken(pe, "agg1", 12)
            for c in range(5):
                for f in range(KF):
                    k = 18 * c + f
                    free("gcn", k)
                    product(bank("gcn", k)[:, 0:250], blocks(W1, f * 128, 128), blocks(aggT, 250 * c, 250)).then_inc(UR, 1)
                pe.wait_ge(S["w2_in"], 16)
                taken(pe, "gcn", 18 * c + KF)
                for i in range(2):
                    k = 18 * c + KF + i
                    product(bank("gcn", k)[0:P, :], blocks(zT, i * P, P), blocks(W2, 0, D)).then_inc(UR, 1)
            taken(pe, "gcn", U.size("gcn"))
            for i in range(NT):
                free("agg2", i)
                product(bank("agg2", i)[0:P, :], [AT[:, s, i * P:(i + 1) * P] for _ in range(2) for s in range(NT)],
                        [h[:, s, :] for h in (XH, XL) for s in range(NT)]).then_inc(UR, 1)
            transposes("xt1", XN, "norm_ready", NT)
            taken(pe, "xt1", NT)
            for n in range(24):
                f, c, m = (n % 12) // 3, n % 3, n // 12
                if n % 12 == 0:
                    pe.wait_ge(S["weights_lo"], m + 1)
                free("qkv", n)
                product(bank("qkv", n)[:, 0:CHUNKS[c][1]], *three((Wh[:, m], Wl[:, m]), (f * 128, 128), (XNTh, XNTl), CHUNKS[c])).then_inc(UR, 1)
            pe.wait_ge(S["weights_lo"], 3)
            for i in range(NT):
                free("qkv", 24 + i)
                product(bank("qkv", 24 + i)[0:P, :], *three((XNTh, XNTl), (i * P, P), (Wh[:, 2], Wl[:, 2]), (0, D))).then_inc(UR, 1)
            taken(pe, "qkv", U.size("qkv"))

            def scores(b, i):
                hh, tt = i // NT % 2, i % NT
                pe.wait_ge(S["staged_by_vector"], b * 4 + 2 * (i // NT + 1))
                pe.wait_ge(S["staged_by_scalar"], b * 6 + 3 * (i // NT + 1))
                for k, (lo, w) in enumerate(CHUNKS):
                    n = 3 * i + k
                    if n >= 4:
                        pe.wait_ge(S["exp_done"], b * 60 + (n - 3))
                    pe.matmul(PS[0:P, n % 4, 0:w], qs[:, hh, tt * P:(tt + 1) * P], ks[:, hh, lo:lo + w], start=True, stop=False)
                    pe.matmul(PS[0:P, n % 4, 0:w], qs[OWN[hh], hh, tt * P:(tt + 1) * P], kl[OWN[hh], lo:lo + w], start=False, stop=True).then_inc(S["scores_ready"], 1)

            def transpose_p(b, i):
                for k, (lo, w) in enumerate(CHUNKS):
                    pe.wait_ge(S["exp_done"], b * 60 + (3 * i + k + 1))
                    if i:
                        if k == 1:
                            pe.wait_ge(S["pt_by_scalar"], b * 20 + i)
                        else:
                            pe.wait_ge(S["pt_by_vector"], b * 40 + (2 * i - (1 if k == 0 else 0)))
                    for m in range(w // P):
                        ins = pe.transpose(PS[0:P, 4 + (3 * i + k) % 3, m * P:(m + 1) * P], Pr[:, i % 2, lo + m * P:lo + (m + 1) * P], ident[0:P, 0:P])
                    ins.then_inc(S["pt_ready"], 1)

            def values(b, i):
                hh = i // NT
                pe.wait_ge(S["pt_by_vector"], b * 40 + 2 * (i + 1))
                pe.wait_ge(S["pt_by_scalar"], b * 20 + (i + 1))
                if i:
                    pe.wait_ge(S["pv_taken"], b * 20 + i)
                for s in range(NT):
                    ins = pe.matmul(PS[0:P, 7, 64 * (i % 2):64 * (i % 2) + 64], PT[:, i % 2, s, :], V[:, s, bass.ds(b * 128 + hh * 64, 64)],
                                    start=(s == 0), stop=(s == NT - 1))
                ins.then_inc(S["pv_ready"], 1)

            def head_pair(b, last):
                for i in range(20):
                    if i < 19 or not last:
                        scores(b, i + 1)
                    transpose_p(b, i)
                    if i:
                        values(b, i - 1)
                values(b, 19)

            scores(0, 0)
            with pe.Fori(0, HEADS // 2 - 1) as b:
                head_pair(b, False)
            head_pair(HEADS // 2 - 1, True)
            pe.wait_ge(S["pv_taken"], HEADS * NT)
            pe.wait_ge(S["pt_by_scalar"], HEADS * NT)
            transposes("ot", O, "pv_taken", HEADS * NT - NT)
            taken(pe, "ot", NT)
            pe.wait_ge(S["wo_in"], 16)
            for i in range(NT):
                free("wo", i)
                product(bank("wo", i)[0:P, :], blocks(OT, i * P, P), blocks(Wq, 0, D)).then_inc(UR, 1)
            transposes("ht", XN, "norm_ready", 2 * NT)
            taken(pe, "gate", 0)
            pe.wait_ge(S["gate_in"], 32)
            for i in range(NT):
                ins = product(bank("gate", 0)[0:P, EXPERTS * i:EXPERTS * (i + 1)], blocks(XNT, i * P, P), blocks(gW, 0, EXPERTS))
            ins.then_inc(UR, 1)
            pe.wait_ge(S["gates_ready"], 1)
            for m, k in ((tri, 1), (ones, 2)):
                pe.matmul(bank("gate", k)[0:P, 0:NT * EXPERTS], m[0:P, 0:P], gb[:].rearrange("p t e -> p (t e)"), start=True, stop=True).then_inc(UR, 1)
            taken(pe, "gate", 3)
            pe.wait_ge(S["rows_loaded"], 16)
            for i in range(ST):
                free("rows", i)
                for k in range(KD):
                    ins = pe.transpose(bank("rows", i)[:, k * 128:(k + 1) * 128], rows_in[:, i, k * 128:(k + 1) * 128], ident[:])
                ins.then_inc(UR, 1)
            taken(pe, "rows", ST)
            pe.wait_ge(S["table_ready"], 1)
            with pe.Fori(0, EXPERTS // 2) as e2:
                for s in range(2):
                    n = pe.value_load(table[0:1, bass.ds(e2 * 2 + s, 1)], min_val=0, max_val=MOST)
                    start = pe.value_load(table[0:1, bass.ds(e2 * 2 + (s + EXPERTS), 1)], min_val=0, max_val=ST)

                    def tile(m):
                        i = nc.s_assert_within(start + m, 0, ST - 1, skip_runtime_bounds_check_because="the experts' tiles add up to at most ST")
                        pe.wait_ge(S[f"w1e_in{s}"], e2 * 16 + 16)
                        for f in range(KF):
                            if f >= 6:
                                pe.wait_ge(S["hid_done"], i * KF + (f - 5))
                            product(PS[:, f % 6, 0:128], [W1e[:, s, k, f * 128:(f + 1) * 128] for k in range(KD)],
                                    [rowsT[:, k, bass.ds(i * 128, 128)] for k in range(KD)]).then_inc(S["hid_ready"], 1)
                        pe.wait_ge(S["y_taken"], i + 1)
                        pe.wait_ge(S[f"w2e_in{s}"], e2 * 32 + 32)
                        for k in range(KF):
                            pe.wait_ge(S["hid_done"], i * KF + (k + 1))
                            ins = pe.matmul(PS[:, 6, :], hid[:, k], W2e[:, s, k, :], start=(k == 0), stop=(k == KF - 1))
                        ins.then_inc(S["y_ready"], 1)

                    up_to(pe, n, MOST, tile)
            transposes("xt2", XN3, "norm_ready", 3 * NT)
            taken(pe, "xt2", NT)
            pe.wait_ge(S["gate2_in"], 32)
            for i in range(NT):
                ins = product(bank("gate2", 0)[0:P, SAGE * i:SAGE * (i + 1)], blocks(XNT3, i * P, P), blocks(gW2, 0, SAGE))
            ins.then_inc(UR, 1)
            taken(pe, "degree2", 0)
            pe.wait_ge(S["adj_ready"], 2)
            for k in range(3):
                product(bank("degree2", k)[:, 0:DCH], [onesr[0:P, :]] * NT, [AT[:, s, k * DCH:(k + 1) * DCH] for s in range(NT)]).then_inc(UR, 1)
            pe.wait_ge(S["split_lo"], 2 * NT)
            for c in range(3):
                aggregate("agg3", KD * c, HH, HL, c, CHUNKS[c])
            with pe.Fori(0, SAGE) as e:
                taken(pe, "sage", 0, e)
                pe.wait_ge(S["sl_in0"], e * 48 + 48)
                for i in range(NT):
                    free("sage", i, e)
                    product(bank("sage", i)[0:P, :], blocks(agg0, i * P, P) + blocks(XNT3, i * P, P),
                            [Wsl[:, 0, k, :] for k in range(KD)] + [Wsr[:, 0, k, :] for k in range(KD)]).then_inc(UR, 1)
                taken(pe, "sage", NT, e)
                for c in range(5):
                    k0 = NT + 8 * c
                    aggregate("sage", k0, HH, HL, c, (250 * c, 250), e)
                    for i in range(2):
                        tt = 2 * c + i
                        free("sage", k0 + 4 + i, e)
                        for k in range(KD):
                            blk = slice(k * 128, (k + 1) * 128)
                            ins = product(bank("sage", k0 + 4 + i)[:, k * 126:(k + 1) * 126], [HH[:, tt, blk], HL[:, tt, blk]], [identr[0:P, 0:126]] * 2)
                        ins.then_inc(UR, 1)
                    if c == 0:
                        pe.wait_ge(S["sl_in1"], e * 48 + 48)
                    taken(pe, "sage", k0 + 6, e)
                    for i in range(2):
                        free("sage", k0 + 6 + i, e)
                        product(bank("sage", k0 + 6 + i)[0:P, :], blocks(aggc, i * P, P) + [hTc[:, k, i, 0:P] for k in range(KD)],
                                [Wsl[:, 1, k, :] for k in range(KD)] + [Wsr[:, 1, k, :] for k in range(KD)]).then_inc(UR, 1)
            transposes("xt3", XN4, "norm_ready", 4 * NT)
            taken(pe, "xt3", NT)
            pe.wait_ge(S["g1_in"], 32)
            for n in range(12):
                f, c = n // 3, n % 3
                free("gh", n)
                product(bank("gh", n)[:, 0:CHUNKS[c][1]], blocks(g1T, f * 128, 128), blocks(XNT4, *CHUNKS[c])).then_inc(UR, 1)
            taken(pe, "merge", 0)
            pe.wait_ge(S["merge_in"], 13 * 16)
            pe.wait_ge(S["ghm_ready"], 1)
            product(bank("merge", 0)[:, 0:EXPERTS], blocks(ghb, 0, 128), blocks(g2T, 0, EXPERTS)).then_inc(UR, 1)
            product(bank("merge", 1)[0:EXPERTS, 0:128], blocks(g2T, 0, EXPERTS), blocks(ghb, 0, 128)).then_inc(UR, 1)
            taken(pe, "merge", 2)
            pe.matmul(bank("merge", 2)[0:P, :], gT[:, 0:P], tvb2[:], start=True, stop=True).then_inc(UR, 1)
            for k, v in ((3, tvg), (4, tvb)):
                pe.matmul(bank("merge", k)[0:P, :], c03[:], v[:], start=True, stop=True).then_inc(UR, 1)
            taken(pe, "merge", 5)
            pe.wait_ge(S["tv_used"], EXPERTS)
            for n in range(6):
                f, c = n // 3, n % 3
                product(bank("up", n)[:, 0:CHUNKS[c][1]], blocks(W1m, f * 128, 128), blocks(XNT4, *CHUNKS[c])).then_inc(UR, 1)
            taken(pe, "up", 6)
            pe.wait_ge(S["tv_used"], 2 * EXPERTS)
            for i in range(NT):
                free("down", i)
                product(bank("down", i)[0:P, :], blocks(upT, i * P, P), blocks(W2m, 0, D)).then_inc(UR, 1)


_IN = ["x", "src", "dst", "L0_gnn_W1", "L0_gnn_b1", "L0_gnn_W2", "L0_gnn_b2", "L0_ffn_ln1_g", "L0_ffn_ln1_b",
       "L0_ffn_Wq", "L0_ffn_bq", "L0_ffn_Wk", "L0_ffn_bk", "L0_ffn_Wv", "L0_ffn_bv", "L0_ffn_Wo", "L0_ffn_bo",
       "L0_ffn_gate_W", "L0_ffn_gate_b", "L0_ffn_W1", "L0_ffn_b1", "L0_ffn_W2", "L0_ffn_b2", "L1_gnn_gate_W",
       "L1_gnn_gate_b", "L1_gnn_Wl", "L1_gnn_bl", "L1_gnn_Wr", "L1_ffn_gfc1_w", "L1_ffn_gfc1_b", "L1_ffn_gfc2_w",
       "L1_ffn_gfc2_b", "L1_ffn_W1", "L1_ffn_b1", "L1_ffn_W2", "L1_ffn_b2", "L1_ffn_ln_g", "L1_ffn_ln_b",
       "L1_ffn_tv_W1", "L1_ffn_tv_b1", "L1_ffn_tv_W2", "L1_ffn_tv_b2", "L1_ffn_tv_ln_g", "L1_ffn_tv_ln_b"]


def _laid_out(inputs):
    import numpy as np

    a = {k: np.asarray(inputs[k]) for k in _IN}
    for k in ("L0_gnn_b1", "L0_ffn_bq", "L0_ffn_bk", "L1_ffn_gfc1_b", "L1_ffn_b1"):
        a[k] = a[k].reshape(-1, 128).T
    a["L0_ffn_b1"] = a["L0_ffn_b1"].reshape(EXPERTS, KF, 128).transpose(2, 0, 1)
    a["L1_ffn_tv_b1"] = a["L1_ffn_tv_b1"].reshape(EXPERTS, KM, 128).transpose(2, 1, 0)
    for k in ("L1_ffn_gfc1_w", "L1_ffn_gfc2_w", "L1_ffn_W1", "L1_ffn_W2"):
        a[k] = a[k].T
    for k in ("L1_ffn_tv_W1", "L1_ffn_tv_W2"):
        a[k] = a[k].transpose(0, 2, 1)
    return {k: np.ascontiguousarray(v) for k, v in a.items()}


def build(nc, arrays):
    t = {k: nc.dram_tensor(f"in_{k}", v.shape, mybir.dt.from_np(v.dtype), kind="ExternalInput").ap() for k, v in arrays.items()}
    out = nc.dram_tensor("out_0", (N, D), F32, kind="ExternalOutput").ap()
    rows_x = nc.dram_tensor("rows_by_expert", (SLOT_ROWS, D), F32, kind="Internal").ap()
    rows_y = nc.dram_tensor("rows_out_by_expert", (SLOT_ROWS, D), F32, kind="Internal").ap()
    spill = nc.dram_tensor("adjacency_spill", (P, NT, NPAD), F32, kind="Internal").ap()
    program(nc, t, out, spill, rows_x, rows_y)


def kernel(**inputs):
    import concourse.bacc as _bacc
    from concourse.bass_utils import run_bass_kernel_spmd as _run

    arrays = _laid_out(inputs)
    nc = _bacc.Bacc("TRN2", target_bir_lowering=False, num_devices=1)
    build(nc, arrays)
    r = _run(nc, [{f"in_{k}": v for k, v in arrays.items()}], core_ids=[0])
    return r.results[0]["out_0"]
```

```python
from contextlib import ExitStack

import concourse.bass as bass
from concourse import mybir

F32 = mybir.dt.float32
F32R = mybir.dt.float32r
F16 = mybir.dt.float16
I32 = mybir.dt.int32
U32 = mybir.dt.uint32
ALU = mybir.AluOpType
ACT = mybir.ActivationFunctionType
AX = mybir.AxisListType.X

N = 1250
NE = 20000
P = 125
NT = N // P
D = 512
KD = D // 128
FF = 2048
KF = FF // 128
HEADS, HD = 8, 64
EXPERTS = 8
SAGE = 4
MF = 256
KM = MF // 128
EPS = 1e-5
CHUNKS = [(0, 500), (500, 500), (1000, 250)]
TILES_OF = [range(0, 4), range(4, 8), range(8, 10)]
HALF = N // 2
FIELD = 4096.0
GROUP = 8
GROUPS = NE // P // GROUP
EROWS = 80
PACKED = HALF // P
DCH = 418
NDC = 3
ST = (N - EXPERTS) // 128 + EXPERTS
SLOT_ROWS = ST * 128
THIRDS = [(0, 5), (5, 11), (11, ST)]
MOST = -(-N // 128)
NPAD = DCH * NDC


class UnitPlan:

    def __init__(self, phases):
        self.at, units, v, a = {}, 0, 0, 0
        for name, owners, times in phases:
            self.at[name] = (units, v, a, owners)
            units += len(owners) * times
            v += owners.count("V") * times
            a += owners.count("A") * times

    def ready(self, name, k, i=0):
        units, _, _, owners = self.at[name]
        return i * len(owners) + (units + k + 1)

    def taken(self, name, k, i=0):
        _, v, a, owners = self.at[name]
        return (i * owners.count("V") + (v + owners[:k].count("V")),
                i * owners.count("A") + (a + owners[:k].count("A")))

    def size(self, name):
        return len(self.at[name][3])


def program(nc, t, out, spill, rows_x, rows_y):
    U = UnitPlan([
        ("edges", "VVV", 1),
        ("degree", "AAA", 1),
        ("agg1", "V" * 12, 1),
        ("gcn", ("VA" * 8 + "VV") * 5, 1),
        ("agg2", "V" * NT, 1),
        ("xt1", "V" * NT, 1),
        ("qkv", "VA" * 12 + "V" * NT, 1),
        ("ot", "VA" * 5, 1),
        ("wo", "V" * NT, 1),
        ("ht", "VA" * 5, 1),
        ("gate", "VVV", 1),
        ("rows", "VA" * (ST // 2) + "V" * (ST % 2), 1),
        ("xt2", "VA" * 5, 1),
        ("gate2", "V", 1),
        ("degree2", "VVV", 1),
        ("agg3", "V" * 12, 1),
        ("sage", "V" * NT + "VVVVAVAVVV" * 5, SAGE),
        ("xt3", "VA" * 5, 1),
        ("gh", "A" * 12, 1),
        ("merge", "VVVVV", 1),
        ("up", "A" * 6, 1),
        ("down", "V" * NT, 1),
    ])

    ctx = ExitStack()
    with ctx:
        def sem(name):
            return ctx.enter_context(nc.semaphore(name))

        PS = ctx.enter_context(nc.psum_tensor("PS", [128, 8, 512], F32))

        BASE = 16512
        TOP = 229344

        def at(name, shape, dt, off):
            size = 2 if dt == F16 else 4
            for s in shape[1:]:
                size *= s
            assert BASE + off + size <= TOP, (name, BASE + off + size - TOP)
            return nc.alloc_sbuf_tensor_at(name, shape, dt, offset=BASE + off), off + (size + 31) // 32 * 32

        o = 0
        ident, o = at("ident", [128, 128], F32, o)
        identr, o = at("identr", [128, 128], F32R, o)
        onesr, o = at("onesr", [128, 128], F32R, o)
        eps, o = at("eps", [128, 1], F32, o)
        bnst, o = at("bnst", [P, NT, 6], F32, o)
        mv, o = at("mv", [P, NT, 2], F32, o)
        std, o = at("std", [P, NT], F32, o)
        rstd, o = at("rstd", [P, NT], F32, o)
        dcol, o = at("dcol", [P, NT], F32, o)
        l0b1, o = at("l0b1", [128, KF], F32, o)
        bq, o = at("bq", [128, KD], F32, o)
        bk, o = at("bk", [128, KD], F32, o)
        b1e, o = at("b1e", [128, EXPERTS + 2, KF], F32, o)
        b1c, o = at("b1c", [128, 2, KF], F32, o)
        bias_at = o
        tri, o = at("tri", [128, 128], F32, o)
        ones, o = at("ones", [128, 128], F32, o)
        before, o = at("before", [P, NT, EXPERTS], F32, o)
        inall, o = at("inall", [P, NT, EXPERTS], F32, o)
        count, o = at("count", [P, EXPERTS], F32, o)
        counti, o = at("counti", [P, EXPERTS], I32, o)
        tilesf, o = at("tilesf", [P, EXPERTS], F32, o)
        startf, o = at("startf", [P, EXPERTS], F32, o)
        start128, o = at("start128", [P, EXPERTS], F32, o)
        table, o = at("table", [P, 3 * EXPERTS], I32, o)
        slotf, o = at("slotf", [P, NT], F32, o)
        sloti, o = at("sloti", [P, NT], U32, o)
        topw, o = at("topw", [P, NT], F32, o)
        assert o - bias_at >= 4 * D
        gbc, o = at("gbc", [128, EXPERTS], F32, o)
        ga, o = at("ga", [P, NT, EXPERTS], F32, o)
        gc, o = at("gc", [P, NT, SAGE], F32, o)
        gb, o = at("gb", [P, NT, EXPERTS], F32, o)
        wexp, o = at("wexp", [P, NT, EXPERTS], F32, o)
        gs, o = at("gs", [P, 4, NT], F32, o)
        idx8, o = at("idx8", [P, EXPERTS], F32, o)
        assert o <= 7680, o
        X, o = at("X", [P, NT, D], F32, 7680)
        A0 = o
        AT, o = at("AT", [P, NT, NPAD], F32R, A0)
        f0 = o
        aggT, _ = at("aggT", [128, KD, N], F32, 7680)
        XS, _ = at("XS", [P, NT, D], F32, 7680)
        rowbc, o = at("rowbc", [128, NPAD], F32, f0)
        XH, oh = at("XH", [P, NT, D], F32R, o)
        XL, o2 = at("XL", [P, NT, D], F32R, oh)
        diag, _ = at("diag", [P, NT, P], F32, oh)
        e0 = o
        edgei, e0 = at("edgei", [EROWS, 2, 2 * P], I32, e0)
        edgef, e0 = at("edgef", [EROWS, 2, 2 * P], F32, e0)
        srcf, e0 = at("srcf", [P, NE // P], F32, e0)
        dstf, e0 = at("dstf", [P, NE // P], F32, e0)
        srcw, e0 = at("srcw", [P, NE // P], F32, e0)
        srcq, e0 = at("srcq", [P, NE // P], F32, e0)
        above, e0 = at("above", [P, NT - 1, NE // P], F32, e0)
        aboves, e0 = at("aboves", [P, NT - 1, GROUPS], F32, e0)
        within, e0 = at("within", [P, 2, NT - 1, GROUPS], F32, e0)
        spanf, e0 = at("spanf", [P, 2, GROUPS], F32, e0)
        span, e0 = at("span", [P, 2 * GROUPS], I32, e0)
        edge, e0 = at("edge", [P, 3, GROUP], F32, e0)
        iota, e0 = at("iota", [P, NPAD], F16, e0)
        iotaj, e0 = at("iotaj", [P, P], F16, e0)
        ohs, e0 = at("ohs", [P, GROUP, HALF], F16, e0)
        ohd, e0 = at("ohd", [P, GROUP, P], F16, e0)
        cnt, e0 = at("cnt", [P, 2, PACKED, P], F32, e0)
        assert e0 <= o2, (e0, o2)
        W1, o3 = at("W1", [128, KD, FF], F32, o2)
        ZF, _ = at("ZF", [P, NT, D], F32, o2)
        b2bc, _ = at("b2bc", [P, D], F32, o2 + 20480)
        W2, o4 = at("W2", [128, KF, D], F32, o3)
        x0, _ = at("x0", [P, NT, D], F32, o3)
        cnthi, _ = at("cnthi", [P, 2, PACKED, P], I32, o2)
        cntlo, _ = at("cntlo", [P, 2, PACKED, P], F32, o2 + 8384)
        cnthf, _ = at("cnthf", [P, 2, PACKED, P], F32, o2 + 16768)
        zT, o5 = at("zT", [128, KF, 250], F32, o4)
        zrow, _ = at("zrow", [128, D], F32, o4)
        zsq, _ = at("zsq", [P, 2, D], F32, o4)
        znr, _ = at("znr", [P, NT, 8], F32, o4 + 4096)
        XNT, o = at("XNT", [128, KD, N], F32, A0)
        O, o = at("O", [P, NT, D], F32, A0)
        XN, o = at("XN", [P, NT, D], F32, o)
        qT, oq = at("qT", [128, KD, N], F32, o)
        OT, _ = at("OT", [128, KD, N], F32, o)
        kT, o = at("kT", [128, KD, N], F32, oq)
        V, o = at("V", [P, NT, D], F32, o)
        Wq, o = at("Wq", [128, KD, D], F32, o)
        o += 2 * 8192
        XNTh, oh = at("XNTh", [128, KD, N], F32R, o)
        XNTl, _ = at("XNTl", [128, KD, N], F32R, A0)
        Wh, oh = at("Wh", [128, 3, KD, D], F32R, oh)
        Wl, _ = at("Wl", [128, 3, KD, D], F32R, o - 3 * 8192)
        Wf, _ = at("Wf", [128, 3, KD, D], F32, o - 3 * 8192)
        qs, o = at("qs", [128, 2, N], F32R, o)
        ks, o = at("ks", [128, 2, N], F32R, o)
        kl, o = at("kl", [128, N], F32R, o)
        Pr, o = at("Pr", [P, 2, N], F32, o)
        PT, o = at("PT", [P, 2, NT, P], F32, o)
        assert oh <= o
        bvbc, o = at("bvbc", [P, D], F32, o)
        bobc, o = at("bobc", [P, D], F32, o)
        lngbc, o = at("lngbc", [P, D], F32, o)
        lnbbc, o = at("lnbbc", [P, D], F32, o)
        smm, o = at("smm", [P, 2, 3], F32, o)
        smb, o = at("smb", [P, 2], F32, o)
        sms, o = at("sms", [P, 2, 3], F32, o)
        smr, o = at("smr", [P, 4], F32, o)
        rowsT, o = at("rowsT", [128, KD, SLOT_ROWS], F32, A0)
        outrow, o = at("outrow", [128, D], F32, o)
        b2s, o = at("b2s", [128, 2, D], F32, o)
        assert o <= A0 + 40960
        We, o = at("We", [128, 2, KD * FF + KF * D], F32, A0 + 40960)
        rows_in, _ = at("rows_in", [128, ST, D], F32, A0 + 40960 + 65536)
        hid, o = at("hid", [128, KF, 128], F32, o)
        W1e = We[:, :, 0:KD * FF].rearrange("p s (k n) -> p s k n", k=KD)
        W2e = We[:, :, KD * FF:].rearrange("p s (k n) -> p s k n", k=KF)
        gW, _ = at("gW", [128, KD, EXPERTS], F32, o)
        gbias, _ = at("gbias", [P, EXPERTS], F32, o + 128)
        back, _ = at("back", [P, NT, D], F32, f0)
        XNT3, o = at("XNT3", [128, KD, N], F32, f0)
        rowbc3, o = at("rowbc3", [128, NPAD], F32, o)
        agg0, o6 = at("agg0", [128, KD, N], F32, o)
        XN3, o = at("XN3", [P, NT, D], F32, o)
        o = max(o, o6)
        HH, o = at("HH", [P, NT, D], F32R, o)
        HL, o = at("HL", [P, NT, D], F32R, o)
        WL, _ = at("WL", [128, 2, KD, D], F32R, o)
        WLf, o = at("WLf", [128, 2, KD, D], F32, o)
        WR, _ = at("WR", [128, 2, KD, D], F32R, o)
        WRf, o = at("WRf", [128, 2, KD, D], F32, o)
        part, _ = at("part", [128, 2, 2, KD, P], F32R, o)
        aggh, o = at("aggh", [128, KD, 250], F32R, o)
        aggl, _ = at("aggl", [128, KD, 250], F32R, o)
        aggc, o = at("aggc", [128, KD, 250], F32, o)
        hTh, o = at("hTh", [128, 2, KD, 126], F32R, o)
        hTl, o = at("hTl", [128, KD, 126], F32R, o)
        bias, _ = at("bias", [P, D], F32, bias_at)
        gW2, _ = at("gW2", [128, KD, SAGE], F32, o - 4096)
        gbias2, _ = at("gbias2", [P, SAGE], F32, o - 4096 + 64)
        XNT4, o = at("XNT4", [128, KD, N], F32, A0)
        XN4, o = at("XN4", [P, NT, D], F32, o)
        g1T, o = at("g1T", [128, KD, D], F32, o)
        g1b, o = at("g1b", [128, KD], F32, o)
        g2T, o = at("g2T", [128, KD, EXPERTS], F32, o)
        g2bbc, o = at("g2bbc", [128, EXPERTS], F32, o)
        g2bcol, o = at("g2bcol", [EXPERTS, 1], F32, o)
        W1m, o = at("W1m", [128, KD, MF], F32, o)
        W2m, o = at("W2m", [128, KM, D], F32, o)
        tv, o = at("tv", [128, 4, 1024], F32, o)
        m1b, o = at("m1b", [128, KM], F32, o)
        tvb1, o = at("tvb1", [128, KM, EXPERTS], F32, o)
        tvt, o = at("tvt", [128, KM, EXPERTS], F32, o)
        tvr, o = at("tvr", [128, KM], F32, o)
        tvb2, o = at("tvb2", [EXPERTS, D], F32, o)
        tvg, o = at("tvg", [EXPERTS, D], F32, o)
        tvb, o = at("tvb", [EXPERTS, D], F32, o)
        m2bc, o = at("m2bc", [P, D], F32, o)
        mgbc, o = at("mgbc", [P, D], F32, o)
        mbbc, o = at("mbbc", [P, D], F32, o)
        c03, o = at("c03", [EXPERTS, P], F32, o)
        ghs, o = at("ghs", [128, KD, 3], F32, o)
        ghm, o = at("ghm", [128, KD], F32, o)
        ghb, o = at("ghb", [128, KD, 128], F32, o)
        gT, o = at("gT", [EXPERTS, 128], F32, o)
        upT, o = at("upT", [128, KM, N], F32, o)

        names = """unit_ready taken_by_vector taken_by_scalar vector_step edges_in x_in w1_in w2_in l0b_in xback_in qkvw_in
            attnb_in wo_in gate_in w1e_in0 w1e_in1 w2e_in0 w2e_in1 table_ready slots_ready rows_scattered rows_loaded0
            rows_loaded1 rows_loaded2 rows_stored rows_back0 rows_back1 hid_ready hid_done y_ready y_taken expert_done
            rows_zero rows_out_ready spilled unspilled gate2_in wl_in wr_in wl_hi wr_hi wl_lo wr_lo left_used part_hi
            part_lo part_used agg_hi agg_lo bias_in g1_in merge_in tv_in0 tv_in1 tv_in2 tv_in3 out_stored iota_done
            ident_done adj_zero onehots_used onehots_ready counts_read0 counts_read1 counts_added0 counts_added1
            high_ready low_ready fields_ready loops_ready edges_ready span_ready dcol_ready chunk_staged adj_ready
            moments_ready std_ready norm_ready split_hi split_lo h2_hi znorm_sq znorm_sum znorm_root x_ready
            staged_by_vector staged_by_scalar weights_hi weights_lo xt_hi scores_ready rowmax_ready exp_done pt_ready
            pt_by_vector pt_by_scalar pv_ready pv_taken gate_max gate_exp gates_ready bias_added relu_done relu2_done
            ghm_ready gate_bc bias_in_residual tail_ready bias_in_x std_of_tile2 std_of_tile5 const_ready tv_used
            resid_ready""".split()
        S = {n: sem(n) for n in names}

        def ready(eng, name, k, i=0):
            eng.wait_ge(S["unit_ready"], U.ready(name, k, i))

        def taken(eng, name, k, i=0):
            v, a = U.taken(name, k, i)
            for who, n in (("taken_by_vector", v), ("taken_by_scalar", a)):
                if not (isinstance(n, int) and n == 0):
                    eng.wait_ge(S[who], n)

        def bank(name, k):
            return PS[:, k % 8, :]

        STD_BEFORE = [0, 1, 2, 2, 3, 4]
        PARTS = [(tt, right) for g in (range(0, 4), range(4, 8), range(8, 10)) for right in range(2) for tt in g]

        def part_free(eng, u, e):
            if u >= 2:
                tt, right = PARTS[u - 2]
                if right:
                    ready(eng, "sage", tt, e)
                else:
                    eng.wait_ge(S["part_used"], e * NT + (tt + 1))


        def up_to(eng, n, most, body, sure=False):
            def step(m):
                if m == 2:
                    with eng.Fori(2, most) as m:
                        with eng.If(m < n):
                            body(m)
                    return
                body(m)
                with eng.If(n > m + 1):
                    step(m + 1)

            if sure:
                step(0)
            else:
                with eng.If(n > 0):
                    step(0)

        def pairs(eng, body, start_group=None):
            name = eng.engine.name
            done, uses = eng.alloc_register(f"pairs_{name}"), [eng.alloc_register(f"set_{s}_{name}") for s in range(2)]
            for r in [done] + uses:
                eng.reg_mov(r, 0)
            eng.wait_ge(S["span_ready"], 1)
            with eng.Fori(0, GROUPS // 2) as g2:
                for half in range(2):
                    g = g2 * 2 + half
                    n = eng.value_load(span[0:1, bass.ds(g, 1)], min_val=1, max_val=NT)
                    first = eng.value_load(span[0:1, bass.ds(g + GROUPS, 1)], min_val=0, max_val=NT - 1)
                    if start_group:
                        start_group(g, eng.snap(done))

                    def pair(m):
                        s = (half + m) % 2 if isinstance(m, int) else 0
                        j = nc.s_assert_within(first + m, 0, NT - 1, skip_runtime_bounds_check_because="a group's chunks lie between its first and last destination")
                        body(eng.snap(done), j, s, [eng.snap(v) for v in uses], isinstance(m, int) and m == 0)
                        eng.reg_add(done, done, 1)
                        eng.reg_add(uses[s], uses[s], 1)

                    up_to(eng, n, NT, pair, sure=True)

        block = ctx.enter_context(nc.Block())

        def bcast(v, n=P):
            return v.rearrange("(a d) -> a d", a=1).to_broadcast([n, v.shape[0]])

        def tiles(v):
            return v.rearrange("(t p) d -> p t d", p=P)

        def rows(v):
            return v.rearrange("(k p) n -> p k n", p=128)

        @block.sync
        def _(sp):
            sp.dma_start(edgei[:, 0], t["src"].rearrange("(r n) -> r n", r=EROWS)).then_inc(S["edges_in"], 16)
            sp.dma_start(edgei[:, 1], t["dst"].rearrange("(r n) -> r n", r=EROWS)).then_inc(S["edges_in"], 16)
            sp.dma_start(x0[:], tiles(t["x"])).then_inc(S["x_in"], 16)
            sp.dma_start(l0b1[:], t["L0_gnn_b1"]).then_inc(S["l0b_in"], 16)
            sp.dma_start(bq[:], t["L0_ffn_bq"]).then_inc(S["l0b_in"], 16)
            sp.dma_start(bk[:], t["L0_ffn_bk"]).then_inc(S["l0b_in"], 16)
            sp.dma_start(b1e[:, 0:EXPERTS], t["L0_ffn_b1"]).then_inc(S["l0b_in"], 16)
            sp.wait_ge(S["ident_done"], 9)
            sp.dma_start(rows_x.rearrange("(i p) d -> p i d", p=128),
                         zrow[:].rearrange("p (a d) -> p a d", a=1).to_broadcast([128, ST, D])).then_inc(S["rows_zero"], 16)
            sp.wait_ge(S["adj_ready"], 1)
            sp.dma_start(W1[:], rows(t["L0_gnn_W1"])).then_inc(S["w1_in"], 16)
            sp.wait_ge(S["norm_ready"], NT)
            sp.dma_start(W2[:], rows(t["L0_gnn_W2"])).then_inc(S["w2_in"], 16)
            ready(sp, "gcn", U.size("gcn") - 1)
            sp.dma_start(X[:], tiles(t["x"])).then_inc(S["xback_in"], 16)
            sp.dma_start(b2bc[:], bcast(t["L0_gnn_b2"])).then_inc(S["xback_in"], 16)
            sp.dma_start(spill, AT[:].bitcast(F32)).then_inc(S["spilled"], 16)
            ready(sp, "agg2", NT - 1)
            sp.wait_ge(S["x_ready"], NT)
            for m, v in enumerate(("L0_ffn_Wq", "L0_ffn_Wk", "L0_ffn_Wv")):
                sp.dma_start(Wf[:, m], rows(t[v])).then_inc(S["qkvw_in"], 16)
            for b, v in ((bvbc, "L0_ffn_bv"), (bobc, "L0_ffn_bo"), (lngbc, "L0_ffn_ln1_g"), (lnbbc, "L0_ffn_ln1_b")):
                sp.dma_start(b[:], bcast(t[v])).then_inc(S["attnb_in"], 16)
            ready(sp, "qkv", U.size("qkv") - 1)
            sp.dma_start(Wq[:], rows(t["L0_ffn_Wo"])).then_inc(S["wo_in"], 16)
            def expert_weights(e, s):
                w1 = t["L0_ffn_W1"][bass.ds(e, 1)].rearrange("a (k p) n -> p (a k) n", p=128)
                w2 = t["L0_ffn_W2"][bass.ds(e, 1)].rearrange("a (k p) n -> p (a k) n", p=128)
                sp.dma_start(W1e[:, s], w1).then_inc(S[f"w1e_in{s}"], 16)
                sp.dma_start(W2e[:, s], w2).then_inc(S[f"w2e_in{s}"], 16)
                sp.dma_start(b2s[:, s], t["L0_ffn_b2"][bass.ds(e, 1)].to_broadcast([128, D])).then_inc(S[f"w2e_in{s}"], 16)

            ready(sp, "wo", NT - 1)
            sp.dma_start(W1e[:, 0], rows(t["L0_ffn_W1"][0])).then_inc(S["w1e_in0"], 16)
            ready(sp, "ht", NT - 1)
            sp.wait_ge(S["norm_ready"], 3 * NT)
            sp.dma_start(gW[:], rows(t["L0_ffn_gate_W"])).then_inc(S["gate_in"], 16)
            sp.dma_start(gbias[:], bcast(t["L0_ffn_gate_b"])).then_inc(S["gate_in"], 16)
            sp.dma_start(W2e[:, 0], rows(t["L0_ffn_W2"][0])).then_inc(S["w2e_in0"], 16)
            sp.wait_ge(S["rows_scattered"], 16 * NT)
            for n, (a, b) in enumerate(THIRDS):
                sp.dma_start(rows_in[:, a:b], rows_x.rearrange("(i p) d -> p i d", p=128)[:, a:b]).then_inc(S[f"rows_loaded{n}"], 16)
            sp.dma_start(b2s[:, 0], bcast(t["L0_ffn_b2"][0], 128)).then_inc(S["w2e_in0"], 16)
            ready(sp, "rows", ST - 1)
            expert_weights(1, 1)
            with sp.Fori(1, EXPERTS // 2) as i:
                for s in range(2):
                    sp.wait_ge(S["expert_done"], i * 2 + (s + 1))
                    expert_weights(i * 2 + s, s)
            sp.wait_ge(S["expert_done"], EXPERTS + 2)
            for half in range(2):
                sp.wait_ge(S[f"rows_back{half}"], 16 * NT // 2)
            sp.dma_start(AT[:].bitcast(F32), spill).then_inc(S["unspilled"], 16)
            sp.dma_start(gW2[:], rows(t["L1_gnn_gate_W"])).then_inc(S["gate2_in"], 16)
            sp.dma_start(gbias2[:], bcast(t["L1_gnn_gate_b"])).then_inc(S["gate2_in"], 16)
            sp.wait_ge(S["gates_ready"], 2)

            def sage_load(dst, name, e, l, done):
                w = t[name][bass.ds(e, 1), l].rearrange("a (k p) n -> p (a k) n", p=128)
                sp.dma_start(dst[:, 1], w).then_inc(S[done], 16)

            def sage_bias(e, l):
                sp.dma_start(bias[:], t["L1_gnn_bl"][bass.ds(e, 1), l].to_broadcast([P, D])).then_inc(S["bias_in"], 16)

            def second_layer(e):
                sp.wait_ge(S["part_used"], e * NT + NT)
                sage_load(WLf, "L1_gnn_Wl", e, 1, "wl_in")
                ready(sp, "sage", NT - 1, e)
                sage_load(WRf, "L1_gnn_Wr", e, 1, "wr_in")
                sp.wait_ge(S["bias_added"], e * (2 * NT) + NT)
                sage_bias(e, 1)

            sage_load(WLf, "L1_gnn_Wl", 0, 0, "wl_in")
            sage_load(WRf, "L1_gnn_Wr", 0, 0, "wr_in")
            sage_bias(0, 0)
            with sp.Fori(0, SAGE - 1) as e:
                second_layer(e)
                sp.wait_ge(S["left_used"], e + 1)
                sage_load(WLf, "L1_gnn_Wl", e + 1, 0, "wl_in")
                ready(sp, "sage", U.size("sage") - 1, e)
                sage_load(WRf, "L1_gnn_Wr", e + 1, 0, "wr_in")
                sp.wait_ge(S["bias_added"], e * (2 * NT) + 2 * NT)
                sage_bias(e + 1, 0)
            second_layer(SAGE - 1)
            taken(sp, "xt3", 0)
            ready(sp, "sage", U.size("sage") - 1, SAGE - 1)
            sp.dma_start(g1T[:], rows(t["L1_ffn_gfc1_w"])).then_inc(S["g1_in"], 16)
            sp.dma_start(g1b[:], t["L1_ffn_gfc1_b"]).then_inc(S["g1_in"], 16)
            for dst, v in ((g2T, rows(t["L1_ffn_gfc2_w"])), (g2bbc, bcast(t["L1_ffn_gfc2_b"], 128)),
                           (g2bcol, t["L1_ffn_gfc2_b"].rearrange("(e a) -> e a", a=1)),
                           (W1m, rows(t["L1_ffn_W1"])), (W2m, rows(t["L1_ffn_W2"])), (m1b, t["L1_ffn_b1"]),
                           (tvb1, t["L1_ffn_tv_b1"]), (tvb2, t["L1_ffn_tv_b2"]), (tvg, t["L1_ffn_tv_ln_g"]),
                           (tvb, t["L1_ffn_tv_ln_b"]), (m2bc, bcast(t["L1_ffn_b2"])),
                           (mgbc, bcast(t["L1_ffn_ln_g"])), (mbbc, bcast(t["L1_ffn_ln_b"]))):
                sp.dma_start(dst[:], v).then_inc(S["merge_in"], 16)
            for n in range(2 * EXPERTS):
                e, second = n % EXPERTS, n // EXPERTS
                if n >= 4:
                    sp.wait_ge(S["tv_used"], n - 3)
                v = t["L1_ffn_tv_W2"][e] if second else t["L1_ffn_tv_W1"][e]
                k = KM if second else KD
                sp.dma_start(tv[:, n % 4].rearrange("p (k n) -> p k n", k=k), rows(v)).then_inc(S[f"tv_in{n % 4}"], 16)
            for i in range(NT):
                sp.wait_ge(S["tail_ready"], i + 1)
                sp.dma_start(tiles(out)[:, i], XN4[:, i]).then_inc(S["out_stored"], 16)
            sp.wait_ge(S["out_stored"], 16 * NT)

        @block.gpsimd
        def _(pool):
            pool.iota(iota[:], [[1, NPAD]], base=0, channel_multiplier=0, allow_small_or_imprecise_dtypes=True).then_inc(S["iota_done"], 1)
            pool.iota(idx8[:], [[-1, EXPERTS]], base=EXPERTS, channel_multiplier=0, allow_small_or_imprecise_dtypes=True).then_inc(S["iota_done"], 1)
            pool.memset(ident[:], 0.0).then_inc(S["ident_done"], 1)
            pool.memset(onesr[:].bitcast(F32), 1.0).then_inc(S["ident_done"], 1)
            pool.memset(eps[:], EPS).then_inc(S["ident_done"], 1)
            pool.memset(tri[:], 1.0).then_inc(S["ident_done"], 1)
            pool.memset(ones[:], 1.0).then_inc(S["ident_done"], 1)
            pool.memset(b1e[:, EXPERTS:EXPERTS + 2], 0.0).then_inc(S["ident_done"], 1)
            pool.memset(zrow[:], 0.0).then_inc(S["ident_done"], 1)
            pool.wait_ge(S["ident_done"], 7)
            pool.affine_select(out=tri[:], in_=tri[:], compare_op=ALU.is_gt, fill=0.0, base=0,
                               pattern=[[1, 128]], channel_multiplier=-1).then_inc(S["ident_done"], 1)
            pool.affine_select(out=ident[:], in_=ident[:], compare_op=ALU.not_equal, fill=1.0, base=0,
                               pattern=[[-1, 128]], channel_multiplier=1).then_inc(S["ident_done"], 1)
            pool.memset(AT[:].bitcast(F32), 0.0).then_inc(S["adj_zero"], 1)
            for s in range(2):
                pool.memset(cnt[:, s], 0.0).then_inc(S[f"counts_read{s}"], 1)
                pool.memset(cnthi[:, s], 0).then_inc(S[f"counts_added{s}"], 1)
            pool.wait_ge(S["adj_zero"], 1)
            pool.wait_ge(S["loops_ready"], 1)
            def fields(q, j, s, u, first):
                cols = bass.ds(j * P, P)
                for m in range(2):
                    pool.wait_ge(S[f"counts_added{m}"], u[m] + 1)
                pool.wait_ge(S["fields_ready"], q + 1)
                pool.tensor_tensor(cntlo[:, s], cnt[:, s], cntlo[:, s], ALU.add).then_inc(S["low_ready"], 1)
                pool.tensor_tensor(AT[:, PACKED:NT, cols], AT[:, PACKED:NT, cols].bitcast(F32), cnthf[:, s], ALU.add)
                pool.wait_ge(S["low_ready"], q + 1)
                pool.tensor_tensor(AT[:, 0:PACKED, cols], AT[:, 0:PACKED, cols].bitcast(F32), cntlo[:, s], ALU.add).then_inc(S[f"counts_added{s}"], 1)

            pairs(pool, fields)
            pool.memset(cnt[:, 0, 0, 0:1], 0.0).then_inc(S["adj_ready"], 1)
            pool.dma_start(rows_y.rearrange("(i p) d -> p i d", p=128),
                           zrow[:].rearrange("p (a d) -> p a d", a=1).to_broadcast([128, ST, D])).then_inc(S["rows_stored"], 16)
            pool.wait_ge(S["qkvw_in"], 48)
            for m in range(3):
                pool.wait_ge(S["weights_hi"], m + 1)
                pool.tensor_tensor(Wl[:, m], Wf[:, m], Wh[:, m].bitcast(F32), ALU.subtract).then_inc(S["weights_lo"], 1)
            pool.wait_ge(S["attnb_in"], 64)
            ready(pool, "xt1", NT - 1)
            for i in range(NT):
                pool.tensor_tensor(XN[:, i], XN[:, i], bobc[:], ALU.add).then_inc(S["resid_ready"], 1)
            pool.wait_ge(S["slots_ready"], 1)
            pool.wait_ge(S["norm_ready"], 3 * NT)
            pool.wait_ge(S["rows_zero"], 16)
            for i in range(NT):
                pool.indirect_dma_start(rows_x[:, :], bass.IndirectOffsetOnAxis(ap=sloti[:, i:i + 1], axis=0), XN[:, i], None).then_inc(S["rows_scattered"], 16)
            pool.wait_ge(S["table_ready"], 1)
            with pool.Fori(0, EXPERTS) as e:
                n = pool.value_load(table[0:1, bass.ds(e, 1)], min_val=0, max_val=MOST)
                start = pool.value_load(table[0:1, bass.ds(e + EXPERTS, 1)], min_val=0, max_val=ST)

                def tile(m):
                    i = nc.s_assert_within(start + m, 0, ST - 1, skip_runtime_bounds_check_because="the experts' tiles add up to at most ST")
                    pool.wait_ge(S["y_taken"], i + 2)
                    pool.dma_start(rows_y[bass.ds(i * 128, 128), :], outrow[:]).then_inc(S["rows_stored"], 16)

                up_to(pool, n, MOST, tile)
            pool.wait_ge(S["rows_out_ready"], 1)
            for i in range(NT):
                pool.indirect_dma_start(back[:, i], None, rows_y[:, :], bass.IndirectOffsetOnAxis(ap=sloti[:, i:i + 1], axis=0)).then_inc(S[f"rows_back{i // (NT // 2)}"], 16)
            with pool.Fori(0, SAGE) as e:
                for l in range(2):
                    pool.wait_ge(S["wr_hi"], e * 2 + (l + 1))
                    pool.tensor_tensor(WR[:, 1], WRf[:, 1], WR[:, 0].bitcast(F32), ALU.subtract).then_inc(S["wr_lo"], 1)
            taken(pool, "merge", 5)
            for i in range(NT):
                pool.tensor_tensor(XN4[:, i], XN4[:, i], m2bc[:], ALU.add).then_inc(S["bias_in_residual"], 1)
            for i in range(NT):
                pool.tensor_tensor(X[:, i], X[:, i], mbbc[:], ALU.add).then_inc(S["bias_in_x"], 1)

        OWN = [slice(0, HD), slice(HD, 2 * HD)]

        def pt_out_scalar(act, b, i):
            act.wait_ge(S["pt_ready"], b * 60 + (3 * i + 2))
            if i >= 2:
                act.wait_ge(S["pv_ready"], b * 20 + (i - 1))
            act.activation(PT[:, i % 2, 4:8, :], PS[0:P, 4 + (3 * i + 1) % 3, 0:500].rearrange("p (k n) -> p k n", n=P),
                           ACT.Copy).then_inc(S["pt_by_scalar"], 1)

        @block.scalar
        def _(act):
            TV, TA = S["taken_by_vector"], S["taken_by_scalar"]
            def root(k):
                act.wait_ge(S["moments_ready"], NT * (k + 1))
                if k:
                    act.wait_ge(S["std_ready"], STD_BEFORE[k])
                act.activation(std[:], mv[:, :, 1], ACT.Sqrt, bias=eps[0:P, :]).then_inc(S["std_ready"], 1)

            def roots(k):
                act.wait_ge(S["std_ready"], STD_BEFORE[k])
                for i in range(NT):
                    act.wait_ge(S["moments_ready"], NT * k + i + 1)
                    act.activation(std[:, i:i + 1], mv[:, i, 1:2], ACT.Sqrt, bias=eps[0:P, :]).then_inc(S[f"std_of_tile{k}"], 1)

            act.wait_ge(S["ident_done"], 9)
            act.wait_ge(S["adj_zero"], 1)
            for i in range(NT):
                ins = act.activation(AT[:, i, i * P:(i + 1) * P], ident[0:P, 0:P], ACT.Copy)
            ins.then_inc(S["loops_ready"], 1)
            def counts(q, j, s, u, first):
                act.wait_ge(S["onehots_used"], q * GROUP + 2 * GROUP)
                act.wait_ge(S[f"counts_added{s}"], u[s] + 1)
                for dst, scale, done in ((cnthi, 1.0 / FIELD, "high_ready"), (cnt, 1.0, f"counts_read{s}")):
                    act.activation(dst[:, s, 0:4], PS[0:P, 2 * s, 0:4 * P].rearrange("p (k n) -> p k n", n=P), ACT.Copy, scale=scale)
                    act.activation(dst[:, s, 4], PS[0:P, 2 * s + 1, 0:P], ACT.Copy, scale=scale).then_inc(S[done], 1)
                act.wait_ge(S["high_ready"], q + 1)
                act.activation(cnthf[:, s], cnthi[:, s], ACT.Copy)
                act.activation(cntlo[:, s], cnthi[:, s], ACT.Copy, scale=-FIELD).then_inc(S["fields_ready"], 1)

            pairs(act, counts)
            for k in range(3):
                ready(act, "degree", k)
                act.activation(rowbc[:, k * DCH:(k + 1) * DCH], bank("degree", k)[:, 0:DCH], ACT.Sqrt).then_inc(TA, 1)
            root(0)
            act.wait_ge(S["dcol_ready"], 1)
            for i in range(NT):
                act.wait_ge(S["norm_ready"], i + 1)
                act.activation(XH[:, i], XS[:, i], ACT.Copy, scale=dcol[:, i:i + 1]).then_inc(S["split_hi"], 1)
            act.wait_ge(S["rows_zero"], 16)
            act.wait_ge(S["rows_stored"], 16)
            act.wait_ge(S["l0b_in"], 64)
            for c in range(5):
                for f in range(1, KF, 2):
                    k = 18 * c + f
                    ready(act, "gcn", k)
                    act.activation(zT[:, f], bank("gcn", k)[:, 0:250], ACT.Relu, bias=l0b1[:, f:f + 1]).then_inc(TA, 1)
                for i in range(2):
                    k, tt = 18 * c + KF + i, 2 * c + i
                    ready(act, "gcn", k)
                    act.activation(XH[:, tt], bank("gcn", k)[0:P, :], ACT.Copy, scale=dcol[:, tt:tt + 1]).then_inc(S["h2_hi"], 1)
            for i in range(NT):
                taken(act, "agg2", i + 1)
                act.activation(zsq[:, i % 2], ZF[:, i], ACT.Square).then_inc(S["znorm_sq"], 1)
                act.wait_ge(S["znorm_sum"], i + 1)
                act.activation(znr[:, i], znr[:, i], ACT.Sqrt).then_inc(S["znorm_root"], 1)
            root(1)
            act.wait_ge(S["qkvw_in"], 48)
            for m in range(3):
                act.activation(Wh[:, m], Wf[:, m], ACT.Copy).then_inc(S["weights_hi"], 1)
            for i in range(NT):
                ready(act, "xt1", i)
                act.activation(XNTh[:, :, i * P:(i + 1) * P], bank("xt1", i)[:, 0:KD * P].rearrange("p (k n) -> p k n", k=KD),
                               ACT.Copy).then_inc(S["xt_hi"], 1)

            def transposed(name, dst, stride=P):
                for i in range(1, NT, 2):
                    ready(act, name, i)
                    act.activation(dst[:, :, i * P:(i + 1) * P], bank(name, i)[:, 0:KD * P].rearrange("p (k n) -> p k n", k=KD),
                                   ACT.Copy).then_inc(TA, 1)

            for n in range(1, 24, 2):
                f, c = (n % 12) // 3, n % 3
                lo, w = CHUNKS[c]
                ready(act, "qkv", n)
                if n < 12:
                    act.wait_ge(S["const_ready"], 1)
                    act.activation(qT[:, f, lo:lo + w], bank("qkv", n)[:, 0:w], ACT.Identity, bias=bq[:, f:f + 1], scale=-0.125).then_inc(TA, 1)
                else:
                    act.activation(kT[:, f, lo:lo + w], bank("qkv", n)[:, 0:w], ACT.Identity, bias=bk[:, f:f + 1]).then_inc(TA, 1)
            taken(act, "qkv", U.size("qkv"))

            def upper_bits(b, hh, m):
                src, dst = ((qT, qs[OWN[hh], hh:hh + 1]), (kT, ks[OWN[hh], hh:hh + 1]), (kT, ks[OWN[1 - hh], hh:hh + 1]))[m]
                act.activation(dst, src[OWN[hh], bass.ds(b, 1)], ACT.Copy).then_inc(S["staged_by_scalar"], 1)

            def exponentials(b, i):
                act.wait_ge(S["rowmax_ready"], b * 20 + (i + 1))
                if i >= 2:
                    act.wait_ge(S["pt_ready"], b * 60 + 3 * (i - 1))
                for k, (lo, w) in enumerate(CHUNKS):
                    act.activation(Pr[:, i % 2, lo:lo + w], PS[0:P, (3 * i + k) % 4, 0:w], ACT.Exp, bias=smb[:, i % 2:i % 2 + 1],
                                   scale=-1.0, accum_out=sms[:, i % 2, k:k + 1]).then_inc(S["exp_done"], 1)

            def head_pair(b, last):
                for i in range(20):
                    if i < 19 or not last:
                        exponentials(b, i + 1)
                    pt_out_scalar(act, b, i)
                    if i in (1, 3, 5):
                        upper_bits(b, 1, i // 2)
                    if i in (11, 13, 15) and not last:
                        upper_bits(b + 1, 0, i // 2 - 5)

            for m in range(3):
                upper_bits(0, 0, m)
            exponentials(0, 0)
            with act.Fori(0, HEADS // 2 - 1) as b:
                head_pair(b, False)
            head_pair(HEADS // 2 - 1, True)
            transposed("ot", OT)
            roots(2)
            transposed("ht", XNT)
            act.wait_ge(S["gate_max"], 1)
            act.activation(ga[:], ga[:], ACT.Exp).then_inc(S["gate_exp"], 1)
            for i in range(1, ST, 2):
                ready(act, "rows", i)
                act.activation(rowsT[:, :, i * 128:(i + 1) * 128], bank("rows", i).rearrange("p (k n) -> p k n", k=KD), ACT.Copy).then_inc(TA, 1)
            act.wait_ge(S["table_ready"], 1)
            with act.Fori(0, EXPERTS // 2) as e2:
                for s in range(2):
                    n = act.value_load(table[0:1, bass.ds(e2 * 2 + s, 1)], min_val=0, max_val=MOST)
                    start = act.value_load(table[0:1, bass.ds(e2 * 2 + (s + EXPERTS), 1)], min_val=0, max_val=ST)

                    def tile(m):
                        act.wait_ge(S["expert_done"], e2 * 2 + (s + 1))
                        i = nc.s_assert_within(start + m, 0, ST - 1, skip_runtime_bounds_check_because="the experts' tiles add up to at most ST")
                        for f in range(KF):
                            act.wait_ge(S["hid_ready"], i * KF + (f + 1))
                            act.activation(hid[:, f], PS[:, f % 6, 0:128], ACT.Gelu_apprx_tanh, bias=b1c[:, s, f:f + 1]).then_inc(S["hid_done"], 1)

                    up_to(act, n, MOST, tile)
            root(3)
            transposed("xt2", XNT3)
            for i in range(NT):
                act.wait_ge(S["norm_ready"], 3 * NT + i + 1)
                act.activation(HH[:, i], XN3[:, i], ACT.Copy).then_inc(S["split_hi"], 1)
            act.wait_ge(S["gate_max"], 2)
            act.activation(ga[:, :, 0:SAGE], ga[:, :, 0:SAGE], ACT.Exp).then_inc(S["gate_exp"], 1)
            taken(act, "sage", 0)
            with act.Fori(0, SAGE) as e:
                def upper(w, side, l):
                    act.wait_ge(S[side + "_in"], e * 32 + 16 * (l + 1))
                    act.activation(w[:, 0], w_landed[side][:, 1], ACT.Copy).then_inc(S[side + "_hi"], 1)

                w_landed = {"wl": WLf, "wr": WRf}
                upper(WL, "wl", 0)
                for u in range(len(PARTS) + 3):
                    if u < len(PARTS):
                        tt, right = PARTS[u]
                        if u == 3:
                            upper(WR, "wr", 0)
                        part_free(act, u, e)
                        act.activation(part[:, u % 2, 0], (agg0, XNT3)[right][:, :, tt * P:(tt + 1) * P], ACT.Copy).then_inc(S["part_hi"], 1)
                    if u >= 3 and PARTS[u - 3][1]:
                        i = PARTS[u - 3][0]
                        act.wait_ge(S["bias_added"], e * (2 * NT) + (i + 1))
                        act.activation(HH[:, i], bank("sage", i)[0:P, :], ACT.Relu).then_inc(S["relu_done"], 1)
                upper(WL, "wl", 1)
                for c in range(5):
                    k0 = NT + 10 * c
                    for f in range(KD):
                        act.wait_ge(TV, U.taken("sage", k0 + f + 1, e)[0])
                        act.activation(aggh[:, f], aggc[:, f], ACT.Copy).then_inc(S["agg_hi"], 1)
                    for i in range(2):
                        ready(act, "sage", k0 + 4 + 2 * i, e)
                        act.activation(hTh[:, i], bank("sage", k0 + 4 + 2 * i)[:, 0:KD * 126].rearrange("p (k n) -> p k n", k=KD), ACT.Copy).then_inc(TA, 1)
                    if c == 0:
                        upper(WR, "wr", 1)
                    for i in range(2):
                        k, tt = k0 + 7 + 2 * i, 2 * c + i
                        act.wait_ge(S["bias_added"], e * (2 * NT) + (NT + tt + 1))
                        act.activation(bank("sage", k)[0:P, :], bank("sage", k)[0:P, :], ACT.Relu).then_inc(S["relu2_done"], 1)
            root(4)
            transposed("xt3", XNT4)
            act.wait_ge(S["g1_in"], 32)
            for n in range(12):
                f, c = n // 3, n % 3
                ready(act, "gh", n)
                w = CHUNKS[c][1]
                act.activation(bank("gh", n)[:, 0:w], bank("gh", n)[:, 0:w], ACT.Relu, bias=g1b[:, f:f + 1],
                               accum_out=ghs[:, f, c:c + 1]).then_inc(TA, 1)
            act.wait_ge(S["tv_used"], EXPERTS)
            for n in range(6):
                f, c = n // 3, n % 3
                lo, w = CHUNKS[c]
                ready(act, "up", n)
                act.activation(upT[:, f, lo:lo + w], bank("up", n)[:, 0:w], ACT.Relu, bias=m1b[:, f:f + 1]).then_inc(TA, 1)
            roots(5)

        @block.vector
        def _(dve):
            TV, TA = S["taken_by_vector"], S["taken_by_scalar"]
            steps = [0]

            def did(ins):
                ins.then_inc(S["vector_step"], 1)
                steps[0] += 1
                return steps[0]

            def own(n, extra=0):
                dve.wait_ge(S["vector_step"], extra + n)

            def moments(i, src):
                own(did(dve.bn_stats(bnst[:, i], src)))
                dve.bn_aggr(mv[:, i], bnst[:, i]).then_inc(S["moments_ready"], 1)

            def inverse(k):
                dve.wait_ge(S["std_ready"], STD_BEFORE[k] + 1)
                own(did(dve.reciprocal(rstd[:], std[:])))

            def inverse_of(i, k):
                dve.wait_ge(S[f"std_of_tile{k}"], i + 1)
                own(did(dve.reciprocal(rstd[:, i:i + 1], std[:, i:i + 1])))

            def normalized(i, dst, src):
                return dve.tensor_scalar(dst, src, mv[:, i, 0:1], rstd[:, i:i + 1], ALU.subtract, ALU.mult)

            dve.wait_ge(S["edges_in"], 32)
            dve.tensor_copy(edgef[:], edgei[:]).then_inc(S["edges_ready"], 1)
            for k, v in enumerate((srcf, dstf)):
                ready(dve, "edges", k)
                dve.tensor_copy(v[:].rearrange("p (r h) -> p h r", h=2), bank("edges", k)[0:P, 0:2 * EROWS].rearrange("p (h r) -> p h r", h=2)).then_inc(TV, 1)
            dve.wait_ge(TV, 2)
            for j in range(1, NT):
                n = did(dve.tensor_scalar(above[:, j - 1], dstf[:], float(j * P), None, ALU.is_ge))
            own(n)
            dve.tensor_reduce(aboves[:], above[:].rearrange("p j (g c) -> p j g c", c=GROUP), AX, ALU.add).then_inc(S["edges_ready"], 1)
            own(did(dve.tensor_scalar(srcq[:], srcf[:], float(HALF), None, ALU.is_ge)))
            did(dve.tensor_scalar(srcw[:], srcq[:], FIELD - 1.0, 1.0, ALU.mult, ALU.add))
            own(did(dve.scalar_tensor_tensor(out=srcf[:], in0=srcq[:], scalar=-float(HALF), in1=srcf[:], op0=ALU.mult, op1=ALU.add)))
            ready(dve, "edges", 2)
            cum = bank("edges", 2)[0:P, 0:(NT - 1) * GROUPS].rearrange("p (j g) -> p j g", g=GROUPS)
            did(dve.tensor_scalar(within[:, 0], cum, 1.0, None, ALU.is_ge))
            dve.tensor_scalar(within[:, 1], cum, float(GROUP * P), None, ALU.is_ge).then_inc(TV, 1)
            own(steps[0])
            dve.wait_ge(TV, 3)
            own(did(dve.tensor_reduce(spanf[:], within[:].rearrange("p a j g -> p a g j"), AX, ALU.add)))
            did(dve.tensor_copy(span[:, GROUPS:2 * GROUPS], spanf[:, 1]))
            own(did(dve.tensor_tensor(spanf[:, 0], spanf[:, 0], spanf[:, 1], ALU.subtract)))
            dve.tensor_scalar(span[:, 0:GROUPS], spanf[:, 0], 1.0, None, ALU.add).then_inc(S["span_ready"], 1)
            dve.wait_ge(S["iota_done"], 2)
            dve.memset(ohs[:, 0, 0:2], 0.0).then_inc(S["onehots_used"], GROUP)
            dve.memset(ohd[:, 0, 0:2], 0.0).then_inc(S["onehots_ready"], 1)
            def stage_edges(g, done):
                dve.wait_ge(S["onehots_ready"], done * GROUP + 1)
                for m, v in enumerate((srcf, srcw, dstf)):
                    dve.tensor_copy(edge[:, m], v[:, bass.ds(g * GROUP, GROUP)])

            def onehots(q, j, s, u, first):
                dve.wait_ge(S["onehots_ready"], q * GROUP + 1)
                dve.tensor_copy(iotaj[:], iota[:, bass.ds(j * P, P)]).then_inc(S["chunk_staged"], 1)
                dve.wait_ge(S["chunk_staged"], q + 1)
                for c in range(GROUP):
                    dve.wait_ge(S["onehots_used"], q * GROUP + (c + 1))
                    if first:
                        dve.tensor_scalar(ohs[:, c], iota[:, 0:HALF], edge[:, 0, c:c + 1], edge[:, 1, c:c + 1], ALU.is_equal, ALU.mult)
                    dve.tensor_scalar(ohd[:, c], iotaj[:], edge[:, 2, c:c + 1], None, ALU.is_equal).then_inc(S["onehots_ready"], 1)

            pairs(dve, onehots, stage_edges)
            dve.wait_ge(S["ident_done"], 9)
            own(did(dve.tensor_copy(identr[:], ident[:])))
            dve.wait_ge(S["x_in"], 16)
            for i in range(NT):
                moments(i, x0[:, i])
            inverse(0)
            for i in range(NT):
                normalized(i, XS[:, i], x0[:, i]).then_inc(S["norm_ready"], 1)
            taken(dve, "degree", 3)
            own(did(dve.tensor_tensor(diag[:], rowbc[0:P, 0:N].rearrange("p (t n) -> p t n", n=P),
                                      ident[0:P, 0:P].rearrange("p (a n) -> p a n", a=1).to_broadcast([P, NT, P]), ALU.mult)))
            own(did(dve.tensor_reduce(dcol[:], diag[:], AX, ALU.add)))
            dve.reciprocal(dcol[:], dcol[:]).then_inc(S["dcol_ready"], 1)
            for i in range(NT):
                dve.wait_ge(S["split_hi"], i + 1)
                dve.scalar_tensor_tensor(out=XL[:, i], in0=XS[:, i], scalar=dcol[:, i:i + 1], in1=XH[:, i].bitcast(F32),
                                         op0=ALU.mult, op1=ALU.subtract).then_inc(S["split_lo"], 1)
            own(did(dve.reciprocal(rowbc[:, 0:N], rowbc[:, 0:N])))
            for k in range(12):
                c, f = k // KD, k % KD
                lo, w = CHUNKS[c]
                ready(dve, "agg1", k)
                dve.tensor_tensor(aggT[:, f, lo:lo + w], bank("agg1", k)[:, 0:w], rowbc[:, lo:lo + w], ALU.mult).then_inc(TV, 1)
            dve.wait_ge(S["rows_zero"], 16)
            dve.wait_ge(S["rows_stored"], 16)
            dve.wait_ge(S["l0b_in"], 64)
            dve.tensor_scalar(bq[:], bq[:], -0.125, None, ALU.mult).then_inc(S["const_ready"], 1)
            for c in range(5):
                for f in range(0, KF, 2):
                    k = 18 * c + f
                    ready(dve, "gcn", k)
                    dve.tensor_scalar(zT[:, f], bank("gcn", k)[:, 0:250], l0b1[:, f:f + 1], 0.0, ALU.add, ALU.max).then_inc(TV, 1)
                for i in range(2):
                    k, tt = 18 * c + KF + i, 2 * c + i
                    dve.wait_ge(S["h2_hi"], tt + 1)
                    dve.scalar_tensor_tensor(out=XL[:, tt], in0=bank("gcn", k)[0:P, :], scalar=dcol[:, tt:tt + 1],
                                             in1=XH[:, tt].bitcast(F32), op0=ALU.mult, op1=ALU.subtract).then_inc(TV, 1)
            dve.wait_ge(S["xback_in"], 32)

            def groupsum(i):
                dve.wait_ge(S["znorm_sq"], i + 1)
                dve.tensor_reduce(znr[:, i], zsq[:, i % 2].rearrange("p (g d) -> p g d", g=8), AX, ALU.add).then_inc(S["znorm_sum"], 1)

            def groupnorm(i):
                dve.wait_ge(S["znorm_root"], i + 1)
                own(did(dve.tensor_scalar(znr[:, i], znr[:, i], 1e-12, None, ALU.max)))
                own(did(dve.reciprocal(znr[:, i], znr[:, i])))
                z = ZF[:, i].rearrange("p (g d) -> p g d", g=8)
                own(did(dve.tensor_tensor(z, z, znr[:, i].rearrange("p (g a) -> p g a", a=1).to_broadcast([P, 8, 64]), ALU.mult)))
                dve.tensor_tensor(X[:, i], X[:, i], ZF[:, i], ALU.add).then_inc(S["x_ready"], 1)
                dve.wait_ge(S["x_ready"], i + 1)
                moments(i, X[:, i])

            for i in range(NT):
                ready(dve, "agg2", i)
                dve.scalar_tensor_tensor(out=ZF[:, i], in0=bank("agg2", i)[0:P, :], scalar=dcol[:, i:i + 1],
                                         in1=b2bc[:], op0=ALU.mult, op1=ALU.add).then_inc(TV, 1)
                if i:
                    groupnorm(i - 1)
                groupsum(i)
            groupnorm(NT - 1)
            inverse(1)
            dve.wait_ge(S["spilled"], 16)
            for i in range(NT):
                normalized(i, XN[:, i], X[:, i]).then_inc(S["norm_ready"], 1)

            def transposed(name, dst):
                for i in range(0, NT, 2):
                    ready(dve, name, i)
                    dve.tensor_copy(dst[:, :, i * P:(i + 1) * P], bank(name, i)[:, 0:KD * P].rearrange("p (k n) -> p k n", k=KD)).then_inc(TV, 1)

            for i in range(NT):
                ready(dve, "xt1", i)
                dve.wait_ge(S["xt_hi"], i + 1)
                dve.tensor_tensor(XNTl[:, :, i * P:(i + 1) * P], bank("xt1", i)[:, 0:KD * P].rearrange("p (k n) -> p k n", k=KD),
                                  XNTh[:, :, i * P:(i + 1) * P].bitcast(F32), ALU.subtract).then_inc(TV, 1)
            dve.wait_ge(S["const_ready"], 1)
            for n in range(0, 24, 2):
                f, c = (n % 12) // 3, n % 3
                lo, w = CHUNKS[c]
                ready(dve, "qkv", n)
                if n < 12:
                    dve.tensor_scalar(qT[:, f, lo:lo + w], bank("qkv", n)[:, 0:w], -0.125, bq[:, f:f + 1], ALU.mult, ALU.add).then_inc(TV, 1)
                else:
                    dve.tensor_scalar(kT[:, f, lo:lo + w], bank("qkv", n)[:, 0:w], bk[:, f:f + 1], None, ALU.add).then_inc(TV, 1)
            dve.wait_ge(S["attnb_in"], 64)
            for i in range(NT):
                ready(dve, "qkv", 24 + i)
                dve.tensor_tensor(V[:, i], bank("qkv", 24 + i)[0:P, :], bvbc[:], ALU.add).then_inc(TV, 1)

            per = 60
            taken(dve, "qkv", U.size("qkv"))

            def lower_bits(b, hh, m):
                own_, other = OWN[hh], OWN[1 - hh]
                src, hi = ((qT, qs), (kT, ks))[m]
                dst = kl[own_] if m else qs[other, hh]
                dve.wait_ge(S["staged_by_scalar"], b * 6 + (3 * hh + m + 1))
                dve.tensor_tensor(dst, src[own_, bass.ds(b, 1)].rearrange("p a n -> p (a n)"), hi[own_, hh].bitcast(F32), ALU.subtract).then_inc(S["staged_by_vector"], 1)

            def rowmax(b, i):
                for k, (lo, w) in enumerate(CHUNKS):
                    dve.wait_ge(S["scores_ready"], b * 60 + (3 * i + k + 1))
                    ins = dve.tensor_reduce(smm[:, i % 2, k:k + 1], PS[0:P, (3 * i + k) % 4, 0:w], AX, ALU.min)
                own(did(ins), b * per)
                dve.scalar_tensor_tensor(out=smb[:, i % 2:i % 2 + 1], in0=smm[:, i % 2, 0:1], scalar=smm[:, i % 2, 1:2],
                                         in1=smm[:, i % 2, 2:3], op0=ALU.min, op1=ALU.min).then_inc(S["rowmax_ready"], 1)

            def weighted(b, i):
                hh, tt = i // NT, i % NT
                dve.wait_ge(S["pv_ready"], b * 20 + (i + 1))
                dve.tensor_scalar(O[:, tt, bass.ds(b * 128 + hh * 64, 64)], PS[0:P, 7, 64 * (i % 2):64 * (i % 2) + 64],
                                  smr[:, i % 2:i % 2 + 1], None, ALU.mult).then_inc(S["pv_taken"], 1)

            def head_pair(b, last):
                for i in range(20):
                    if i < 19 or not last:
                        rowmax(b, i + 1)
                    for k in (0, 2):
                        nb = 4 if k == 0 else 2
                        dve.wait_ge(S["pt_ready"], b * 60 + (3 * i + k + 1))
                        if i >= 2:
                            dve.wait_ge(S["pv_ready"], b * 20 + (i - 1))
                        dve.tensor_copy(PT[:, i % 2, 4 * k:4 * k + nb, :], PS[0:P, 4 + (3 * i + k) % 3, 0:nb * P].rearrange("p (k n) -> p k n", n=P)).then_inc(S["pt_by_vector"], 1)
                    if i:
                        weighted(b, i - 1)
                    dve.wait_ge(S["exp_done"], b * 60 + (3 * i + 3))
                    own(did(dve.scalar_tensor_tensor(out=smr[:, 2 + i % 2:3 + i % 2], in0=sms[:, i % 2, 0:1], scalar=sms[:, i % 2, 1:2],
                                                     in1=sms[:, i % 2, 2:3], op0=ALU.add, op1=ALU.add)), b * per)
                    own(did(dve.reciprocal(smr[:, i % 2:i % 2 + 1], smr[:, 2 + i % 2:3 + i % 2])), b * per)
                    if i in (2, 4):
                        lower_bits(b, 1, i // 2 - 1)
                    if i in (12, 14) and not last:
                        lower_bits(b + 1, 0, i // 2 - 6)
                weighted(b, 19)

            for m in range(2):
                lower_bits(0, 0, m)
            rowmax(0, 0)
            base = steps[0]
            with dve.Fori(0, HEADS // 2 - 1) as b:
                head_pair(b, False)
                assert steps[0] - base == per
            steps[0] = base
            head_pair(HEADS // 2 - 1, True)
            steps[0] += per * (HEADS // 2 - 1)
            transposed("ot", OT)
            dve.wait_ge(S["resid_ready"], NT)
            def post_norm(i):
                inverse_of(i, 2)
                own(did(normalized(i, XN[:, i], XN[:, i])))
                own(did(dve.tensor_tensor(XN[:, i], XN[:, i], lngbc[:], ALU.mult)))
                dve.tensor_tensor(XN[:, i], XN[:, i], lnbbc[:], ALU.add).then_inc(S["norm_ready"], 1)

            for i in range(NT):
                ready(dve, "wo", i)
                dve.tensor_tensor(XN[:, i], bank("wo", i)[0:P, :], XN[:, i], ALU.add).then_inc(TV, 1)
                dve.wait_ge(TV, U.taken("wo", i + 1)[0])
                moments(i, XN[:, i])
                if i:
                    post_norm(i - 1)
            post_norm(NT - 1)
            transposed("ht", XNT)

            def over_experts(v, n):
                return v.rearrange("p (t a) -> p t a", a=1).to_broadcast([P, NT, n])

            def first_hot(hot, src, top, n):
                own(did(dve.tensor_reduce(top, src, AX, ALU.max)))
                own(did(dve.tensor_tensor(hot, src, over_experts(top, n), ALU.is_equal)))
                order = idx8[:, 0:n].rearrange("p (a e) -> p a e", a=1).to_broadcast([P, NT, n])
                own(did(dve.tensor_tensor(hot, hot, order, ALU.mult)))
                own(did(dve.tensor_reduce(gs[:, 3], hot, AX, ALU.max)))
                ins = dve.tensor_tensor(hot, hot, over_experts(gs[:, 3], n), ALU.is_equal)
                return ins

            def probabilities(name, bias, n, time):
                g = ga[:, :, 0:n]
                ready(dve, name, 0)
                dve.tensor_tensor(g, bank(name, 0)[0:P, 0:NT * n].rearrange("p (t e) -> p t e", e=n),
                                  bias[:].rearrange("p (a e) -> p a e", a=1).to_broadcast([P, NT, n]), ALU.add).then_inc(TV, 1)
                dve.wait_ge(TV, U.taken(name, 1)[0])
                own(did(dve.tensor_reduce(gs[:, 0], g, AX, ALU.max)))
                dve.tensor_tensor(g, g, over_experts(gs[:, 0], n), ALU.subtract).then_inc(S["gate_max"], 1)
                dve.wait_ge(S["gate_exp"], time)
                own(did(dve.tensor_reduce(gs[:, 1], g, AX, ALU.add)))
                own(did(dve.reciprocal(gs[:, 2], gs[:, 1])))
                own(did(dve.tensor_tensor(g, g, over_experts(gs[:, 2], n), ALU.mult)))

            dve.wait_ge(S["gate_in"], 32)
            probabilities("gate", gbias, EXPERTS, 1)
            first_hot(gb[:], ga[:], gs[:, 0], EXPERTS).then_inc(S["gates_ready"], 1)
            ready(dve, "gate", 2)
            own(did(dve.tensor_copy(inall[:], bank("gate", 2)[0:P, 0:NT * EXPERTS].rearrange("p (t e) -> p t e", e=EXPERTS))))
            own(did(dve.memset(before[:, 0], 0.0)))
            for i in range(1, NT):
                own(did(dve.tensor_tensor(before[:, i], before[:, i - 1], inall[:, i - 1], ALU.add)))
            own(did(dve.tensor_tensor(count[:], before[:, NT - 1], inall[:, NT - 1], ALU.add)))
            own(did(dve.tensor_scalar(counti[:], count[:], 127.0, None, ALU.add)))
            own(did(dve.tensor_scalar(table[:, 0:EXPERTS], counti[:], 7, None, ALU.arith_shift_right)))
            did(dve.memset(startf[:, 0:1], 0.0))
            own(did(dve.tensor_copy(tilesf[:], table[:, 0:EXPERTS])))
            for e in range(1, EXPERTS):
                own(did(dve.tensor_tensor(startf[:, e:e + 1], startf[:, e - 1:e], tilesf[:, e - 1:e], ALU.add)))
            did(dve.tensor_tensor(table[:, 2 * EXPERTS:2 * EXPERTS + 1], startf[:, EXPERTS - 1:EXPERTS], tilesf[:, EXPERTS - 1:EXPERTS], ALU.add))
            did(dve.tensor_scalar(start128[:], startf[:], 128.0, None, ALU.mult))
            dve.tensor_copy(table[:, EXPERTS:2 * EXPERTS], startf[:]).then_inc(S["table_ready"], 1)
            dve.wait_ge(S["table_ready"], 1)
            own(did(dve.tensor_tensor(before[:], before[:], start128[:].rearrange("p (a e) -> p a e", a=1).to_broadcast([P, NT, EXPERTS]), ALU.add)))
            dve.tensor_tensor(before[:], bank("gate", 1)[0:P, 0:NT * EXPERTS].rearrange("p (t e) -> p t e", e=EXPERTS), before[:], ALU.add).then_inc(TV, 1)
            dve.wait_ge(TV, U.taken("gate", 2)[0])
            dve.tensor_tensor(before[:], before[:], gb[:], ALU.mult).then_inc(TV, 1)
            dve.wait_ge(TV, U.taken("gate", 3)[0])
            own(did(dve.tensor_reduce(slotf[:], before[:], AX, ALU.add)))
            dve.tensor_copy(sloti[:], slotf[:]).then_inc(S["slots_ready"], 1)
            for s in range(2):
                dve.tensor_copy(b1c[:, s], b1e[:, s]).then_inc(S["expert_done"], 1)
            dve.tensor_copy(startf[:], tilesf[:]).then_inc(S["y_taken"], 1)
            for i in range(0, ST, 2):
                ready(dve, "rows", i)
                dve.tensor_copy(rowsT[:, :, i * 128:(i + 1) * 128], bank("rows", i).rearrange("p (k n) -> p k n", k=KD)).then_inc(TV, 1)
            with dve.Fori(0, EXPERTS // 2) as e2:
                for s in range(2):
                    n = dve.value_load(table[0:1, bass.ds(e2 * 2 + s, 1)], min_val=0, max_val=MOST)
                    start = dve.value_load(table[0:1, bass.ds(e2 * 2 + (s + EXPERTS), 1)], min_val=0, max_val=ST)

                    def tile(m):
                        i = nc.s_assert_within(start + m, 0, ST - 1, skip_runtime_bounds_check_because="the experts' tiles add up to at most ST")
                        dve.wait_ge(S["rows_stored"], i * 16 + 16)
                        dve.wait_ge(S[f"w2e_in{s}"], e2 * 32 + 32)
                        dve.wait_ge(S["y_ready"], i + 1)
                        dve.tensor_tensor(outrow[:], PS[:, 6, :], b2s[:, s], ALU.add).then_inc(S["y_taken"], 1)

                    up_to(dve, n, MOST, tile)
                    dve.wait_ge(S[f"w1e_in{s}"], e2 * 16 + 16)
                    dve.wait_ge(S[f"w2e_in{s}"], e2 * 32 + 32)
                    dve.tensor_scalar(b1c[:, s:s + 1], b1e[:, bass.ds(e2 * 2 + (s + 2), 1)], 1.0, None, ALU.mult).then_inc(S["expert_done"], 1)
            last = dve.value_load(table[0:1, 2 * EXPERTS:2 * EXPERTS + 1], min_val=1, max_val=ST)
            dve.wait_ge(S["rows_stored"], last * 16 + 16)
            dve.tensor_scalar(topw[:], gs[:, 0], 1.0, None, ALU.mult).then_inc(S["rows_out_ready"], 1)
            dve.wait_ge(S["rows_out_ready"], 1)
            for i in range(NT):
                if i % (NT // 2) == 0:
                    dve.wait_ge(S[f"rows_back{i // (NT // 2)}"], 16 * NT // 2)
                own(did(dve.scalar_tensor_tensor(out=X[:, i], in0=back[:, i], scalar=topw[:, i:i + 1], in1=X[:, i], op0=ALU.mult, op1=ALU.add)))
                moments(i, X[:, i])
            taken(dve, "xt2", 0)
            inverse(3)
            for i in range(NT):
                normalized(i, XN3[:, i], X[:, i]).then_inc(S["norm_ready"], 1)
            transposed("xt2", XNT3)
            for i in range(NT):
                dve.wait_ge(S["split_hi"], NT + i + 1)
                dve.tensor_tensor(HL[:, i], XN3[:, i], HH[:, i].bitcast(F32), ALU.subtract).then_inc(S["split_lo"], 1)
            dve.wait_ge(S["unspilled"], 16)
            for i in range(NT):
                blk = AT[:, i, i * P:(i + 1) * P]
                ins = dve.tensor_tensor(blk, blk.bitcast(F32), ident[0:P, 0:P], ALU.subtract)
            ins.then_inc(S["adj_ready"], 1)
            dve.wait_ge(S["gate2_in"], 32)
            probabilities("gate2", gbias2, SAGE, 2)
            p, w4, hot = ga[:, :, 0:SAGE], wexp[:, :, 0:SAGE], gb[:, :, 0:SAGE]
            own(did(first_hot(w4, p, gs[:, 0], SAGE)))
            own(did(dve.scalar_tensor_tensor(out=gc[:], in0=w4, scalar=-2.0, in1=p, op0=ALU.mult, op1=ALU.add)))
            own(did(first_hot(hot, gc[:], gs[:, 1], SAGE)))
            own(did(dve.tensor_tensor(w4, w4, hot, ALU.add)))
            dve.tensor_tensor(w4, w4, p, ALU.mult).then_inc(S["gates_ready"], 1)
            dve.wait_ge(S["gates_ready"], 2)
            for k in range(3):
                ready(dve, "degree2", k)
                r = rowbc3[:, k * DCH:(k + 1) * DCH]
                deg = bank("degree2", k)[:, 0:DCH]
                dve.tensor_scalar(r, deg, 1.0, None, ALU.max).then_inc(TV, 1)
            dve.wait_ge(TV, U.taken("agg3", 0)[0])
            own(did(dve.reciprocal(rowbc3[:], rowbc3[:])))
            taken(dve, "agg3", 0)
            for k in range(12):
                c, f = k // KD, k % KD
                lo, w = CHUNKS[c]
                ready(dve, "agg3", k)
                dve.tensor_tensor(agg0[:, f, lo:lo + w], bank("agg3", k)[:, 0:w], rowbc3[:, lo:lo + w], ALU.mult).then_inc(TV, 1)
            with dve.Fori(0, SAGE) as e:
                def lower(l):
                    dve.wait_ge(S["wl_hi"], e * 2 + (l + 1))
                    dve.tensor_tensor(WL[:, 1], WLf[:, 1], WL[:, 0].bitcast(F32), ALU.subtract).then_inc(S["wl_lo"], 1)

                def low_part(i):
                    dve.wait_ge(S["relu_done"], e * NT + (i + 1))
                    dve.scalar_tensor_tensor(out=HL[:, i], in0=bank("sage", i)[0:P, :], scalar=0.0,
                                             in1=HH[:, i].bitcast(F32), op0=ALU.max, op1=ALU.subtract).then_inc(TV, 1)

                lower(0)
                for u in range(len(PARTS) + 3):
                    if u < len(PARTS):
                        tt, right = PARTS[u]
                        dve.wait_ge(S["part_hi"], e * len(PARTS) + (u + 1))
                        dve.tensor_tensor(part[:, u % 2, 1], (agg0, XNT3)[right][:, :, tt * P:(tt + 1) * P], part[:, u % 2, 0].bitcast(F32), ALU.subtract).then_inc(S["part_lo"], 1)
                    if u == 2:
                        dve.wait_ge(S["bias_in"], e * 32 + 16)
                    if 2 <= u < len(PARTS) + 2 and PARTS[u - 2][1]:
                        i = PARTS[u - 2][0]
                        ready(dve, "sage", i, e)
                        dve.tensor_tensor(bank("sage", i)[0:P, :], bank("sage", i)[0:P, :], bias[:], ALU.add).then_inc(S["bias_added"], 1)
                    if u >= 3 and PARTS[u - 3][1]:
                        low_part(PARTS[u - 3][0])
                lower(1)
                for c in range(5):
                    k0 = NT + 10 * c

                    def agg_low(f):
                        dve.wait_ge(S["agg_hi"], e * (5 * KD) + (c * KD + f + 1))
                        dve.tensor_tensor(aggl[:, f], aggc[:, f], aggh[:, f].bitcast(F32), ALU.subtract).then_inc(S["agg_lo"], 1)

                    def transposed_low():
                        dve.tensor_copy(hTl[:], bank("sage", k)[:, 0:KD * 126].rearrange("p (k n) -> p k n", k=KD)).then_inc(TV, 1)

                    for f in range(KD):
                        ready(dve, "sage", k0 + f, e)
                        dve.tensor_tensor(aggc[:, f], bank("sage", k0 + f)[:, 0:250], rowbc3[:, c * 250:(c + 1) * 250], ALU.mult).then_inc(TV, 1)
                        if f:
                            agg_low(f - 1)
                    agg_low(KD - 1)
                    for i in range(2):
                        k = k0 + (5, 8)[i]
                        ready(dve, "sage", k, e)
                        transposed_low()
                        k, tt = k0 + 7 + 2 * i, 2 * c + i
                        if c == 0 and i == 0:
                            dve.wait_ge(S["bias_in"], e * 32 + 32)
                        ready(dve, "sage", k, e)
                        dve.tensor_tensor(bank("sage", k)[0:P, :], bank("sage", k)[0:P, :], bias[:], ALU.add).then_inc(S["bias_added"], 1)
                        dve.wait_ge(S["relu2_done"], e * NT + (tt + 1))
                        dve.wait_ge(TV, U.taken("sage", 0, e)[0])
                        dve.scalar_tensor_tensor(out=X[:, tt], in0=bank("sage", k)[0:P, :], scalar=wexp[:, tt, bass.ds(e, 1)],
                                                 in1=X[:, tt], op0=ALU.mult, op1=ALU.add).then_inc(TV, 1)
            taken(dve, "xt3", 0)
            for i in range(NT):
                moments(i, X[:, i])
            inverse(4)
            for i in range(NT):
                normalized(i, XN4[:, i], X[:, i]).then_inc(S["norm_ready"], 1)
            transposed("xt3", XNT4)
            own(did(dve.memset(c03[:], 0.03)))
            taken(dve, "merge", 0)
            own(did(dve.tensor_reduce(ghm[:], ghs[:], AX, ALU.add)))
            own(did(dve.tensor_scalar(ghm[:], ghm[:], 1.0 / N, None, ALU.mult)))
            dve.tensor_copy(ghb[:], ghm[:].rearrange("p (k a) -> p k a", a=1).to_broadcast([128, KD, 128])).then_inc(S["ghm_ready"], 1)
            dve.wait_ge(S["merge_in"], 13 * 16)
            ready(dve, "merge", 0)
            dve.tensor_tensor(gbc[:], bank("merge", 0)[:, 0:EXPERTS], g2bbc[:], ALU.add).then_inc(TV, 1)
            ready(dve, "merge", 1)
            dve.tensor_scalar(gT[:], bank("merge", 1)[0:EXPERTS, 0:128], g2bcol[:], None, ALU.add).then_inc(TV, 1)
            ready(dve, "merge", 2)
            dve.tensor_tensor(m2bc[:], m2bc[:], bank("merge", 2)[0:P, :], ALU.add).then_inc(TV, 1)
            for k, v in ((3, mgbc), (4, mbbc)):
                ready(dve, "merge", k)
                dve.scalar_tensor_tensor(out=v[:], in0=v[:], scalar=1.0 - 0.03 * EXPERTS, in1=bank("merge", k)[0:P, :],
                                         op0=ALU.mult, op1=ALU.add).then_inc(TV, 1)
            dve.wait_ge(TV, U.taken("merge", 5)[0])
            own(did(dve.tensor_tensor(tvt[:], tvb1[:], gbc[:].rearrange("p (a e) -> p a e", a=1).to_broadcast([128, KM, EXPERTS]), ALU.mult)))
            own(did(dve.tensor_reduce(tvr[:], tvt[:], AX, ALU.add)))
            own(did(dve.tensor_tensor(m1b[:], m1b[:], tvr[:], ALU.add)))
            for n in range(2 * EXPERTS):
                e, m = n % EXPERTS, (W1m, W2m)[n // EXPERTS]
                dve.wait_ge(S[f"tv_in{n % 4}"], 16 * (n // 4 + 1))
                if n:
                    dve.wait_ge(S["tv_used"], n)
                flat = m[:].rearrange("p k n -> p (k n)")
                dve.scalar_tensor_tensor(out=flat, in0=tv[:, n % 4], scalar=gbc[:, e:e + 1], in1=flat, op0=ALU.mult, op1=ALU.add).then_inc(S["tv_used"], 1)

            def last_norm(i):
                inverse_of(i, 5)
                own(did(normalized(i, XN4[:, i], XN4[:, i])))
                own(did(dve.tensor_tensor(XN4[:, i], XN4[:, i], mgbc[:], ALU.mult)))
                dve.wait_ge(S["bias_in_x"], i + 1)
                dve.tensor_tensor(XN4[:, i], XN4[:, i], X[:, i], ALU.add).then_inc(S["tail_ready"], 1)

            for i in range(NT):
                ready(dve, "down", i)
                dve.wait_ge(S["bias_in_residual"], i + 1)
                dve.tensor_tensor(XN4[:, i], bank("down", i)[0:P, :], XN4[:, i], ALU.add).then_inc(TV, 1)
                dve.wait_ge(TV, U.taken("down", i + 1)[0])
                moments(i, XN4[:, i])
                if i:
                    last_norm(i - 1)
            last_norm(NT - 1)

        @block.tensor
        def _(pe):
            UR = S["unit_ready"]

            def free(name, k, i=0):
                if k == 0:
                    taken(pe, name, 0, i)
                elif k >= 8:
                    taken(pe, name, k - 7, i)

            def product(dst, lhs, rhs):
                for n, (a, b) in enumerate(zip(lhs, rhs)):
                    ins = pe.matmul(dst, a, b, start=(n == 0), stop=(n == len(lhs) - 1))
                return ins

            def transposes(name, src, wait, base):
                for i in range(NT):
                    pe.wait_ge(S[wait], base + i + 1)
                    free(name, i)
                    for k in range(KD):
                        ins = pe.transpose(bank(name, i)[:, k * P:(k + 1) * P], src[:, i, k * 128:(k + 1) * 128], ident[0:P, 0:P])
                    ins.then_inc(UR, 1)

            def blocks(m, lo, w):
                return [m[:, k, lo:lo + w] for k in range(m.shape[1])]

            def three(a, cols_a, b, cols_b):
                return ([x for m in (0, 1, 0) for x in blocks(a[m], *cols_a)],
                        [x for m in (0, 0, 1) for x in blocks(b[m], *cols_b)])

            pe.wait_ge(S["ident_done"], 9)
            pe.wait_ge(S["edges_ready"], 1)
            for k in range(2):
                for h in range(2):
                    ins = pe.transpose(bank("edges", k)[0:P, h * EROWS:(h + 1) * EROWS], edgef[:, k, h * P:(h + 1) * P], ident[0:EROWS, 0:EROWS])
                ins.then_inc(UR, 1)
            pe.wait_ge(S["edges_ready"], 2)
            pe.matmul(bank("edges", 2)[0:P, 0:(NT - 1) * GROUPS], ones[0:P, 0:P], aboves[:].rearrange("p j g -> p (j g)"), start=True, stop=True).then_inc(UR, 1)
            taken(pe, "edges", 3)

            def count(q, j, s, u, first):
                pe.wait_ge(S[f"counts_read{s}"], u[s] + 1)
                for c in range(GROUP):
                    pe.wait_ge(S["onehots_ready"], q * GROUP + (c + 2))
                    for r in range(PACKED):
                        ins = pe.matmul(PS[0:P, 2 * s + r // 4, (r % 4) * P:(r % 4 + 1) * P], ohs[:, c, r * P:(r + 1) * P], ohd[:, c],
                                        start=(c == 0 and r % 4 == 0), stop=(c == GROUP - 1 and r >= 3))
                    ins.then_inc(S["onehots_used"], 1)

            pairs(pe, count)
            pe.wait_ge(S["adj_ready"], 1)
            for k in range(3):
                product(bank("degree", k)[:, 0:DCH], [onesr[0:P, :]] * NT, [AT[:, s, k * DCH:(k + 1) * DCH] for s in range(NT)]).then_inc(UR, 1)

            def aggregate(name, k0, hi, lo_, c, cols, i=0):
                lo, w = cols
                for f in range(KD):
                    free(name, k0 + f, i)
                    lhs = [h[:, s, f * 128:(f + 1) * 128] for h in (hi, lo_) for s in range(NT)]
                    rhs = [AT[:, s, lo:lo + w] for _ in range(2) for s in range(NT)]
                    product(bank(name, k0 + f)[:, 0:w], lhs, rhs).then_inc(UR, 1)

            pe.wait_ge(S["split_lo"], NT)
            for c in range(3):
                aggregate("agg1", KD * c, XH, XL, c, CHUNKS[c])
            pe.wait_ge(S["w1_in"], 16)
            taken(pe, "agg1", 12)
            for c in range(5):
                for f in range(KF):
                    k = 18 * c + f
                    free("gcn", k)
                    product(bank("gcn", k)[:, 0:250], blocks(W1, f * 128, 128), blocks(aggT, 250 * c, 250)).then_inc(UR, 1)
                pe.wait_ge(S["w2_in"], 16)
                taken(pe, "gcn", 18 * c + KF)
                for i in range(2):
                    k = 18 * c + KF + i
                    product(bank("gcn", k)[0:P, :], blocks(zT, i * P, P), blocks(W2, 0, D)).then_inc(UR, 1)
            taken(pe, "gcn", U.size("gcn"))
            for i in range(NT):
                free("agg2", i)
                product(bank("agg2", i)[0:P, :], [AT[:, s, i * P:(i + 1) * P] for _ in range(2) for s in range(NT)],
                        [h[:, s, :] for h in (XH, XL) for s in range(NT)]).then_inc(UR, 1)
            transposes("xt1", XN, "norm_ready", NT)
            taken(pe, "xt1", NT)
            for n in range(24):
                f, c, m = (n % 12) // 3, n % 3, n // 12
                if n % 12 == 0:
                    pe.wait_ge(S["weights_lo"], m + 1)
                free("qkv", n)
                product(bank("qkv", n)[:, 0:CHUNKS[c][1]], *three((Wh[:, m], Wl[:, m]), (f * 128, 128), (XNTh, XNTl), CHUNKS[c])).then_inc(UR, 1)
            pe.wait_ge(S["weights_lo"], 3)
            for i in range(NT):
                free("qkv", 24 + i)
                product(bank("qkv", 24 + i)[0:P, :], *three((XNTh, XNTl), (i * P, P), (Wh[:, 2], Wl[:, 2]), (0, D))).then_inc(UR, 1)
            taken(pe, "qkv", U.size("qkv"))

            def scores(b, i):
                hh, tt = i // NT % 2, i % NT
                pe.wait_ge(S["staged_by_vector"], b * 4 + 2 * (i // NT + 1))
                pe.wait_ge(S["staged_by_scalar"], b * 6 + 3 * (i // NT + 1))
                for k, (lo, w) in enumerate(CHUNKS):
                    n = 3 * i + k
                    if n >= 4:
                        pe.wait_ge(S["exp_done"], b * 60 + (n - 3))
                    pe.matmul(PS[0:P, n % 4, 0:w], qs[:, hh, tt * P:(tt + 1) * P], ks[:, hh, lo:lo + w], start=True, stop=False)
                    pe.matmul(PS[0:P, n % 4, 0:w], qs[OWN[hh], hh, tt * P:(tt + 1) * P], kl[OWN[hh], lo:lo + w], start=False, stop=True).then_inc(S["scores_ready"], 1)

            def transpose_p(b, i):
                for k, (lo, w) in enumerate(CHUNKS):
                    pe.wait_ge(S["exp_done"], b * 60 + (3 * i + k + 1))
                    if i:
                        if k == 1:
                            pe.wait_ge(S["pt_by_scalar"], b * 20 + i)
                        else:
                            pe.wait_ge(S["pt_by_vector"], b * 40 + (2 * i - (1 if k == 0 else 0)))
                    for m in range(w // P):
                        ins = pe.transpose(PS[0:P, 4 + (3 * i + k) % 3, m * P:(m + 1) * P], Pr[:, i % 2, lo + m * P:lo + (m + 1) * P], ident[0:P, 0:P])
                    ins.then_inc(S["pt_ready"], 1)

            def values(b, i):
                hh = i // NT
                pe.wait_ge(S["pt_by_vector"], b * 40 + 2 * (i + 1))
                pe.wait_ge(S["pt_by_scalar"], b * 20 + (i + 1))
                if i:
                    pe.wait_ge(S["pv_taken"], b * 20 + i)
                for s in range(NT):
                    ins = pe.matmul(PS[0:P, 7, 64 * (i % 2):64 * (i % 2) + 64], PT[:, i % 2, s, :], V[:, s, bass.ds(b * 128 + hh * 64, 64)],
                                    start=(s == 0), stop=(s == NT - 1))
                ins.then_inc(S["pv_ready"], 1)

            def head_pair(b, last):
                for i in range(20):
                    if i < 19 or not last:
                        scores(b, i + 1)
                    transpose_p(b, i)
                    if i:
                        values(b, i - 1)
                values(b, 19)

            scores(0, 0)
            with pe.Fori(0, HEADS // 2 - 1) as b:
                head_pair(b, False)
            head_pair(HEADS // 2 - 1, True)
            pe.wait_ge(S["pv_taken"], HEADS * NT)
            pe.wait_ge(S["pt_by_scalar"], HEADS * NT)
            transposes("ot", O, "pv_taken", HEADS * NT - NT)
            taken(pe, "ot", NT)
            pe.wait_ge(S["wo_in"], 16)
            for i in range(NT):
                free("wo", i)
                product(bank("wo", i)[0:P, :], blocks(OT, i * P, P), blocks(Wq, 0, D)).then_inc(UR, 1)
            transposes("ht", XN, "norm_ready", 2 * NT)
            taken(pe, "gate", 0)
            pe.wait_ge(S["gate_in"], 32)
            for i in range(NT):
                ins = product(bank("gate", 0)[0:P, EXPERTS * i:EXPERTS * (i + 1)], blocks(XNT, i * P, P), blocks(gW, 0, EXPERTS))
            ins.then_inc(UR, 1)
            pe.wait_ge(S["gates_ready"], 1)
            for m, k in ((tri, 1), (ones, 2)):
                pe.matmul(bank("gate", k)[0:P, 0:NT * EXPERTS], m[0:P, 0:P], gb[:].rearrange("p t e -> p (t e)"), start=True, stop=True).then_inc(UR, 1)
            taken(pe, "gate", 3)
            for i in range(ST):
                for n, (a, b) in enumerate(THIRDS):
                    if i == a:
                        pe.wait_ge(S[f"rows_loaded{n}"], 16)
                free("rows", i)
                for k in range(KD):
                    ins = pe.transpose(bank("rows", i)[:, k * 128:(k + 1) * 128], rows_in[:, i, k * 128:(k + 1) * 128], ident[:])
                ins.then_inc(UR, 1)
            taken(pe, "rows", ST)
            pe.wait_ge(S["table_ready"], 1)
            with pe.Fori(0, EXPERTS // 2) as e2:
                for s in range(2):
                    n = pe.value_load(table[0:1, bass.ds(e2 * 2 + s, 1)], min_val=0, max_val=MOST)
                    start = pe.value_load(table[0:1, bass.ds(e2 * 2 + (s + EXPERTS), 1)], min_val=0, max_val=ST)

                    def tile(m):
                        i = nc.s_assert_within(start + m, 0, ST - 1, skip_runtime_bounds_check_because="the experts' tiles add up to at most ST")
                        pe.wait_ge(S[f"w1e_in{s}"], e2 * 16 + 16)
                        for f in range(KF):
                            if f >= 6:
                                pe.wait_ge(S["hid_done"], i * KF + (f - 5))
                            product(PS[:, f % 6, 0:128], [W1e[:, s, k, f * 128:(f + 1) * 128] for k in range(KD)],
                                    [rowsT[:, k, bass.ds(i * 128, 128)] for k in range(KD)]).then_inc(S["hid_ready"], 1)
                        pe.wait_ge(S["y_taken"], i + 1)
                        pe.wait_ge(S[f"w2e_in{s}"], e2 * 32 + 32)
                        for k in range(KF):
                            pe.wait_ge(S["hid_done"], i * KF + (k + 1))
                            ins = pe.matmul(PS[:, 6, :], hid[:, k], W2e[:, s, k, :], start=(k == 0), stop=(k == KF - 1))
                        ins.then_inc(S["y_ready"], 1)

                    up_to(pe, n, MOST, tile)
            transposes("xt2", XN3, "norm_ready", 3 * NT)
            taken(pe, "xt2", NT)
            pe.wait_ge(S["gate2_in"], 32)
            for i in range(NT):
                ins = product(bank("gate2", 0)[0:P, SAGE * i:SAGE * (i + 1)], blocks(XNT3, i * P, P), blocks(gW2, 0, SAGE))
            ins.then_inc(UR, 1)
            taken(pe, "degree2", 0)
            pe.wait_ge(S["adj_ready"], 2)
            for k in range(3):
                product(bank("degree2", k)[:, 0:DCH], [onesr[0:P, :]] * NT, [AT[:, s, k * DCH:(k + 1) * DCH] for s in range(NT)]).then_inc(UR, 1)
            pe.wait_ge(S["split_lo"], 2 * NT)
            for c in range(3):
                aggregate("agg3", KD * c, HH, HL, c, CHUNKS[c])
            with pe.Fori(0, SAGE) as e:
                def add(dst, a, cols_a, b, cols_b, first, last):
                    lhs, rhs = three(a, cols_a, b, cols_b)
                    for n, (x, y) in enumerate(zip(lhs, rhs)):
                        ins = pe.matmul(dst, x, y, start=(first and n == 0), stop=(last and n == len(lhs) - 1))
                    return ins

                for u, (tt, right) in enumerate(PARTS):
                    if not right:
                        free("sage", tt, e)
                    if u == 0:
                        pe.wait_ge(S["wl_lo"], e * 2 + 1)
                    if u == 4:
                        pe.wait_ge(S["wr_lo"], e * 2 + 1)
                    pe.wait_ge(S["part_lo"], e * len(PARTS) + (u + 1))
                    w = WR if right else WL
                    ins = add(bank("sage", tt)[0:P, :], (part[:, u % 2, 0], part[:, u % 2, 1]), (0, P), (w[:, 0], w[:, 1]), (0, D), not right, bool(right))
                    ins.then_inc(UR if right else S["part_used"], 1)
                taken(pe, "sage", NT, e)
                for c in range(5):
                    k0 = NT + 10 * c
                    aggregate("sage", k0, HH, HL, c, (250 * c, 250), e)

                    def transpose_h(k, h, tt):
                        free("sage", k, e)
                        for f in range(KD):
                            ins = pe.matmul(bank("sage", k)[:, f * 126:(f + 1) * 126], h[:, tt, f * 128:(f + 1) * 128], identr[0:P, 0:126], start=True, stop=True)
                        ins.then_inc(UR, 1)

                    transpose_h(k0 + 4, HH, 2 * c)
                    transpose_h(k0 + 5, HL, 2 * c)
                    transpose_h(k0 + 6, HH, 2 * c + 1)
                    if c == 0:
                        pe.wait_ge(S["wl_lo"], e * 2 + 2)
                    pe.wait_ge(S["agg_lo"], e * (5 * KD) + (c + 1) * KD)
                    for i in range(2):
                        k = k0 + 7 + 2 * i
                        free("sage", k, e)
                        ins = add(bank("sage", k)[0:P, :], (aggh, aggl), (i * P, P), (WL[:, 0], WL[:, 1]), (0, D), True, False)
                    if c == 4:
                        ins.then_inc(S["left_used"], 1)
                    if c == 0:
                        pe.wait_ge(S["wr_lo"], e * 2 + 2)
                    taken(pe, "sage", k0 + 7, e)
                    add(bank("sage", k0 + 7)[0:P, :], (hTh[:, 0], hTl), (0, P), (WR[:, 0], WR[:, 1]), (0, D), False, True).then_inc(UR, 1)
                    transpose_h(k0 + 8, HL, 2 * c + 1)
                    dst = bank("sage", k0 + 9)[0:P, :]
                    for part_w in range(2):
                        for f in range(KD):
                            pe.matmul(dst, hTh[:, 1, f, 0:P], WR[:, part_w, f], start=False, stop=False)
                    taken(pe, "sage", k0 + 9, e)
                    for f in range(KD):
                        ins = pe.matmul(dst, hTl[:, f, 0:P], WR[:, 0, f], start=False, stop=(f == KD - 1))
                    ins.then_inc(UR, 1)
            transposes("xt3", XN4, "norm_ready", 4 * NT)
            taken(pe, "xt3", NT)
            pe.wait_ge(S["g1_in"], 32)
            for n in range(12):
                f, c = n // 3, n % 3
                free("gh", n)
                product(bank("gh", n)[:, 0:CHUNKS[c][1]], blocks(g1T, f * 128, 128), blocks(XNT4, *CHUNKS[c])).then_inc(UR, 1)
            taken(pe, "merge", 0)
            pe.wait_ge(S["merge_in"], 13 * 16)
            pe.wait_ge(S["ghm_ready"], 1)
            product(bank("merge", 0)[:, 0:EXPERTS], blocks(ghb, 0, 128), blocks(g2T, 0, EXPERTS)).then_inc(UR, 1)
            product(bank("merge", 1)[0:EXPERTS, 0:128], blocks(g2T, 0, EXPERTS), blocks(ghb, 0, 128)).then_inc(UR, 1)
            taken(pe, "merge", 2)
            pe.matmul(bank("merge", 2)[0:P, :], gT[:, 0:P], tvb2[:], start=True, stop=True).then_inc(UR, 1)
            for k, v in ((3, tvg), (4, tvb)):
                pe.matmul(bank("merge", k)[0:P, :], c03[:], v[:], start=True, stop=True).then_inc(UR, 1)
            taken(pe, "merge", 5)
            pe.wait_ge(S["tv_used"], EXPERTS)
            for n in range(6):
                f, c = n // 3, n % 3
                product(bank("up", n)[:, 0:CHUNKS[c][1]], blocks(W1m, f * 128, 128), blocks(XNT4, *CHUNKS[c])).then_inc(UR, 1)
            taken(pe, "up", 6)
            pe.wait_ge(S["tv_used"], 2 * EXPERTS)
            for i in range(NT):
                free("down", i)
                product(bank("down", i)[0:P, :], blocks(upT, i * P, P), blocks(W2m, 0, D)).then_inc(UR, 1)


_IN = ["x", "src", "dst", "L0_gnn_W1", "L0_gnn_b1", "L0_gnn_W2", "L0_gnn_b2", "L0_ffn_ln1_g", "L0_ffn_ln1_b",
       "L0_ffn_Wq", "L0_ffn_bq", "L0_ffn_Wk", "L0_ffn_bk", "L0_ffn_Wv", "L0_ffn_bv", "L0_ffn_Wo", "L0_ffn_bo",
       "L0_ffn_gate_W", "L0_ffn_gate_b", "L0_ffn_W1", "L0_ffn_b1", "L0_ffn_W2", "L0_ffn_b2", "L1_gnn_gate_W",
       "L1_gnn_gate_b", "L1_gnn_Wl", "L1_gnn_bl", "L1_gnn_Wr", "L1_ffn_gfc1_w", "L1_ffn_gfc1_b", "L1_ffn_gfc2_w",
       "L1_ffn_gfc2_b", "L1_ffn_W1", "L1_ffn_b1", "L1_ffn_W2", "L1_ffn_b2", "L1_ffn_ln_g", "L1_ffn_ln_b",
       "L1_ffn_tv_W1", "L1_ffn_tv_b1", "L1_ffn_tv_W2", "L1_ffn_tv_b2", "L1_ffn_tv_ln_g", "L1_ffn_tv_ln_b"]


def _laid_out(inputs):
    import numpy as np

    a = {k: np.asarray(inputs[k]) for k in _IN}
    for k in ("L0_gnn_b1", "L0_ffn_bq", "L0_ffn_bk", "L1_ffn_gfc1_b", "L1_ffn_b1"):
        a[k] = a[k].reshape(-1, 128).T
    a["L0_ffn_b1"] = a["L0_ffn_b1"].reshape(EXPERTS, KF, 128).transpose(2, 0, 1)
    a["L1_ffn_tv_b1"] = a["L1_ffn_tv_b1"].reshape(EXPERTS, KM, 128).transpose(2, 1, 0)
    for k in ("L1_ffn_gfc1_w", "L1_ffn_gfc2_w", "L1_ffn_W1", "L1_ffn_W2"):
        a[k] = a[k].T
    for k in ("L1_ffn_tv_W1", "L1_ffn_tv_W2"):
        a[k] = a[k].transpose(0, 2, 1)
    return {k: np.ascontiguousarray(v) for k, v in a.items()}


def build(nc, arrays):
    t = {k: nc.dram_tensor(f"in_{k}", v.shape, mybir.dt.from_np(v.dtype), kind="ExternalInput").ap() for k, v in arrays.items()}
    out = nc.dram_tensor("out_0", (N, D), F32, kind="ExternalOutput").ap()
    rows_x = nc.dram_tensor("rows_by_expert", (SLOT_ROWS, D), F32, kind="Internal").ap()
    rows_y = nc.dram_tensor("rows_out_by_expert", (SLOT_ROWS, D), F32, kind="Internal").ap()
    spill = nc.dram_tensor("adjacency_spill", (P, NT, NPAD), F32, kind="Internal").ap()
    program(nc, t, out, spill, rows_x, rows_y)


def kernel(**inputs):
    import concourse.bacc as _bacc
    from concourse.bass_utils import run_bass_kernel_spmd as _run

    arrays = _laid_out(inputs)
    nc = _bacc.Bacc("TRN2", target_bir_lowering=False, num_devices=1)
    build(nc, arrays)
    r = _run(nc, [{f"in_{k}": v for k, v in arrays.items()}], core_ids=[0])
    return r.results[0]["out_0"]
```
